# Optimizing a Trainium2 kernel written in Bass

```python
import numpy as np
import jax
import jax.numpy as jnp

def _softmax(x, axis=-1):
    return jax.nn.softmax(x, axis=axis)

def _gelu(x):
    return jax.nn.gelu(x, approximate=True)

def _silu(x):
    return jax.nn.silu(x)

def _sigmoid(x):
    return jax.nn.sigmoid(x)

def _layernorm(x, axis=-1, eps=1e-05):
    m = jnp.mean(x, axis=axis, keepdims=True)
    v = jnp.var(x, axis=axis, keepdims=True)
    return (x - m) / jnp.sqrt(v + eps)

def _scatter_add(tgt, idx, src, axis=0):
    return tgt.at[idx].add(src)

def _segment_sum(src, seg, n):
    return jax.ops.segment_sum(src, seg, n)
kernel_name = 'mk_sandwich_d4_jaxref_r8_8674ff'

def setup_inputs(seed: int=0):
    np.random.seed(seed)
    _w = jnp.asarray

    def _L0_attn_setup():
        import jax, jax.numpy as jnp
        import numpy as np
        D_MODEL = 128
        N_HEADS = 16
        D_K = D_MODEL // N_HEADS
        THETA = 10000.0
        MAX_SEQ = 256

        def _trunc_normal(key, shape, std):
            return jnp.clip(jax.random.normal(key, shape) * std, -3 * std, 3 * std).astype(jnp.float32)

        def _rope(x, positions):
            d = x.shape[-1]
            inv_freq = THETA ** (-2.0 * jnp.arange(0, d // 2, dtype=jnp.float32) / d)
            angles = positions.astype(jnp.float32)[:, None] * inv_freq[None, :]
            cos, sin = (jnp.cos(angles), jnp.sin(angles))
            xp = x.reshape(x.shape[:-1] + (d // 2, 2))
            x_even, x_odd = (xp[..., 0], xp[..., 1])
            out_even = x_even * cos - x_odd * sin
            out_odd = x_even * sin + x_odd * cos
            return jnp.stack((out_even, out_odd), axis=-1).reshape(x.shape)
        key = jax.random.key(seed)
        kx, kq, kk, kv, ko = jax.random.split(key, 5)
        std = np.sqrt(2.0 / (D_MODEL + D_MODEL))
        x = jax.random.normal(kx, (2, 256, D_MODEL), dtype=jnp.float32)
        W_q = _trunc_normal(kq, (D_MODEL, D_MODEL), std)
        W_k = _trunc_normal(kk, (D_MODEL, D_MODEL), std)
        W_v = _trunc_normal(kv, (D_MODEL, D_MODEL), std)
        W_o = _trunc_normal(ko, (D_MODEL, D_MODEL), std)
        return {'x': x, 'W_q': W_q, 'W_k': W_k, 'W_v': W_v, 'W_o': W_o}
    _L0_attn_in = _L0_attn_setup()

    def _L0_ffn_setup():
        import jax, jax.numpy as jnp
        import numpy as np
        B, S, H, F, G = (8, 256, 128, 512, 128)
        EPS = 1e-05

        def _dequant(q, scales, g):
            K, N = q.shape
            w = (q.astype(jnp.float32) - 128.0).reshape(K // g, g, N) * scales[:, None, :]
            return w.reshape(K, N)
        key = jax.random.key(seed)
        ks = jax.random.split(key, 8)
        x = jax.random.normal(ks[0], (B, S, H), dtype=jnp.float32)
        ln_gamma = jnp.ones((H,), jnp.float32)
        ln_beta = jnp.zeros((H,), jnp.float32)
        fc1_q = jax.random.randint(ks[1], (H, F), 0, 32, dtype=jnp.int32)
        fc2_q = jax.random.randint(ks[2], (F, H), 0, 32, dtype=jnp.int32)
        fc1_scales = jax.random.uniform(ks[3], (H // G, F), jnp.float32) * 0.02 + 0.001
        fc2_scales = jax.random.uniform(ks[4], (F // G, H), jnp.float32) * 0.02 + 0.001
        fc1_bias = jax.random.normal(ks[5], (F,), jnp.float32) * 0.02
        fc2_bias = jax.random.normal(ks[6], (H,), jnp.float32) * 0.02
        return {'x': x, 'ln_gamma': ln_gamma, 'ln_beta': ln_beta, 'fc1_q': fc1_q, 'fc1_scales': fc1_scales, 'fc1_bias': fc1_bias, 'fc2_q': fc2_q, 'fc2_scales': fc2_scales, 'fc2_bias': fc2_bias}
    _L0_ffn_in = _L0_ffn_setup()

    def _L1_attn_setup():
        import jax, jax.numpy as jnp
        import numpy as np
        D_MODEL = 128
        N_HEADS = 16
        HEAD_DIM = D_MODEL // N_HEADS
        EPS = 1e-06

        def _split_heads(x):
            b, s, d = x.shape
            return x.reshape(b, s, N_HEADS, HEAD_DIM).transpose(0, 2, 1, 3)
        key = jax.random.key(seed)
        ks = jax.random.split(key, 10)
        s = 0.02
        return {'sequence': jax.random.normal(ks[0], (4, 256, D_MODEL), dtype=jnp.float32), 'ln_gamma': jnp.ones((D_MODEL,), jnp.float32), 'ln_beta': jnp.zeros((D_MODEL,), jnp.float32), 'Wq': jax.random.normal(ks[1], (D_MODEL, D_MODEL), jnp.float32) * s, 'bq': jnp.zeros((D_MODEL,), jnp.float32), 'Wk': jax.random.normal(ks[2], (D_MODEL, D_MODEL), jnp.float32) * s, 'bk': jnp.zeros((D_MODEL,), jnp.float32), 'Wv': jax.random.normal(ks[3], (D_MODEL, D_MODEL), jnp.float32) * s, 'bv': jnp.zeros((D_MODEL,), jnp.float32), 'Wo': jax.random.normal(ks[4], (D_MODEL, D_MODEL), jnp.float32) * s, 'bo': jnp.zeros((D_MODEL,), jnp.float32), 'mu': jnp.zeros((1, 1, 1, 1), jnp.float32)}
    _L1_attn_in = _L1_attn_setup()

    def _L1_ffn_setup():
        import jax, jax.numpy as jnp
        import numpy as np
        DIM = 128
        HIDDEN = 384
        SCALE = 1.0 / 127.0

        def _dequant(w_int, dtype):
            return w_int.astype(dtype) * jnp.asarray(SCALE, dtype)
        key = jax.random.key(seed)
        k_x, k_g, k_u, k_d = jax.random.split(key, 4)
        x = jax.random.normal(k_x, (4, 256, DIM), dtype=jnp.float32)
        w_gate = jax.random.randint(k_g, (HIDDEN, DIM), -127, 128, dtype=jnp.int32)
        w_up = jax.random.randint(k_u, (HIDDEN, DIM), -127, 128, dtype=jnp.int32)
        w_down = jax.random.randint(k_d, (DIM, HIDDEN), -127, 128, dtype=jnp.int32)
        return {'x': x, 'w_gate': w_gate, 'w_up': w_up, 'w_down': w_down}
    _L1_ffn_in = _L1_ffn_setup()

    def _L2_attn_setup():
        import jax, jax.numpy as jnp
        import numpy as np
        DIM = 128
        HEADS = 16
        HIDDEN = 512
        EPS_ATTN = 1e-06
        EPS_LN = 1e-05

        def layer_norm(x, g, b):
            mu = jnp.mean(x, axis=-1, keepdims=True)
            var = jnp.var(x, axis=-1, keepdims=True)
            return (x - mu) * jax.lax.rsqrt(var + EPS_LN) * g + b
        key = jax.random.key(seed)
        ks = jax.random.split(key, 8)
        s = 0.02
        return {'x': jax.random.normal(ks[0], (4, 512, DIM), jnp.float32), 'norm1_g': jnp.ones((DIM,), jnp.float32), 'norm1_b': jnp.zeros((DIM,), jnp.float32), 'qkv_w': jax.random.normal(ks[1], (3 * DIM, DIM), jnp.float32) * s, 'proj_w': jax.random.normal(ks[2], (DIM, DIM), jnp.float32) * s, 'proj_b': jnp.zeros((DIM,), jnp.float32), 'norm2_g': jnp.ones((DIM,), jnp.float32), 'norm2_b': jnp.zeros((DIM,), jnp.float32), 'fc1_w': jax.random.normal(ks[3], (HIDDEN, DIM), jnp.float32) * s, 'fc1_b': jnp.zeros((HIDDEN,), jnp.float32), 'fc2_w': jax.random.normal(ks[4], (DIM, HIDDEN), jnp.float32) * s, 'fc2_b': jnp.zeros((DIM,), jnp.float32)}
    _L2_attn_in = _L2_attn_setup()

    def _L2_ffn_setup():
        import jax, jax.numpy as jnp
        import numpy as np
        E = 16
        K = 4
        G = 4
        TG = 2
        NS = 2
        H = 128
        I = 176
        SCALE = 1.0

        def _gate(x2d, gate_w, gate_bias):
            T = x2d.shape[0]
            logits = x2d.astype(jnp.float32) @ gate_w.astype(jnp.float32).T
            scores = jax.nn.sigmoid(logits)
            sfc = scores + gate_bias[None, :]
            grp = sfc.reshape(T, G, E // G)
            top2, _ = jax.lax.top_k(grp, 2)
            group_scores = top2.sum(-1)
            _, gidx = jax.lax.top_k(group_scores, TG)
            gmask = jnp.zeros((T, G), sfc.dtype).at[jnp.arange(T)[:, None], gidx].set(1.0)
            smask = jnp.repeat(gmask, E // G, axis=1) > 0
            tmp = jnp.where(smask, sfc, 0.0)
            _, topk_idx = jax.lax.top_k(tmp, K)
            topk_w = jnp.take_along_axis(scores, topk_idx, axis=1)
            topk_w = topk_w / (topk_w.sum(-1, keepdims=True) + 1e-20)
            return (topk_idx, topk_w * SCALE)
        key = jax.random.key(seed)
        ks = jax.random.split(key, 8)
        bound = 1.0 / np.sqrt(H)
        return {'hidden_states': jax.random.normal(ks[0], (1, 128, H), jnp.float32), 'gate_w': jax.random.uniform(ks[1], (E, H), jnp.float32, -bound, bound), 'gate_bias': jnp.zeros((E,), jnp.float32), 'gate_proj': jax.random.normal(ks[2], (E, I, H), jnp.float32) * 0.02, 'up_proj': jax.random.normal(ks[3], (E, I, H), jnp.float32) * 0.02, 'down_proj': jax.random.normal(ks[4], (E, H, I), jnp.float32) * 0.02, 'shared_gate_w': jax.random.normal(ks[5], (I * NS, H), jnp.float32) * 0.02, 'shared_up_w': jax.random.normal(ks[6], (I * NS, H), jnp.float32) * 0.02, 'shared_down_w': jax.random.normal(ks[7], (H, I * NS), jnp.float32) * 0.02}
    _L2_ffn_in = _L2_ffn_setup()

    def _L3_attn_setup():
        import jax, jax.numpy as jnp
        import numpy as np
        EMBED_DIM = 128
        NUM_HEADS = 16
        BATCH = 4
        SEQ = 512
        key = jax.random.key(seed)
        ks = jax.random.split(key, 5)
        scale = 0.02
        E = EMBED_DIM
        x = jax.random.normal(ks[0], (BATCH, SEQ, E), dtype=jnp.float32)
        Wq = jax.random.normal(ks[1], (E, E), dtype=jnp.float32) * scale
        Wk = jax.random.normal(ks[2], (E, E), dtype=jnp.float32) * scale
        Wv = jax.random.normal(ks[3], (E, E), dtype=jnp.float32) * scale
        Wo = jax.random.normal(ks[4], (E, E), dtype=jnp.float32) * scale
        z = jnp.zeros((E,), dtype=jnp.float32)
        return {'x': x, 'Wq': Wq, 'bq': z, 'Wk': Wk, 'bk': z, 'Wv': Wv, 'bv': z, 'Wo': Wo, 'bo': z}
    _L3_attn_in = _L3_attn_setup()

    def _L3_ffn_setup():
        import jax, jax.numpy as jnp
        import numpy as np
        B, T, C = (2, 256, 128)
        E = 8
        K = 2
        DFF = 4 * C
        key = jax.random.key(seed)
        ks = jax.random.split(key, 7)
        s_in = 1.0 / np.sqrt(C)
        s_ff = 1.0 / np.sqrt(DFF)
        return {'inputs': jax.random.normal(ks[0], (B, T, C), dtype=jnp.float32), 'Wr': jax.random.uniform(ks[1], (C, E), jnp.float32, -s_in, s_in), 'br': jax.random.uniform(ks[2], (E,), jnp.float32, -s_in, s_in), 'W1': jax.random.uniform(ks[3], (E, C, DFF), jnp.float32, -s_in, s_in), 'b1': jax.random.uniform(ks[4], (E, DFF), jnp.float32, -s_in, s_in), 'W2': jax.random.uniform(ks[5], (E, DFF, C), jnp.float32, -s_ff, s_ff), 'b2': jax.random.uniform(ks[6], (E, C), jnp.float32, -s_ff, s_ff)}
    _L3_ffn_in = _L3_ffn_setup()
    _d = {'L0_attn_x': _L0_attn_in['x'], 'L0_attn_W_q': _L0_attn_in['W_q'], 'L0_attn_W_k': _L0_attn_in['W_k'], 'L0_attn_W_v': _L0_attn_in['W_v'], 'L0_attn_W_o': _L0_attn_in['W_o'], 'L0_ffn_ln_gamma': _L0_ffn_in['ln_gamma'], 'L0_ffn_ln_beta': _L0_ffn_in['ln_beta'], 'L0_ffn_fc1_q': _L0_ffn_in['fc1_q'], 'L0_ffn_fc1_scales': _L0_ffn_in['fc1_scales'], 'L0_ffn_fc1_bias': _L0_ffn_in['fc1_bias'], 'L0_ffn_fc2_q': _L0_ffn_in['fc2_q'], 'L0_ffn_fc2_scales': _L0_ffn_in['fc2_scales'], 'L0_ffn_fc2_bias': _L0_ffn_in['fc2_bias'], 'L1_attn_ln_gamma': _L1_attn_in['ln_gamma'], 'L1_attn_ln_beta': _L1_attn_in['ln_beta'], 'L1_attn_Wq': _L1_attn_in['Wq'], 'L1_attn_bq': _L1_attn_in['bq'], 'L1_attn_Wk': _L1_attn_in['Wk'], 'L1_attn_bk': _L1_attn_in['bk'], 'L1_attn_Wv': _L1_attn_in['Wv'], 'L1_attn_bv': _L1_attn_in['bv'], 'L1_attn_Wo': _L1_attn_in['Wo'], 'L1_attn_bo': _L1_attn_in['bo'], 'L1_attn_mu': _L1_attn_in['mu'], 'L1_ffn_w_gate': _L1_ffn_in['w_gate'], 'L1_ffn_w_up': _L1_ffn_in['w_up'], 'L1_ffn_w_down': _L1_ffn_in['w_down'], 'L2_attn_norm1_g': _L2_attn_in['norm1_g'], 'L2_attn_norm1_b': _L2_attn_in['norm1_b'], 'L2_attn_qkv_w': _L2_attn_in['qkv_w'], 'L2_attn_proj_w': _L2_attn_in['proj_w'], 'L2_attn_proj_b': _L2_attn_in['proj_b'], 'L2_attn_norm2_g': _L2_attn_in['norm2_g'], 'L2_attn_norm2_b': _L2_attn_in['norm2_b'], 'L2_attn_fc1_w': _L2_attn_in['fc1_w'], 'L2_attn_fc1_b': _L2_attn_in['fc1_b'], 'L2_attn_fc2_w': _L2_attn_in['fc2_w'], 'L2_attn_fc2_b': _L2_attn_in['fc2_b'], 'L2_ffn_gate_w': _L2_ffn_in['gate_w'], 'L2_ffn_gate_bias': _L2_ffn_in['gate_bias'], 'L2_ffn_gate_proj': _L2_ffn_in['gate_proj'], 'L2_ffn_up_proj': _L2_ffn_in['up_proj'], 'L2_ffn_down_proj': _L2_ffn_in['down_proj'], 'L2_ffn_shared_gate_w': _L2_ffn_in['shared_gate_w'], 'L2_ffn_shared_up_w': _L2_ffn_in['shared_up_w'], 'L2_ffn_shared_down_w': _L2_ffn_in['shared_down_w'], 'L3_attn_Wq': _L3_attn_in['Wq'], 'L3_attn_bq': _L3_attn_in['bq'], 'L3_attn_Wk': _L3_attn_in['Wk'], 'L3_attn_bk': _L3_attn_in['bk'], 'L3_attn_Wv': _L3_attn_in['Wv'], 'L3_attn_bv': _L3_attn_in['bv'], 'L3_attn_Wo': _L3_attn_in['Wo'], 'L3_attn_bo': _L3_attn_in['bo'], 'L3_ffn_Wr': _L3_ffn_in['Wr'], 'L3_ffn_br': _L3_ffn_in['br'], 'L3_ffn_W1': _L3_ffn_in['W1'], 'L3_ffn_b1': _L3_ffn_in['b1'], 'L3_ffn_W2': _L3_ffn_in['W2'], 'L3_ffn_b2': _L3_ffn_in['b2']}
    _x0 = _d['L0_attn_x']
    _d['L0_attn_x'] = jax.random.normal(jax.random.fold_in(jax.random.key(seed), 1), (2, 1024, 128), dtype=_x0.dtype)
    del _x0
    return _d

def reference(L0_attn_x, L0_attn_W_q, L0_attn_W_k, L0_attn_W_v, L0_attn_W_o, L0_ffn_ln_gamma, L0_ffn_ln_beta, L0_ffn_fc1_q, L0_ffn_fc1_scales, L0_ffn_fc1_bias, L0_ffn_fc2_q, L0_ffn_fc2_scales, L0_ffn_fc2_bias, L1_attn_ln_gamma, L1_attn_ln_beta, L1_attn_Wq, L1_attn_bq, L1_attn_Wk, L1_attn_bk, L1_attn_Wv, L1_attn_bv, L1_attn_Wo, L1_attn_bo, L1_attn_mu, L1_ffn_w_gate, L1_ffn_w_up, L1_ffn_w_down, L2_attn_norm1_g, L2_attn_norm1_b, L2_attn_qkv_w, L2_attn_proj_w, L2_attn_proj_b, L2_attn_norm2_g, L2_attn_norm2_b, L2_attn_fc1_w, L2_attn_fc1_b, L2_attn_fc2_w, L2_attn_fc2_b, L2_ffn_gate_w, L2_ffn_gate_bias, L2_ffn_gate_proj, L2_ffn_up_proj, L2_ffn_down_proj, L2_ffn_shared_gate_w, L2_ffn_shared_up_w, L2_ffn_shared_down_w, L3_attn_Wq, L3_attn_bq, L3_attn_Wk, L3_attn_bk, L3_attn_Wv, L3_attn_bv, L3_attn_Wo, L3_attn_bo, L3_ffn_Wr, L3_ffn_br, L3_ffn_W1, L3_ffn_b1, L3_ffn_W2, L3_ffn_b2):

    def _L0_attn_ref(x, W_q, W_k, W_v, W_o):
        import jax, jax.numpy as jnp
        import numpy as np
        D_MODEL = 128
        N_HEADS = 16
        D_K = D_MODEL // N_HEADS
        THETA = 10000.0
        MAX_SEQ = 256

        def _trunc_normal(key, shape, std):
            return jnp.clip(jax.random.normal(key, shape) * std, -3 * std, 3 * std).astype(jnp.float32)

        def _rope(x, positions):
            d = x.shape[-1]
            inv_freq = THETA ** (-2.0 * jnp.arange(0, d // 2, dtype=jnp.float32) / d)
            angles = positions.astype(jnp.float32)[:, None] * inv_freq[None, :]
            cos, sin = (jnp.cos(angles), jnp.sin(angles))
            xp = x.reshape(x.shape[:-1] + (d // 2, 2))
            x_even, x_odd = (xp[..., 0], xp[..., 1])
            out_even = x_even * cos - x_odd * sin
            out_odd = x_even * sin + x_odd * cos
            return jnp.stack((out_even, out_odd), axis=-1).reshape(x.shape)
        b, s, _ = x.shape

        def split_heads(t):
            return t.reshape(b, s, N_HEADS, D_K).transpose(0, 2, 1, 3)
        Q = split_heads(x @ W_q.T)
        K = split_heads(x @ W_k.T)
        V = split_heads(x @ W_v.T)
        pos = jnp.arange(s)
        Q = _rope(Q, pos)
        K = _rope(K, pos)
        score = jnp.einsum('bnqd,bnkd->bnqk', Q, K) / jnp.sqrt(jnp.float32(D_K))
        causal = jnp.triu(jnp.ones((s, s), dtype=bool), k=1)
        score = jnp.where(causal[None, None], -jnp.inf, score)
        attn = jax.nn.softmax(score, axis=-1)
        out = jnp.einsum('bnqk,bnkd->bnqd', attn, V)
        out = out.transpose(0, 2, 1, 3).reshape(b, s, D_MODEL)
        return out @ W_o.T

    def _L0_ffn_ref(x, ln_gamma, ln_beta, fc1_q, fc1_scales, fc1_bias, fc2_q, fc2_scales, fc2_bias):
        import jax, jax.numpy as jnp
        import numpy as np
        B, S, H, F, G = (8, 256, 128, 512, 128)
        EPS = 1e-05

        def _dequant(q, scales, g):
            K, N = q.shape
            w = (q.astype(jnp.float32) - 128.0).reshape(K // g, g, N) * scales[:, None, :]
            return w.reshape(K, N)
        residual = x
        mu = jnp.mean(x, axis=-1, keepdims=True)
        var = jnp.mean(jnp.square(x - mu), axis=-1, keepdims=True)
        h = (x - mu) * jax.lax.rsqrt(var + EPS) * ln_gamma + ln_beta
        hf = h.reshape(-1, H)
        w1 = _dequant(fc1_q, fc1_scales, G)
        y = hf @ w1 + fc1_bias
        y = jax.nn.silu(y)
        w2 = _dequant(fc2_q, fc2_scales, G)
        z = y @ w2 + fc2_bias
        return residual + 0.5 * z.reshape(residual.shape)

    def _L1_attn_ref(sequence, ln_gamma, ln_beta, Wq, bq, Wk, bk, Wv, bv, Wo, bo, mu):
        import jax, jax.numpy as jnp
        import numpy as np
        D_MODEL = 128
        N_HEADS = 16
        HEAD_DIM = D_MODEL // N_HEADS
        EPS = 1e-06

        def _split_heads(x):
            b, s, d = x.shape
            return x.reshape(b, s, N_HEADS, HEAD_DIM).transpose(0, 2, 1, 3)
        mean = jnp.mean(sequence, axis=-1, keepdims=True)
        var = jnp.mean(jnp.square(sequence - mean), axis=-1, keepdims=True)
        x = (sequence - mean) / jnp.sqrt(var + EPS) * ln_gamma + ln_beta
        q = _split_heads(x @ Wq.T + bq)
        k = _split_heads(x @ Wk.T + bk)
        v = _split_heads(x @ Wv.T + bv)
        scale = HEAD_DIM ** 0.5
        scores = jnp.einsum('bhqd,bhkd->bhqk', q, k) / scale
        scores = jax.nn.sigmoid(scores - mu) * jnp.exp(scores)
        scores = scores / jnp.sum(scores, axis=-1, keepdims=True)
        out = jnp.einsum('bhqk,bhkd->bhqd', scores, v)
        b, h, s, hd = out.shape
        out = out.transpose(0, 2, 1, 3).reshape(b, s, h * hd)
        return out @ Wo.T + bo

    def _L1_ffn_ref(x, w_gate, w_up, w_down):
        import jax, jax.numpy as jnp
        import numpy as np
        DIM = 128
        HIDDEN = 384
        SCALE = 1.0 / 127.0

        def _dequant(w_int, dtype):
            return w_int.astype(dtype) * jnp.asarray(SCALE, dtype)
        wg = _dequant(w_gate, x.dtype)
        wu = _dequant(w_up, x.dtype)
        wd = _dequant(w_down, x.dtype)
        gate = jnp.einsum('bsd,hd->bsh', x, wg)
        up = jnp.einsum('bsd,hd->bsh', x, wu)
        h = jax.nn.silu(gate) * up
        return jnp.einsum('bsh,dh->bsd', h, wd)

    def _L2_attn_ref(x, norm1_g, norm1_b, qkv_w, proj_w, proj_b, norm2_g, norm2_b, fc1_w, fc1_b, fc2_w, fc2_b):
        import jax, jax.numpy as jnp
        import numpy as np
        DIM = 128
        HEADS = 16
        HIDDEN = 512
        EPS_ATTN = 1e-06
        EPS_LN = 1e-05

        def layer_norm(x, g, b):
            mu = jnp.mean(x, axis=-1, keepdims=True)
            var = jnp.var(x, axis=-1, keepdims=True)
            return (x - mu) * jax.lax.rsqrt(var + EPS_LN) * g + b
        B, N, C = x.shape
        H = HEADS
        d = C // H
        h = layer_norm(x, norm1_g, norm1_b)
        qkv = jnp.einsum('bnc,oc->bno', h, qkv_w)
        qkv = qkv.reshape(B, N, 3, H, d)
        q = jnp.transpose(qkv[:, :, 0], (0, 2, 1, 3))
        k = jnp.transpose(qkv[:, :, 1], (0, 2, 1, 3))
        v = jnp.transpose(qkv[:, :, 2], (0, 2, 1, 3))
        q = jax.nn.elu(q) + 1.0
        k = jax.nn.elu(k) + 1.0
        kv = jnp.einsum('bhnd,bhne->bhde', k, v)
        ksum = jnp.sum(k, axis=2)
        z = 1.0 / (jnp.einsum('bhnd,bhd->bhn', q, ksum) + EPS_ATTN)
        attn_out = jnp.einsum('bhnd,bhde->bhne', q, kv) * z[..., None]
        attn_out = jnp.transpose(attn_out, (0, 2, 1, 3)).reshape(B, N, C)
        attn_out = jnp.einsum('bnc,oc->bno', attn_out, proj_w) + proj_b
        x = x + attn_out
        h = layer_norm(x, norm2_g, norm2_b)
        h = jax.nn.gelu(jnp.einsum('bnc,hc->bnh', h, fc1_w) + fc1_b, approximate=False)
        h = jnp.einsum('bnh,ch->bnc', h, fc2_w) + fc2_b
        return x + h

    def _L2_ffn_ref(hidden_states, gate_w, gate_bias, gate_proj, up_proj, down_proj, shared_gate_w, shared_up_w, shared_down_w):
        import jax, jax.numpy as jnp
        import numpy as np
        E = 16
        K = 4
        G = 4
        TG = 2
        NS = 2
        H = 128
        I = 176
        SCALE = 1.0

        def _gate(x2d, gate_w, gate_bias):
            T = x2d.shape[0]
            logits = x2d.astype(jnp.float32) @ gate_w.astype(jnp.float32).T
            scores = jax.nn.sigmoid(logits)
            sfc = scores + gate_bias[None, :]
            grp = sfc.reshape(T, G, E // G)
            top2, _ = jax.lax.top_k(grp, 2)
            group_scores = top2.sum(-1)
            _, gidx = jax.lax.top_k(group_scores, TG)
            gmask = jnp.zeros((T, G), sfc.dtype).at[jnp.arange(T)[:, None], gidx].set(1.0)
            smask = jnp.repeat(gmask, E // G, axis=1) > 0
            tmp = jnp.where(smask, sfc, 0.0)
            _, topk_idx = jax.lax.top_k(tmp, K)
            topk_w = jnp.take_along_axis(scores, topk_idx, axis=1)
            topk_w = topk_w / (topk_w.sum(-1, keepdims=True) + 1e-20)
            return (topk_idx, topk_w * SCALE)
        orig_shape = hidden_states.shape
        x = hidden_states.reshape(-1, H)
        topk_idx, topk_w = _gate(x, gate_w, gate_bias)
        combine_w = (jax.nn.one_hot(topk_idx, E, dtype=x.dtype) * topk_w[..., None]).sum(1)
        g = jnp.einsum('th,eih->tei', x, gate_proj)
        u = jnp.einsum('th,eih->tei', x, up_proj)
        act = jax.nn.silu(g) * u
        y = jnp.einsum('tei,ehi,te->th', act, down_proj, combine_w)
        sg = x @ shared_gate_w.T
        su = x @ shared_up_w.T
        y = y + jax.nn.silu(sg) * su @ shared_down_w.T
        return y.reshape(orig_shape)

    def _L3_attn_ref(x, Wq, bq, Wk, bk, Wv, bv, Wo, bo):
        import jax, jax.numpy as jnp
        import numpy as np
        EMBED_DIM = 128
        NUM_HEADS = 16
        BATCH = 4
        SEQ = 512
        B, S, E = x.shape
        H = NUM_HEADS
        D = E // H

        def proj(W, b):
            return (jnp.einsum('bse,fe->bsf', x, W) + b).reshape(B, S, H, D)
        q = jax.nn.elu(proj(Wq, bq)) + 1.0
        k = jax.nn.elu(proj(Wk, bk)) + 1.0
        v = proj(Wv, bv)
        kv = jnp.einsum('bshd,bshe->bhde', k, v)
        out = jnp.einsum('bshd,bhde->bshe', q, kv).reshape(B, S, E)
        out = jnp.einsum('bse,fe->bsf', out, Wo) + bo
        return out

    def _L3_ffn_ref(inputs, Wr, br, W1, b1, W2, b2):
        import jax, jax.numpy as jnp
        import numpy as np
        B, T, C = (2, 256, 128)
        E = 8
        K = 2
        DFF = 4 * C
        scores = jax.nn.softmax(inputs @ Wr + br, axis=-1)
        _, top_idx = jax.lax.top_k(scores, K)
        mask = jax.nn.one_hot(top_idx, E, dtype=scores.dtype).sum(-2)
        masked = jnp.where(mask > 0, scores, -jnp.inf)
        weights = jax.nn.softmax(masked, axis=-1)
        hid = jax.nn.gelu(jnp.einsum('btc,ecd->bted', inputs, W1) + b1, approximate=False)
        expert_out = jnp.einsum('bted,edc->btec', hid, W2) + b2
        expert_out = jnp.where(jnp.isnan(expert_out), 0.0, expert_out)
        return jnp.einsum('bte,btec->btc', weights, expert_out)
    x = L0_attn_x
    x = x + _layernorm(_L0_attn_ref(_layernorm(x, axis=-1), L0_attn_W_q, L0_attn_W_k, L0_attn_W_v, L0_attn_W_o), axis=-1)
    x = x + _layernorm(_L0_ffn_ref(_layernorm(x, axis=-1), L0_ffn_ln_gamma, L0_ffn_ln_beta, L0_ffn_fc1_q, L0_ffn_fc1_scales, L0_ffn_fc1_bias, L0_ffn_fc2_q, L0_ffn_fc2_scales, L0_ffn_fc2_bias), axis=-1)
    x = x + _layernorm(_L1_attn_ref(_layernorm(x, axis=-1), L1_attn_ln_gamma, L1_attn_ln_beta, L1_attn_Wq, L1_attn_bq, L1_attn_Wk, L1_attn_bk, L1_attn_Wv, L1_attn_bv, L1_attn_Wo, L1_attn_bo, L1_attn_mu), axis=-1)
    x = x + _layernorm(_L1_ffn_ref(_layernorm(x, axis=-1), L1_ffn_w_gate, L1_ffn_w_up, L1_ffn_w_down), axis=-1)
    x = x + _layernorm(_L2_attn_ref(_layernorm(x, axis=-1), L2_attn_norm1_g, L2_attn_norm1_b, L2_attn_qkv_w, L2_attn_proj_w, L2_attn_proj_b, L2_attn_norm2_g, L2_attn_norm2_b, L2_attn_fc1_w, L2_attn_fc1_b, L2_attn_fc2_w, L2_attn_fc2_b), axis=-1)
    x = x + _layernorm(_L2_ffn_ref(_layernorm(x, axis=-1), L2_ffn_gate_w, L2_ffn_gate_bias, L2_ffn_gate_proj, L2_ffn_up_proj, L2_ffn_down_proj, L2_ffn_shared_gate_w, L2_ffn_shared_up_w, L2_ffn_shared_down_w), axis=-1)
    x = x + _layernorm(_L3_attn_ref(_layernorm(x, axis=-1), L3_attn_Wq, L3_attn_bq, L3_attn_Wk, L3_attn_bk, L3_attn_Wv, L3_attn_bv, L3_attn_Wo, L3_attn_bo), axis=-1)
    x = x + _layernorm(_L3_ffn_ref(_layernorm(x, axis=-1), L3_ffn_Wr, L3_ffn_br, L3_ffn_W1, L3_ffn_b1, L3_ffn_W2, L3_ffn_b2), axis=-1)
    return x

_drawn_inputs = setup_inputs


def setup_inputs(seed=0):
    import zlib

    import numpy as np

    out = dict(_drawn_inputs(seed))
    spreads = {'L0_ffn_ln_gamma': (1.0, 0.2),
     'L0_ffn_ln_beta': (0.0, 0.1),
     'L1_attn_ln_gamma': (1.0, 0.2),
     'L1_attn_ln_beta': (0.0, 0.1),
     'L1_attn_bq': (0.0, 0.661),
     'L1_attn_bk': (0.0, 2.0),
     'L1_attn_bv': (0.0, 0.1),
     'L1_attn_bo': (0.0, 0.1),
     'L2_attn_norm1_g': (1.0, 0.6),
     'L2_attn_norm1_b': (0.0, 0.551),
     'L2_attn_proj_b': (0.0, 0.1),
     'L2_attn_norm2_g': (1.0, 0.6),
     'L2_attn_norm2_b': (0.0, 0.634),
     'L2_attn_fc1_b': (0.0, 0.281),
     'L2_attn_fc2_b': (0.0, 0.1),
     'L2_ffn_gate_bias': (0.0, 0.1),
     'L3_attn_bq': (0.0, 0.293),
     'L3_attn_bk': (0.0, 0.329),
     'L3_attn_bv': (0.0, 0.1),
     'L3_attn_bo': (0.0, 2.0)}
    factors = {'L0_ffn_fc1_bias': 4.704,
     'L0_ffn_fc2_bias': 7.349,
     'L1_attn_Wq': 3.183,
     'L1_attn_Wk': 2.771}
    for name, (base, spread) in spreads.items():
        noise = np.random.default_rng([zlib.crc32(name.encode()), seed]).standard_normal(out[name].shape)
        drawn = base * np.exp(spread * noise) if base else spread * noise
        out[name] = jnp.asarray(drawn.astype(out[name].dtype))
    for name, factor in factors.items():
        out[name] = (out[name] * factor).astype(out[name].dtype)
    return out
```

```python
import concourse.bass as bass
from concourse import mybir
from contextlib import ExitStack

F32 = mybir.dt.float32
BF16 = mybir.dt.bfloat16
I32 = mybir.dt.int32
ALU = mybir.AluOpType
ACT = mybir.ActivationFunctionType
AX = mybir.AxisListType

P = 128
D = 128
B = 2
S = 1024
TOK = B * S
NT = TOK // P
CH = 512
NC = TOK // CH
TPC = CH // P
H = 16
HD = D // H
HG = 4
NG = B * H // HG
KT = S // P
QH = S // CH
VC = 16
TERMS = 6
ROWS = TERMS * HD
PADDED = 53
SHIFT = 3
Q_PART = (0, 0, 0, 1, 1, 2)
K_PART = (0, 1, 2, 0, 1, 0)
BF16_BIG = 0xF180
BF16_ONE = 0x3F80
SCORE_SCALE = float(HD) ** -0.5
EPS = 1e-5
E2, I2, NS2 = 16, 176, 2
R2 = 25
HID2 = E2 * I2
E3, F3 = 8, 512

COLS = dict(g0=0, b0=1, s1=2, fb1=6, g1=10, bb1=11, bq1=12, bk1=13, mu=14, g2a=15, b2a=16,
            g2b=17, b2b=18, fb2=19, bq3=23, bk3=24, eb1=25, eb2=57)
NCOLS = 65
RW = dict(fc2b=0, bv1=128, bo1=256, pb2=384, fc2b2=512, bkv3=640, bo3=896)
NROWS = 1024
WM = dict(q0=0, qs0=1, k0=2, ks0=3, v0=4, o0=5, q1=6, k1=7, v1=8, o1=9, q2=10, kv2=11, p2=13,
          q3=14, kv3=15, o3=17)
NW = 18


def sandwich(nc, x, w, cols, rows, rope, fc1q, fc2q, s2row, l1int, l2fc, r2w, r2b, moe2, moe2sel,
             r3w, r3b, moe3a, moe3b, consts, out, only=None):
    def on(n):
        return only is None or n == only

    ctx = ExitStack()
    with ctx:
        def sb(name, shape, dt=F32):
            return ctx.enter_context(nc.sbuf_tensor(name, shape, dt))

        def sem(name):
            return ctx.enter_context(nc.semaphore(name))

        X = sb("X", [P, TOK])
        XH = sb("XH", [P, TOK])
        XN = sb("XN", [P, TOK])
        hT = sb("hT", [P, TOK])
        ARENA = sb("ARENA", [P, 32768])
        QS = [sb(f"QS{i}", [P, 2, S], BF16) for i in range(2)]
        KS = [sb(f"KS{i}", [P, 2, S], BF16) for i in range(2)]
        Vg = [sb(f"Vg{i}", [P, KT, HG, VC]) for i in range(2)]
        OS = sb("OS", [P, CH])
        NM = [sb(f"NM{i}", [P, HG * KT]) for i in range(2)]
        NR = sb("NR", [P, HG * KT])
        NB = [sb(f"NB{i}", [P, SHIFT, HG * KT], BF16) for i in range(2)]
        MT = sb("MT", [SHIFT * HG * KT, P], BF16)
        G2 = [sb(f"G{i}", [P, 2 * CH]) for i in range(2)]
        R4 = sb("R4", [P, TPC, HG])
        NMU = sb("NMU", [P, 1])
        W = sb("W", [P, NW, D])
        C = sb("C", [P, NCOLS])
        RWS = sb("RWS", [1, NROWS])
        ident = sb("ident", [P, P])
        identb = sb("identb", [P, P], BF16)
        maskA = sb("maskA", [P, P], BF16)
        maskB = sb("maskB", [P, P], BF16)
        ones1 = sb("ones1", [1, P])
        ST = sb("ST", [P, NT * 6])
        MV = sb("MV", [P, NT, 2])
        VR = sb("VR", [P, NT])
        SD = sb("SD", [P, NT])
        RS = sb("RS", [P, NT])
        RS2 = sb("RS2", [P, NT])
        SMALL = sb("SMALL", [P, 16])
        EPSC = sb("EPSC", [P, 2])
        PS = ctx.enter_context(nc.psum_tensor("PS", [P, 8 * CH], F32))

        def bank(i, a=0, b=CH):
            return PS[:, i * CH + a:i * CH + b]

        Yp = PS[:, 4 * CH:8 * CH]
        Vall = XH
        AT = XN

        def tile(buf, t):
            if isinstance(t, int):
                return buf[:, t * D:(t + 1) * D]
            return buf[:, bass.ds(t * D, D)]

        def chunk(buf, c):
            if isinstance(c, int):
                return buf[:, c * CH:(c + 1) * CH]
            return buf[:, bass.ds(c * CH, CH)]

        def col(name, n=0):
            return C[:, COLS[name] + n:COLS[name] + n + 1]

        def arena(at, n):
            return ARENA[:, at:at + n]
        PB = [arena(2048 * i, 2048).rearrange("p (h q) -> p h q", h=HG) for i in range(3)]
        COS = arena(6144, S)
        SIN = arena(6144 + S, S)
        PARTS = ARENA[:, 8192:8192 + 6144].bitcast(BF16).rearrange("p (m t n) -> p m t n", m=2, t=3)
        TA = arena(14336, CH)
        TB = arena(14336 + CH, CH)
        QF = [arena(14336 + 2 * CH, CH), arena(14336 + 3 * CH, CH)]
        EX = ARENA[:, :].rearrange("p (a k h q) -> p a k h q", a=QH, k=KT, h=HG)

        qx = nc.dram_tensor("qx", (B * H, ROWS, S), BF16, kind="Internal").ap()
        kx = nc.dram_tensor("kx", (B * H, ROWS, S), BF16, kind="Internal").ap()
        mx = nc.dram_tensor("mx", (2, SHIFT * HG * KT, P), BF16, kind="Internal").ap()

        x_in = sem("x_in")
        w_in = sem("w_in")
        c_in = sem("c_in")
        rope_in = sem("rope_in")
        cbase = sem("cbase")
        v_own = sem("v_own")
        a_own = sem("a_own")
        p_own = sem("p_own")
        var_ready = sem("var_ready")
        sd_ready = sem("sd_ready")
        xn_ready = sem("xn_ready")
        xt_ready = sem("xt_ready")
        h_ready = sem("h_ready")
        y_ready = sem("y_ready")
        x_done = sem("x_done")
        out_done = sem("out_done")

        n_r = [0, 0]
        n_in = [0, 0, 0]
        n_y = [0, 0]

        class Own:

            def __init__(self, eng, s):
                self.eng, self.s, self.n = eng, s, 0

            def mark(self, ins):
                ins.then_inc(self.s, 1)
                self.n += 1

            def wait(self):
                self.eng.wait_ge(self.s, self.n)

            def link(self, ins):
                self.mark(ins)
                self.wait()

        def dve_stats(dve, own, src, wait_chunk=None):
            with dve.Fori(0, NC) as c:
                if wait_chunk is not None:
                    wait_chunk(c)
                for k in range(TPC):
                    ins = dve.bn_stats(ST[:, bass.ds((c * TPC + k) * 6, 6)], src(c * TPC + k))
                ins.then_inc(v_own, 1)
            own.n += NC
            own.wait()
            for t in range(NT):
                ins = dve.bn_aggr(MV[:, t, :], ST[:, t * 6:t * 6 + 6])
            own.link(ins)

        def dve_rsqrt(dve, own, dst, variance):
            dve.tensor_copy(VR[:, :], variance).then_inc(var_ready, 1)
            n_r[0] += 1
            dve.wait_ge(sd_ready, n_r[0])
            own.link(dve.reciprocal(dst, SD[:, :]))

        def act_sqrt(act, eps_ap):
            n_r[1] += 1
            act.wait_ge(var_ready, n_r[1])
            act.activation(SD[:, :], VR[:, :], ACT.Sqrt, bias=eps_ap).then_inc(sd_ready, 1)

        def dve_ln_in(dve, own, second=False, keep=False):
            dve_stats(dve, own, lambda t: tile(X, t))
            dve_rsqrt(dve, own, RS[:, :], MV[:, :, 1])
            scale = RS
            if second:
                own.link(dve.tensor_tensor(RS2[:, :], MV[:, :, 1], RS[:, :], ALU.mult))
                own.link(dve.tensor_tensor(RS2[:, :], RS2[:, :], RS[:, :], ALU.mult))
                dve_rsqrt(dve, own, RS2[:, :], RS2[:, :])
                own.link(dve.tensor_tensor(RS2[:, :], RS2[:, :], RS[:, :], ALU.mult))
                scale = RS2
            dve_apply(dve, own, XN, X, scale)
            if keep:
                for t in range(NT):
                    ins = dve.tensor_scalar(tile(XH, t), tile(X, t), MV[:, t, 0:1], RS[:, t:t + 1],
                                            ALU.subtract, ALU.mult)
                own.link(ins)

        def dve_apply(dve, own, dst, src, scale):
            for t in range(NT):
                ins = dve.tensor_scalar(tile(dst, t), tile(src, t), MV[:, t, 0:1], scale[:, t:t + 1],
                                        ALU.subtract, ALU.mult)
                if t % TPC == TPC - 1:
                    ins.then_inc(xn_ready, 1)

        def pe_turn(pe):
            for t in range(NT):
                if t % TPC == 0:
                    pe.wait_ge(xn_ready, n_in[1] + t // TPC + 1)
                ins = pe.transpose(PS[:, t * D:(t + 1) * D], tile(XN, t), ident[:, :])
                if t % TPC == TPC - 1:
                    ins.then_inc(xt_ready, 1)
            n_in[1] += NC

        def act_turned(act, scale=1.0, bias=None):
            for c in range(NC):
                act.wait_ge(xt_ready, n_in[2] + c + 1)
                if bias is None:
                    ins = act.activation(chunk(hT, c), bank(c), ACT.Copy)
                else:
                    ins = act.activation(chunk(hT, c), bank(c), ACT.Identity, scale=scale, bias=bias)
                ins.then_inc(h_ready, 1)
            n_in[2] += NC

        def dve_ln_out(dve, own, src, waits=True):
            dve_stats(dve, own, src, (lambda c: dve.wait_ge(y_ready, n_y[0] + c + 1)) if waits else None)
            n_y[0] += NC
            dve_rsqrt(dve, own, RS[:, :], MV[:, :, 1])
            for t in range(NT):
                ins = dve.tensor_scalar(tile(XN, t), src(t), MV[:, t, 0:1], RS[:, t:t + 1],
                                        ALU.subtract, ALU.mult)
                if t % TPC == TPC - 1:
                    own.mark(ins)
            for c in range(NC):
                dve.wait_ge(v_own, own.n - NC + c + 1)
                ins = dve.tensor_tensor(chunk(X, c), chunk(X, c), chunk(XN, c), ALU.add)
            own.mark(ins)
            own.wait()

        A = {}

        def sems(L, names):
            for nm in names.split():
                A[L, nm] = sem(f"L{L}_{nm}")

        COMMON = "proj qf rope part0 res part1 part2 vt vall q_wr ld0 ld1 vg o_sb ot ot_free aT aTs "
        sems(0, COMMON + "a_mm a_red b_mm b_exp pv nm nmt mt m_wr m_ld0 m_ld1")
        sems(1, COMMON + "s_mm s_act mul pv")

        def group_rows(t, g, hh):
            v = t.rearrange("(g p x) r n -> g x r p n", p=2, x=2)
            if isinstance(g, int):
                return v[g, hh]
            return v[bass.ds(g, 1), hh].rearrange("g r p n -> (g r) p n")

        def gcols(buf, g, a, b):
            if isinstance(g, int):
                return buf[:, g * 256 + a:g * 256 + b]
            return buf[:, bass.ds(g * 256 + a, b - a)]

        def group_place(g, qh):
            v = AT[:, :].rearrange("p (b a i g e) -> p b a g i e", b=B, a=QH, i=TPC, g=HG)
            if isinstance(g, int):
                w = v[:, g // HG, qh, g % HG]
            else:
                w = v[:, bass.ds(g // HG, 1), qh, bass.ds(g % HG, 1)].rearrange("p b g i e -> p (b g i) e")
            return w.rearrange("p i (h d) -> p i h d", h=HG)

        def pe_values(pe, L, n_h, vbias):
            pe.wait_ge(h_ready, n_h)
            if vbias is not None:
                pe.wait_ge(cbase, NBASE)
            for t in range(NT):
                dst = PS[:, 4 * CH + t * D:4 * CH + (t + 1) * D]
                ins = pe.matmul(dst, tile(hT, t), W[:, WM[f"v{L}"], :], start=True, stop=vbias is None)
                if vbias is not None:
                    ins = pe.matmul(dst, ones1[:, :], RWS[:, vbias:vbias + D], start=False, stop=True)
                if t % TPC == TPC - 1:
                    ins.then_inc(A[L, "vt"], 1)

        def act_values(act, L):
            dst = Vall[:, :].rearrange("p (b g k e) -> p b g k e", b=B, g=HG, k=KT)
            for c in range(NC):
                act.wait_ge(A[L, "vt"], c + 1)
                k0 = (c % QH) * TPC
                act.activation(dst[:, c // QH, :, k0:k0 + TPC, :],
                               bank(4 + c).rearrange("p (k g e) -> p g k e", k=TPC, g=HG), ACT.Copy)\
                   .then_inc(A[L, "vall"], 1)

        def pool_group_values(pool, L, g, par):
            pool.tensor_copy(Vg[par][:, :, :, 0:HD],
                             gcols(Vall, g, 0, 256).rearrange("p (k h d) -> p k h d", k=KT, h=HG))\
                .then_inc(A[L, "vg"], 1)

        def pe_project(pe, L, mats):
            for c in range(NC):
                if c == 1:
                    pe.wait_ge(A[L, "vall"], NC)
                if c >= 2:
                    pe.wait_ge(A[L, "qf"], 2 * (c - 1))
                for m, name in enumerate(mats):
                    ins = pe.matmul(bank(4 * (c % 2) + m), W[:, WM[name], :], chunk(hT, c),
                                    start=True, stop=True)
                ins.then_inc(A[L, "proj"], 1)

        def dve_rope(dve, L):
            for i in range(2 * NC):
                c, m = divmod(i, 2)
                pos = slice((c % QH) * CH, (c % QH) * CH + CH)
                dve.wait_ge(A[L, "proj"], c + 1)
                if i:
                    dve.wait_ge(A[L, "qf"], i)
                dve.tensor_tensor(TA, bank(4 * (c % 2) + 2 * m), COS[:, pos], ALU.mult)
                dve.tensor_tensor(TB, bank(4 * (c % 2) + 2 * m + 1), SIN[:, pos], ALU.mult)\
                   .then_inc(A[L, "rope"], 1)
                dve.wait_ge(A[L, "rope"], i + 1)
                if i >= 2:
                    dve.wait_ge(A[L, "part2"], i - 1)
                dve.tensor_tensor(QF[m], TA, TB, ALU.add).then_inc(A[L, "qf"], 1)

        def act_split_one(act, L, i):
            c, m = divmod(i, 2)
            dst = PARTS[:, m, :, c * CH:(c + 1) * CH]
            act.wait_ge(A[L, "qf"], i + 1)
            act.activation(dst[:, 0], QF[m], ACT.Copy).then_inc(A[L, "part0"], 1)
            act.wait_ge(A[L, "res"], i + 1)
            act.activation(dst[:, 1], QF[m], ACT.Copy).then_inc(A[L, "part1"], 1)

        def act_split(act, L):
            for i in range(2 * NC):
                act_split_one(act, L, i)

        def act_bias_split(act, L):
            for i in range(2 * NC):
                c, m = divmod(i, 2)
                act.wait_ge(A[L, "proj"], c + 1)
                if i >= 2:
                    act.wait_ge(A[L, "part2"], i - 1)
                act.activation(QF[m], bank(4 * (c % 2) + m), ACT.Identity,
                               bias=col(("bq1", "bk1")[m])).then_inc(A[L, "qf"], 1)
                act_split_one(act, L, i)

        def pool_split(pool, L):
            for i in range(2 * NC):
                c, m = divmod(i, 2)
                dst = PARTS[:, m, :, c * CH:(c + 1) * CH]
                pool.wait_ge(A[L, "part0"], i + 1)
                pool.tensor_tensor(QF[m], QF[m], dst[:, 0], ALU.subtract).then_inc(A[L, "res"], 1)
                pool.wait_ge(A[L, "res"], i + 1)
                pool.wait_ge(A[L, "part1"], i + 1)
                pool.tensor_tensor(dst[:, 2], QF[m], dst[:, 1], ALU.subtract)\
                    .then_inc(A[L, "part2"], 1)

        def sp_stack(sp, L):
            for b in range(B):
                sp.wait_ge(A[L, "part2"], 2 * QH * (b + 1))
                for m, (dst, parts) in enumerate(((qx, Q_PART), (kx, K_PART))):
                    for t, part in enumerate(parts):
                        sp.dma_start(dst[b * H:(b + 1) * H, t * HD:(t + 1) * HD, :],
                                     PARTS[:, m, part, b * S:(b + 1) * S]).then_inc(A[L, "q_wr"], 16)
            sp.wait_ge(A[L, "q_wr"], 16 * B * 2 * TERMS)

        def sp_load_group(sp, L, g, par):
            for hh in range(2):
                for dst, src in ((QS[par], qx), (KS[par], kx)):
                    sp.dma_start(dst[64 * hh:64 * hh + ROWS, :, :], group_rows(src, g, hh))\
                      .then_inc(A[L, f"ld{par}"], 16)
        LD = 64

        def act_out(act, L, g, qh, pv):
            act.wait_ge(A[L, "pv"], pv)
            act.wait_ge(A[L, "ot"], QH * g + qh)
            act.activation(OS[:, :], bank(6), ACT.Copy).then_inc(A[L, "o_sb"], 1)

        def pe_out(pe, L, g, qh):
            pe.wait_ge(A[L, "o_sb"], QH * g + qh + 1)
            pe.wait_ge(A[L, "ot_free"], QH * g + qh)
            for i in range(TPC):
                ins = pe.transpose(bank(7, i * P, i * P + P), OS[:, i * P:i * P + P], ident[:, :])
            ins.then_inc(A[L, "ot"], 1)

        def dve_out(dve, own, L, g, qh):
            dve.wait_ge(A[L, "ot"], QH * g + qh + 1)
            v = bank(7).rearrange("p (i h e) -> p i h e", i=TPC, h=HG)
            dve.reciprocal(R4[:, :, :], v[:, :, :, HD]).then_inc(A[L, "rope"], 1)
            rope0 = 2 * NC if L == 0 else 0
            dve.wait_ge(A[L, "rope"], rope0 + QH * g + qh + 1)
            dve.tensor_tensor(group_place(g, qh),
                              v[:, :, :, 0:HD], R4[:, :, :].unsqueeze(3).broadcast_to([P, TPC, HG, HD]),
                              ALU.mult).then_inc(A[L, "ot_free"], 1)

        def pe_attention_end(pe, L, out_w, bias):
            pe.wait_ge(A[L, "ot_free"], QH * NG)
            for t in range(NT):
                ins = pe.transpose(PS[:, t * D:(t + 1) * D], tile(AT, t), ident[:, :])
                if t % TPC == TPC - 1:
                    ins.then_inc(A[L, "aT"], 1)
            for t in range(NT):
                if t % TPC == 0:
                    pe.wait_ge(A[L, "aTs"], t // TPC + 1)
                pe_y(pe, t, [(tile(hT, t), W[:, WM[out_w], :])], bias)

        def pe_y(pe, t, pairs, bias, at=4 * CH, ready=None):
            dst = PS[:, at + t * D:at + (t + 1) * D]
            for n, (a, b) in enumerate(pairs):
                ins = pe.matmul(dst, a, b, start=n == 0, stop=bias is None and n == len(pairs) - 1)
            if bias is not None:
                ins = pe.matmul(dst, ones1[:, :], RWS[:, bias:bias + D], start=False, stop=True)
            if t % TPC == TPC - 1:
                ins.then_inc(ready or y_ready, 1)

        def act_attention_end(act, L):
            for c in range(NC):
                act.wait_ge(A[L, "aT"], c + 1)
                act.activation(chunk(hT, c), bank(c), ACT.Copy).then_inc(A[L, "aTs"], 1)

        STEPS = [(qh, kt) for qh in range(QH) for kt in range(TPC * (qh + 1))]
        NSTEP = len(STEPS)
        NU = HG * KT
        EXP0, PV0 = 1, 2
        UNITS = [0, 2] + [3] * 10
        UNIT0 = [sum(UNITS[:s]) for s in range(NSTEP + 1)]
        TURN0 = 6

        def operands(par, h, rows):
            hh, p = h % 2, h // 2
            return QS[par][64 * hh:64 * hh + rows, p, :], KS[par][64 * hh:64 * hh + rows, p, :]

        def pe_max_unit(pe, g, par, u):
            h, qt = divmod(u, KT)
            q, k = operands(par, h, PADDED)
            at = (u % 2) * 2 * CH
            n = (qt + 1) * P
            if not (isinstance(g, int) and g == 0 and u < 2):
                pe.wait_ge(A[0, "a_red"], NU * g + u - 1)
            for lo in range(0, n, CH):
                hi = min(n, lo + CH)
                diag = lo <= qt * P < hi
                ins = pe.matmul(PS[:, at + lo:at + hi], q[:, qt * P:qt * P + P], k[:, lo:hi],
                                start=True, stop=not diag)
                if diag:
                    ins = pe.matmul(PS[:, at + qt * P:at + qt * P + P], identb[:, :], maskA[:, :],
                                    start=False, stop=True)
            ins.then_inc(A[0, "a_mm"], 1)

        def dve_max_unit(dve, g, par, u):
            h, qt = divmod(u, KT)
            at = (u % 2) * 2 * CH
            dve.wait_ge(A[0, "a_mm"], NU * g + u + 1)
            dve.tensor_reduce(out=NM[par][:, u:u + 1], in_=PS[:, at:at + (qt + 1) * P], axis=AX.X,
                              op=ALU.max, negate=True).then_inc(A[0, "a_red"], 1)

        def dve_max_parts(dve, g, par):
            dve.wait_ge(A[0, "a_red"], NU * g + NU)
            dve.tensor_copy(NB[par][:, 0], NM[par][:, :]).then_inc(A[0, "nm"], 1)
            dve.wait_ge(A[0, "nm"], 4 * g + 1)
            dve.tensor_tensor(NR[:, :], NM[par][:, :], NB[par][:, 0], ALU.subtract).then_inc(A[0, "nm"], 1)
            dve.wait_ge(A[0, "nm"], 4 * g + 2)
            dve.tensor_copy(NB[par][:, 1], NR[:, :]).then_inc(A[0, "nm"], 1)
            dve.wait_ge(A[0, "nm"], 4 * g + 3)
            dve.tensor_tensor(NB[par][:, 2], NR[:, :], NB[par][:, 1], ALU.subtract).then_inc(A[0, "nm"], 1)

        NROW = SHIFT * NU

        def pe_max_turn(pe, g, par, outs):
            pe.wait_ge(A[0, "nm"], 4 * g + 4)
            if outs is not None:
                pe.wait_ge(A[0, "ot_free"], outs)
            pe.transpose(bank(7).bitcast(BF16)[0:NROW, 0:P], NB[par][:, :, :].rearrange("p t n -> p (t n)"),
                         identb[:, :]).then_inc(A[0, "nmt"], 1)

        def act_max_rows(act, g):
            act.wait_ge(A[0, "nmt"], g + 1)
            act.wait_ge(A[0, "m_wr"], 16 * g)
            act.activation(MT[:, :], bank(7).bitcast(BF16)[0:NROW, 0:P], ACT.Copy)\
               .then_inc(A[0, "mt"], 1)

        def sp_max_rows(sp, g, par):
            sp.wait_ge(A[0, "mt"], g + 1)
            sp.dma_start(mx[par], MT[:, :]).then_inc(A[0, "m_wr"], 16)
            sp.wait_ge(A[0, "m_wr"], 16 * g + 16)
            v = mx[par].rearrange("(t p x k) q -> x t p (k q)", t=SHIFT, p=2, x=2)
            for hh in range(2):
                sp.dma_start(QS[par][64 * hh + PADDED:64 * hh + PADDED + SHIFT, :, :], v[hh])\
                  .then_inc(A[0, f"m_ld{par}"], 16)

        def pe_scores(pe, g, par, s):
            qh, kt = STEPS[s]
            q0 = max(0, kt * P - qh * CH)
            for h in range(HG):
                q, k = operands(par, h, PADDED + SHIFT)
                pe.wait_ge(A[0, "b_exp"], HG * NSTEP * g + HG * s + h - 1 + EXP0)
                diag = kt // TPC == qh
                ins = pe.matmul(bank(4 + h % 2, q0), k[:, kt * P:kt * P + P],
                                q[:, qh * CH + q0:qh * CH + CH], start=True, stop=not diag)
                if diag:
                    ins = pe.matmul(bank(4 + h % 2, q0, q0 + P), identb[:, :], maskB[:, :],
                                    start=False, stop=True)
                ins.then_inc(A[0, "b_mm"], 1)

        def act_weights(act, g, s):
            qh, kt = STEPS[s]
            q0 = max(0, kt * P - qh * CH)
            act.wait_ge(A[0, "pv"], NSTEP * g + s - 2 + PV0)
            for h in range(HG):
                act.wait_ge(A[0, "b_mm"], HG * NSTEP * g + HG * s + h + 1)
                act.activation(PB[s % 3][:, h, q0:CH], bank(4 + h % 2, q0), ACT.Exp, scale=SCORE_SCALE)\
                   .then_inc(A[0, "b_exp"], 1)

        def pe_weighted(pe, g, par, s):
            qh, kt = STEPS[s]
            q0 = max(0, kt * P - qh * CH)
            pe.wait_ge(A[0, "b_exp"], HG * (NSTEP * g + s + 1) + EXP0)
            if kt == 0:
                pe.wait_ge(A[0, "o_sb"], QH * g + qh)
                pe.wait_ge(A[0, "vg"], g + 1)
            last = kt == TPC * (qh + 1) - 1
            for h in range(HG):
                ins = pe.matmul(PS[32 * h:32 * h + VC, 6 * CH + q0:7 * CH], Vg[par][:, kt, h, :],
                                PB[s % 3][:, h, q0:CH], start=kt == 0, stop=last)
            ins.then_inc(A[0, "pv"], 1)

        HALF = [TPC, NSTEP]

        def pe_causal(pe, g, par, i, more):
            pe.wait_ge(A[0, f"m_ld{par}"], 32 * (i + 1))
            for s in range(NSTEP):
                pe_scores(pe, g, par, s)
                if s:
                    pe_weighted(pe, g, par, s - 1)
                if s == TURN0:
                    pe_out(pe, 0, g, 0)
                if more:
                    if UNITS[s] and UNIT0[s] == 0:
                        pe.wait_ge(A[0, f"ld{1 - par}"], LD * (i + 1 + par))
                    for u in range(UNIT0[s], UNIT0[s + 1]):
                        pe_max_unit(pe, g + 1, 1 - par, u)
            pe_weighted(pe, g, par, NSTEP - 1)
            if more:
                pe_max_turn(pe, g + 1, 1 - par, QH * g + 1)
                pe.wait_ge(A[0, "mt"], g + 2)
            pe_out(pe, 0, g, 1)

        def dve_causal(dve, own, g, par, more):
            for s in range(NSTEP):
                if s == TURN0:
                    dve_out(dve, own, 0, g, 0)
                if more:
                    for u in range(UNIT0[s], UNIT0[s + 1]):
                        dve_max_unit(dve, g + 1, 1 - par, u)
            if more:
                dve_max_parts(dve, g + 1, 1 - par)
            dve_out(dve, own, 0, g, 1)

        def act_causal(act, g, more):
            for s in range(NSTEP):
                act_weights(act, g, s)
                if s == TURN0 - 1:
                    act_out(act, 0, g, 0, NSTEP * g + HALF[0] + PV0)
            act_out(act, 0, g, 1, NSTEP * g + HALF[1] + PV0)
            if more:
                act_max_rows(act, g + 1)

        def sp_causal(sp, g, par):
            sp.wait_ge(A[0, "pv"], NSTEP * g + PV0)
            sp_load_group(sp, 0, g + 1, 1 - par)
            sp_max_rows(sp, g + 1, 1 - par)

        def pool_causal(pool, g, par):
            pool.wait_ge(A[0, "pv"], NSTEP * g + PV0)
            pool_group_values(pool, 0, g + 1, 1 - par)

        def over_groups(eng, step):
            with eng.Fori(0, NG // 2 - 1) as i:
                step(2 * i, 0, i, True)
                step(2 * i + 1, 1, i, True)
            step(NG - 2, 0, NG // 2 - 1, True)
            step(NG - 1, 1, NG // 2 - 1, False)

        NW2 = QH * KT
        NU2 = 2 * NW2
        TURN2 = 12

        def pe_pair(pe, g, par, u, pss):
            s, p = divmod(u, 2)
            qh, kt = divmod(s, KT)
            v = NU2 * pss + u
            if v >= 3:
                pe.wait_ge(A[1, "s_act"], 2 * NU2 * g + v - 2)
            else:
                pe.wait_ge(A[1, "s_act"], 2 * NU2 * g)
            at = (v % 3) * 2 * CH
            for hh in range(2):
                q, k = operands(par, 2 * p + hh, PADDED)
                ins = pe.matmul(PS[:, at + hh * CH:at + (hh + 1) * CH], k[:, kt * P:kt * P + P],
                                q[:, qh * CH:(qh + 1) * CH], start=True, stop=True)
            ins.then_inc(A[1, "s_mm"], 1)

        def pe_weighted2(pe, g, par, s):
            qh, kt = divmod(s, KT)
            pe.wait_ge(A[1, "mul"], NU2 * g + 2 * s + 2)
            if kt == 0:
                pe.wait_ge(A[1, "o_sb"], QH * g + qh)
                pe.wait_ge(A[1, "vg"], g + 1)
            for h in range(HG):
                ins = pe.matmul(PS[32 * h:32 * h + VC, 6 * CH:7 * CH], Vg[par][:, kt, h, :],
                                EX[:, qh, kt, h, :], start=kt == 0, stop=kt == KT - 1)
            ins.then_inc(A[1, "pv"], 1)

        def pe_gated(pe, g, par, i):
            pe.wait_ge(A[1, f"ld{par}"], LD * (i + 1))
            for u in range(NU2):
                pe_pair(pe, g, par, u, 0)
            for s in range(NW2):
                pe_pair(pe, g, par, 2 * s, 1)
                pe_pair(pe, g, par, 2 * s + 1, 1)
                if s >= 2:
                    pe_weighted2(pe, g, par, s - 2)
                if s == TURN2:
                    pe_out(pe, 1, g, 0)
            pe_weighted2(pe, g, par, NW2 - 2)
            pe_weighted2(pe, g, par, NW2 - 1)
            pe_out(pe, 1, g, 1)

        def unit_weights(u):
            s, p = divmod(u, 2)
            qh, kt = divmod(s, KT)
            return EX[:, qh, kt, 2 * p:2 * p + 2, :].rearrange("p h q -> p (h q)")

        def act_gated(act, g):
            for u in range(NU2):
                act.wait_ge(A[1, "s_mm"], 2 * NU2 * g + u + 1)
                if u % 2 == 0:
                    act.wait_ge(A[1, "pv"], NW2 * g + u // 2 + 1)
                at = (u % 3) * 2 * CH
                act.activation(unit_weights(u), PS[:, at:at + 2 * CH], ACT.Exp, scale=SCORE_SCALE)\
                   .then_inc(A[1, "s_act"], 1)
            for u in range(NU2):
                act.wait_ge(A[1, "s_mm"], 2 * NU2 * g + NU2 + u + 1)
                act.wait_ge(A[1, "mul"], NU2 * g + max(0, u - 1))
                at = ((NU2 + u) % 3) * 2 * CH
                act.activation(G2[u % 2][:, :], PS[:, at:at + 2 * CH], ACT.Sigmoid, scale=SCORE_SCALE,
                               bias=NMU[:, :]).then_inc(A[1, "s_act"], 1)
                if u == 2 * (KT + 1) + 1:
                    act_out(act, 1, g, 0, NW2 * g + NW2 + KT)
            act_out(act, 1, g, 1, NW2 * g + 2 * NW2)

        def dve_gated(dve, own, g):
            for u in range(NU2):
                dve.wait_ge(A[1, "s_act"], 2 * NU2 * g + NU2 + u + 1)
                w = unit_weights(u)
                dve.tensor_tensor(w, w, G2[u % 2][:, :], ALU.mult).then_inc(A[1, "mul"], 1)
                if u == 2 * TURN2 + 1:
                    dve_out(dve, own, 1, g, 0)
            dve_out(dve, own, 1, g, 1)

        FQ1 = arena(16384, 512).bitcast(I32)
        FQ2 = arena(16896, 512).bitcast(I32)
        FW1 = arena(17408, 512)
        FW2 = arena(17920, 512)
        FS2 = arena(18432, 512)
        HID0 = [arena(19456 + 2048 * i, 2048).rearrange("p (m n) -> p m n", n=CH) for i in range(2)]
        HID4 = [arena(23552 + 2048 * i, 2048).rearrange("p (m n) -> p m n", n=CH) for i in range(2)]
        LI = arena(0, 1152).bitcast(I32)
        LF = arena(1152, 1152)
        L2A = arena(2304, 512)
        L2B = arena(2816, 512)
        R2W = arena(3328, E2)
        R2B = arena(3344, E2)
        R3W = arena(3360, E3)
        R3B = arena(3368, E3)
        HEADM = arena(3376, H)
        BLOCKM = arena(3392, D)
        MG = arena(3584, R2 * P)
        MU = arena(6784, R2 * P)
        MD = arena(9984, R2 * P)
        SEL2 = ARENA[:, 13184:14784].bitcast(BF16)
        M3A = arena(14784, E3 * F3)
        M3B = arena(18880, E3 * F3)
        SEL3 = ARENA[:, 22976:23488].bitcast(BF16)
        WORK = 23552

        def work(at, n):
            return arena(WORK + at, n)

        f0_in = sem("f0_in")
        late_in = sem("late_in")
        NLATE = 11

        def sp_late(sp):
            if on(2):
                sp.wait_ge(A[1, "pv"], NW2 * NG + NW2)
            for dst, src in ((LI, l1int), (arena(2304, 1024), l2fc), (arena(3328, 48), r2w),
                             (arena(3376, H + D), r2b), (MG, moe2[0]), (MU, moe2[1]), (MD, moe2[2]),
                             (M3A, moe3a), (M3B, moe3b)):
                sp.dma_start(dst, src).then_inc(late_in, 16)
            sp.dma_start(SEL2[0:51, :], moe2sel.bitcast(BF16)).then_inc(late_in, 16)
            sp.dma_start(SEL3[0:3 * E3, :], r3w.bitcast(BF16)).then_inc(late_in, 16)

        YB = {n: NC * sum(1 for m in range(n) if on(m)) for n in range(9)}

        def ffn_sems(n):
            for nm in ("f_w", "f_mm", "f_act"):
                A[n, nm] = sem(f"S{n}_{nm}")

        ffn_sems(1)
        ffn_sems(4)

        def pe_ffn(pe, n, n_h, w1, w2, hid, bias):
            pe.wait_ge(h_ready, n_h)

            def down(c):
                pe.wait_ge(A[n, "f_act"], 4 * c + 4)
                for i in range(TPC):
                    pe_y(pe, TPC * c + i, [(hid[c % 2][:, m, i * P:i * P + P], w2[:, m * D:m * D + D])
                                           for m in range(4)], bias)
            for c in range(NC):
                for m in range(4):
                    if c:
                        pe.wait_ge(A[n, "f_act"], 4 * (c - 1) + m + 1)
                    pe.matmul(bank(m), w1[:, m * P:m * P + P], chunk(hT, c), start=True, stop=True)\
                      .then_inc(A[n, "f_mm"], 1)
                if c:
                    down(c - 1)
            down(NC - 1)

        def act_ffn(act, n, hid, func, scale, bias):
            for c in range(NC):
                if c >= 2:
                    act.wait_ge(y_ready, YB[n] + c - 1)
                for m in range(4):
                    act.wait_ge(A[n, "f_mm"], 4 * c + m + 1)
                    act.activation(hid[c % 2][:, m, :], bank(m), func, bias=bias(m),
                                   scale=scale(m) if scale else 1.0).then_inc(A[n, "f_act"], 1)

        def dve_add_y(dve, own, factor, src=None, ready=None, n0=0):
            for c in range(NC):
                dve.wait_ge(ready or y_ready, n0 + c + 1)
                ins = dve.scalar_tensor_tensor(out=chunk(XH, c), in0=bank((4 if src is None else src) + c),
                                               scalar=factor, in1=chunk(XH, c), op0=ALU.mult, op1=ALU.add)
            own.link(ins)

        def dve_dequant0(dve):
            dve.wait_ge(f0_in, 48)
            dve.tensor_scalar(FW1, FQ1, 128.0, None, ALU.subtract)
            dve.scalar_tensor_tensor(out=FW2, in0=FQ2, scalar=128.0, in1=FS2, op0=ALU.subtract,
                                     op1=ALU.mult).then_inc(A[1, "f_w"], 1)

        for nm in ("w", "mm", "sg", "mul"):
            A[3, nm] = sem(f"S3_{nm}")
        M3 = 3
        HID3 = [work(1536 * i, 1536).rearrange("p (m n) -> p m n", n=CH) for i in range(2)]
        SG3 = [work(3072 + 512 * i, 512) for i in range(2)]

        def pe_glu(pe, n_h):
            pe.wait_ge(h_ready, n_h)
            pe.wait_ge(A[3, "w"], 1)

            def down(c):
                pe.wait_ge(A[3, "mul"], M3 * c + M3)
                for i in range(TPC):
                    pe_y(pe, TPC * c + i, [(HID3[c % 2][:, m, i * P:i * P + P],
                                            LF[:, 768 + m * D:768 + m * D + D]) for m in range(M3)], None)
            for c in range(NC):
                for m in range(M3):
                    n = M3 * c + m
                    if n >= 2:
                        pe.wait_ge(A[3, "mul"], n - 1)
                    pe.matmul(bank(n % 2), LF[:, m * P:m * P + P], chunk(hT, c), start=True, stop=True)
                    pe.matmul(bank(2 + n % 2), LF[:, 384 + m * P:384 + m * P + P], chunk(hT, c),
                              start=True, stop=True).then_inc(A[3, "mm"], 1)
                if c:
                    down(c - 1)
            down(NC - 1)

        def act_glu(act):
            for n in range(M3 * NC):
                act.wait_ge(A[3, "mm"], n + 1)
                if n >= 2:
                    act.wait_ge(A[3, "mul"], n - 1)
                act.activation(SG3[n % 2], bank(n % 2), ACT.Silu).then_inc(A[3, "sg"], 1)

        def dve_glu(dve):
            for n in range(M3 * NC):
                c, m = divmod(n, M3)
                dve.wait_ge(A[3, "sg"], n + 1)
                if m == 0 and c >= 2:
                    dve.wait_ge(y_ready, YB[3] + c - 1)
                dve.tensor_tensor(HID3[c % 2][:, m, :], SG3[n % 2], bank(2 + n % 2), ALU.mult)\
                   .then_inc(A[3, "mul"], 1)

        NJ = NC + NT // 2
        T1 = [work(512 * i, 512) for i in range(2)]
        T2 = [work(1024 + 512 * i, 512) for i in range(2)]
        QFT = work(2048, TOK)
        KF = work(4096, TOK)
        VF = work(6144, NT * 130).rearrange("p (t e) -> p t e", e=130)
        KVB = [work(8224 + 144 * i, 144) for i in range(2)]
        RD = work(8512, 32)
        for n in (4, 6):
            for nm in ("mm", "exp", "vf", "feat", "kv", "kvb", "l_mm", "o", "aT", "aTs", "pj"):
                A[n, nm] = sem(f"S{n}_{nm}")

        def job_view(j, v=0):
            if j < NC:
                return bank(j)
            return bank(4 + (j - NC) % 4).rearrange("p (t e) -> p t e", t=2)[:, :, v * D:v * D + D]

        def as_job(j, buf):
            return buf if j < NC else buf[:, 0:2 * D].rearrange("p (t e) -> p t e", t=2)

        def pe_linear(pe, n, n_h, q, kv, kvrow, z):
            pe.wait_ge(h_ready, n_h)
            for c in range(NC):
                pe.matmul(bank(c), W[:, q, :], chunk(hT, c), start=True, stop=True).then_inc(A[n, "mm"], 1)
            for t in range(NT):
                i = t // 2
                if t % 2 == 0 and i >= 4:
                    pe.wait_ge(A[n, "feat"], NC + i - 3)
                    pe.wait_ge(A[n, "vf"], i - 3)
                dst = bank(4 + i % 4, t % 2 * 256, t % 2 * 256 + 256)
                ins = pe.matmul(dst, tile(hT, t), W[:, kv:kv + 2, :].rearrange("p a b -> p (a b)"),
                                start=True, stop=kvrow is None)
                if kvrow is not None:
                    ins = pe.matmul(dst, ones1[:, :], RWS[:, kvrow:kvrow + 256], start=False, stop=True)
                if t % 2:
                    ins.then_inc(A[n, "mm"], 1)
            pe.wait_ge(A[n, "feat"], NJ)
            pe.wait_ge(A[n, "vf"], NT // 2)
            for b in range(B):
                for k in range(KT):
                    t = b * KT + k
                    ins = pe.matmul(bank(b, 0, D + z), tile(KF, t), VF[:, t, 0:D + z],
                                    start=k == 0, stop=k == KT - 1)
                ins.then_inc(A[n, "kv"], 1)

        def act_linear(act, n, bias):
            for j in range(NJ):
                act.wait_ge(A[n, "mm"], j + 1)
                if j >= 2:
                    act.wait_ge(A[n, "feat"], j - 1)
                kw = dict(bias=bias) if bias is not None and j < NC else {}
                act.activation(as_job(j, T1[j % 2]), job_view(j), ACT.Exp, **kw)
                act.activation(as_job(j, T2[j % 2]), job_view(j), ACT.Relu, **kw).then_inc(A[n, "exp"], 1)
                if j >= NC:
                    i = j - NC
                    act.activation(VF[:, 2 * i:2 * i + 2, 0:D], job_view(j, 1), ACT.Copy)\
                       .then_inc(A[n, "vf"], 1)

        def dve_linear(dve, n, z):
            if z:
                dve.memset(VF[:, :, D:D + 1], 1.0)
            for j in range(NJ):
                dve.wait_ge(A[n, "exp"], j + 1)
                dst = chunk(QFT, j) if j < NC else \
                    KF[:, (j - NC) * 256:(j - NC) * 256 + 256].rearrange("p (t e) -> p t e", t=2)
                dve.scalar_tensor_tensor(out=dst, in0=as_job(j, T1[j % 2]), scalar=1.0,
                                         in1=as_job(j, T2[j % 2]), op0=ALU.min, op1=ALU.add)\
                   .then_inc(A[n, "feat"], 1)
            for b in range(B):
                dve.wait_ge(A[n, "kv"], b + 1)
                ins = dve.tensor_tensor(KVB[b][:, 0:D], bank(b, 0, D), BLOCKM, ALU.mult)
                if z:
                    ins = dve.tensor_scalar(KVB[b][:, D:D + H], HEADM, bank(b, D, D + 1), None, ALU.mult)
                ins.then_inc(A[n, "kvb"], 1)

        def pe_linear_norm(pe, n, out_w, bias):
            pe.wait_ge(A[n, "kvb"], B)
            for i in range(NT // 2):
                if i >= 2:
                    pe.wait_ge(A[n, "o"], i - 1)
                for k in range(2):
                    t = 2 * i + k
                    ins = pe.matmul(bank(2 + i % 2, k * 256, k * 256 + D + H), tile(QFT, t),
                                    KVB[t // KT], start=True, stop=True)
                ins.then_inc(A[n, "l_mm"], 1)
            for t in range(NT):
                if t % 2 == 0:
                    pe.wait_ge(A[n, "o"], t // 2 + 1)
                ins = pe.transpose(PS[:, 4 * CH + t * D:4 * CH + t * D + D], tile(XN, t), ident[:, :])
                if t % TPC == TPC - 1:
                    ins.then_inc(A[n, "aT"], 1)
            for t in range(NT):
                if t % TPC == 0:
                    pe.wait_ge(A[n, "aTs"], t // TPC + 1)
                pe_y(pe, t, [(tile(hT, t), W[:, out_w, :])], bias, at=0, ready=A[n, "pj"])

        def act_linear_norm(act, n):
            for c in range(NC):
                act.wait_ge(A[n, "aT"], c + 1)
                act.activation(chunk(hT, c), bank(4 + c), ACT.Copy).then_inc(A[n, "aTs"], 1)

        def dve_linear_norm(dve, own, n):
            for i in range(NT // 2):
                dve.wait_ge(A[n, "l_mm"], i + 1)
                v = bank(2 + i % 2).rearrange("p (t e) -> p t e", t=2)
                r = RD.rearrange("p (t h) -> p t h", t=2)
                if i:
                    dve.wait_ge(A[n, "o"], i)
                own.link(dve.tensor_scalar(r, v[:, :, D:D + H], 1e-6, None, ALU.add))
                own.link(dve.reciprocal(r, r))
                dve.tensor_tensor(XN[:, i * 256:i * 256 + 256].rearrange("p (t h d) -> p t h d", t=2, h=H),
                                  v[:, :, 0:D].rearrange("p t (h d) -> p t h d", h=H),
                                  r.unsqueeze(3).broadcast_to([P, 2, H, HD]), ALU.mult)\
                   .then_inc(A[n, "o"], 1)

        def pe_linear_plain(pe, n, out_w, bias):
            pe.wait_ge(A[n, "kvb"], B)
            for c in range(NC):
                if c >= 2:
                    pe.wait_ge(A[n, "aTs"], c - 1)
                pe.matmul(bank(2 + c % 2), KVB[c // QH][:, 0:D], chunk(QFT, c), start=True, stop=True)\
                  .then_inc(A[n, "aT"], 1)
            for t in range(NT):
                if t % TPC == 0:
                    pe.wait_ge(A[n, "aTs"], t // TPC + 1)
                pe_y(pe, t, [(tile(hT, t), W[:, out_w, :])], bias)

        def act_linear_plain(act, n):
            for c in range(NC):
                act.wait_ge(A[n, "aT"], c + 1)
                act.activation(chunk(hT, c), bank(2 + c % 2), ACT.Copy).then_inc(A[n, "aTs"], 1)

        def dve_top_k(dve, own, vals, e, k, sel, best, tmp):
            a, b, c = tmp
            for t in range(NT):
                ins = dve.max(best[:, t, :], vals[:, t, :])
            own.link(ins)
            kth = best[:, :, k - 1:k].broadcast_to([P, NT, e])
            dve.tensor_tensor(sel, vals, kth, ALU.is_gt)
            own.link(dve.tensor_tensor(a, vals, kth, ALU.is_equal))
            own.link(dve.tensor_reduce(out=best[:, :, 7:8] if k < 8 else None, in_=sel, axis=AX.X, op=ALU.add))
            own.link(dve.tensor_scalar(best[:, :, 7:8], best[:, :, 7:8], -1.0, float(k), ALU.mult, ALU.add))
            src, dst, n = a, b, 1
            while n < e:
                dve.tensor_copy(dst[:, :, 0:n], src[:, :, 0:n])
                own.link(dve.tensor_tensor(dst[:, :, n:e], src[:, :, n:e], src[:, :, 0:e - n], ALU.add))
                src, dst = dst, (c if dst is b else b)
                n *= 2
            own.link(dve.tensor_tensor(dst, src, best[:, :, 7:8].broadcast_to([P, NT, e]), ALU.is_le))
            own.link(dve.tensor_tensor(dst, dst, a, ALU.mult))
            own.link(dve.tensor_tensor(sel, sel, dst, ALU.add))

        def dve_bf16_parts(dve, own, src, dst, rest, e):
            own.link(dve.tensor_copy(dst[:, :, 0, 0:e], src))
            own.link(dve.tensor_tensor(rest, src, dst[:, :, 0, 0:e], ALU.subtract))
            own.link(dve.tensor_copy(dst[:, :, 1, 0:e], rest))
            return dve.tensor_tensor(dst[:, :, 2, 0:e], rest, dst[:, :, 1, 0:e], ALU.subtract)

        def grid(at, e):
            return work(at, NT * e).rearrange("p (t e) -> p t e", e=e)

        for n in (5, 7):
            for nm in ("lg", "sc", "sc2", "cw", "cwT", "cwTs"):
                A[n, nm] = sem(f"S{n}_{nm}")

        CWB5 = ARENA[:, WORK + 7168:WORK + 7168 + 408].bitcast(BF16).rearrange("p (t c e) -> p t c e", c=3, e=17)
        CWT = ARENA[:, WORK + 7680:WORK + 8704].bitcast(BF16)
        CWB7 = ARENA[:, WORK + 7168:WORK + 7168 + 192].bitcast(BF16).rearrange("p (t c e) -> p t c e", c=3, e=E3)
        SC5 = grid(5120, E2)

        def pe_logits(pe, n, n_h, w, e):
            pe.wait_ge(h_ready, n_h)
            for t in range(NT):
                ins = pe.matmul(bank(6, t * e, t * e + e), tile(hT, t), w, start=True, stop=True)
            ins.then_inc(A[n, "lg"], 1)

        def pe_turn_weights(pe, n, cwb, rows):
            pe.wait_ge(A[n, "cw"], 1)
            for t in range(NT):
                v = PS[:, 6 * CH:8 * CH].bitcast(BF16)
                ins = pe.transpose(v[0:rows, t * P:t * P + P], cwb[:, t].rearrange("p c e -> p (c e)"),
                                   identb[:, :])
            ins.then_inc(A[n, "cwT"], 1)

        def act_turn_weights(act, n, rows):
            act.wait_ge(A[n, "cwT"], 1)
            for k in range(2):
                ins = act.activation(CWT[0:rows, k * S:k * S + S], bank(6 + k).bitcast(BF16)[0:rows, :], ACT.Copy)
            ins.then_inc(A[n, "cwTs"], 1)

        def dve_route5(dve, own):
            g4 = lambda at: work(at, NT * 4)
            SF, SEL, TMP = grid(5376, E2), grid(5632, E2), grid(5888, E2)
            U1, U2, U3 = grid(6144, E2), grid(6400, E2), grid(6656, E2)
            BEST = work(6912, NT * 8).rearrange("p (t e) -> p t e", e=8)
            GS, GR = work(7040, NT * 4), work(7104, NT * 4)
            dve.wait_ge(A[5, "sc"], 1)
            own.link(dve.tensor_tensor(SF, SC5, R2B.unsqueeze(1).broadcast_to([P, NT, E2]), ALU.add))
            v = SF.rearrange("p t (g j) -> p (t g) j", j=4)
            first = True
            w = U1.rearrange("p t e -> p (t e)")[:, 0:NT * 4]
            for i in range(4):
                for j in range(i + 1, 4):
                    if first:
                        own.link(dve.tensor_tensor(GS, v[:, :, i], v[:, :, j], ALU.add))
                    else:
                        own.link(dve.tensor_tensor(w, v[:, :, i], v[:, :, j], ALU.add))
                        own.link(dve.tensor_tensor(GS, GS, w, ALU.max))
                    first = False
            gs = GS.rearrange("p (t g) -> p t g", g=4)
            gr = GR.rearrange("p (t g) -> p t g", g=4)
            u = w.rearrange("p (t g) -> p t g", g=4)
            own.link(dve.memset(GR, 0.0))
            for g in range(4):
                other = gs[:, :, g:g + 1]
                if g + 1 < 4:
                    dve.tensor_tensor(u[:, :, g + 1:4], other.broadcast_to([P, NT, 3 - g]), gs[:, :, g + 1:4], ALU.is_ge)
                if g:
                    dve.tensor_tensor(u[:, :, 0:g], other.broadcast_to([P, NT, g]), gs[:, :, 0:g], ALU.is_gt)
                own.link(dve.memset(u[:, :, g:g + 1], 0.0))
                own.link(dve.tensor_tensor(gr, gr, u, ALU.add))
            own.link(dve.tensor_scalar(GR, GR, 1.5, None, ALU.is_lt))
            m = TMP.rearrange("p t (g j) -> p (t g) j", j=4)
            own.link(dve.tensor_tensor(m, v, GR.unsqueeze(2).broadcast_to([P, NT * 4, 4]), ALU.mult))
            dve_top_k(dve, own, TMP, E2, 4, SEL, BEST, (U1, U2, U3))
            own.link(dve.tensor_tensor(SEL, SEL, SC5, ALU.mult))
            own.link(dve.tensor_reduce(out=BEST[:, :, 0:1], in_=SEL, axis=AX.X, op=ALU.add))
            own.link(dve.tensor_scalar(BEST[:, :, 0:1], BEST[:, :, 0:1], 1e-20, None, ALU.add))
            own.link(dve.reciprocal(BEST[:, :, 1:2], BEST[:, :, 0:1]))
            own.link(dve.tensor_tensor(SEL, SEL, BEST[:, :, 1:2].broadcast_to([P, NT, E2]), ALU.mult))
            own.link(dve.memset(CWB5[:, :, 0, 16:17], 1.0))
            own.link(dve.memset(CWB5[:, :, 1:3, 16:17], 0.0))
            dve_bf16_parts(dve, own, SEL, CWB5, U1, E2).then_inc(A[5, "cw"], 1)

        for nm in ("gm", "um", "sg", "t", "h", "dm", "ot"):
            A[5, nm] = sem(f"S5_{nm}")
        SG5 = [work(512 * i, 512) for i in range(2)]
        TM5 = [work(1024 + 512 * i, 512) for i in range(2)]
        HD5 = [work(2048 + 512 * i, 512) for i in range(2)]
        OT5 = work(3072, TOK)

        def before(c, r, n):
            return n * c + (r - 1 if r >= 2 else 0)

        def pe_moe5(pe):
            pe.wait_ge(A[5, "cwTs"], 1)

            def down(c, r):
                pe.wait_ge(A[5, "h"], R2 * c + r + 1)
                if r == 0:
                    pe.wait_ge(A[5, "ot"], c)
                pe.matmul(bank(6), MD[:, r * D:r * D + D], HD5[r % 2], start=r == 0, stop=r == R2 - 1)\
                  .then_inc(A[5, "dm"], 1)
            with pe.Fori(0, NC) as c:
                for r in range(R2):
                    pe.wait_ge(A[5, "h"], before(c, r, R2))
                    pe.matmul(bank(r % 2), MG[:, r * P:r * P + P], chunk(hT, c), start=True, stop=True)\
                      .then_inc(A[5, "gm"], 1)
                    pe.matmul(bank(4 + r % 2), SEL2[0:51, r * P:r * P + P], chunk(CWT[0:51, :], c),
                              start=True, stop=True)
                    pe.matmul(bank(2 + r % 2), MU[:, r * P:r * P + P], chunk(hT, c), start=True, stop=True)\
                      .then_inc(A[5, "um"], 1)
                    if r:
                        down(c, r - 1)
                down(c, R2 - 1)
            pe.wait_ge(A[5, "ot"], NC)
            pe_turn_y(pe, OT5)

        def pe_turn_y(pe, src):
            for t in range(NT):
                ins = pe.transpose(PS[:, 4 * CH + t * D:4 * CH + t * D + D], tile(src, t), ident[:, :])
                if t % TPC == TPC - 1:
                    ins.then_inc(y_ready, 1)

        def act_moe5(act):
            with act.Fori(0, NC) as c:
                for r in range(R2):
                    act.wait_ge(A[5, "gm"], R2 * c + r + 1)
                    act.wait_ge(A[5, "t"], before(c, r, R2))
                    act.activation(SG5[r % 2], bank(r % 2), ACT.Silu).then_inc(A[5, "sg"], 1)
                act.wait_ge(A[5, "dm"], R2 * c + R2)
                act.activation(chunk(OT5, c), bank(6), ACT.Copy).then_inc(A[5, "ot"], 1)

        def dve_moe5(dve):
            with dve.Fori(0, NC) as c:
                for r in range(R2):
                    dve.wait_ge(A[5, "sg"], R2 * c + r + 1)
                    dve.wait_ge(A[5, "um"], R2 * c + r + 1)
                    dve.wait_ge(A[5, "h"], before(c, r, R2))
                    dve.tensor_tensor(TM5[r % 2], SG5[r % 2], bank(4 + r % 2), ALU.mult)\
                       .then_inc(A[5, "t"], 1)
                    dve.wait_ge(A[5, "t"], R2 * c + r + 1)
                    dve.wait_ge(A[5, "dm"], before(c, r, R2))
                    dve.tensor_tensor(HD5[r % 2], TM5[r % 2], bank(2 + r % 2), ALU.mult)\
                       .then_inc(A[5, "h"], 1)

        for nm in ("hm", "ge", "w2", "wr", "ye", "ca", "cb", "cc", "acc"):
            A[7, nm] = sem(f"S7_{nm}")
        HG7 = [work(512 * i, 512) for i in range(4)]
        YE7 = [work(2048 + 512 * i, 512) for i in range(2)]
        CA7 = work(3072, 512)
        CB7 = work(3584, 512)
        CC7 = work(4096, 512)
        ACC7 = work(4608, TOK)
        R7 = 6656
        M7 = E3 * 4

        def dve_route7(dve, own):
            SC, SEL = grid(3072, E3), grid(3200, E3)
            U1, U2, U3 = grid(3328, E3), grid(3456, E3), grid(3584, E3)
            BEST = grid(3712, E3)
            MXS = grid(3840, 2)
            lg = bank(6, 0, NT * E3).rearrange("p (t e) -> p t e", e=E3)
            dve.wait_ge(A[7, "lg"], 1)
            own.link(dve.tensor_tensor(SC, lg, R3B.unsqueeze(1).broadcast_to([P, NT, E3]), ALU.add))
            own.link(dve.tensor_reduce(out=MXS[:, :, 0:1], in_=SC, axis=AX.X, op=ALU.max))
            dve.tensor_tensor(SC, SC, MXS[:, :, 0:1].broadcast_to([P, NT, E3]), ALU.subtract)\
               .then_inc(A[7, "sc"], 1)
            dve.wait_ge(A[7, "sc2"], 1)
            own.link(dve.tensor_reduce(out=MXS[:, :, 0:1], in_=SC, axis=AX.X, op=ALU.add))
            own.link(dve.reciprocal(MXS[:, :, 1:2], MXS[:, :, 0:1]))
            own.link(dve.tensor_tensor(SC, SC, MXS[:, :, 1:2].broadcast_to([P, NT, E3]), ALU.mult))
            dve_top_k(dve, own, SC, E3, 2, SEL, BEST, (U1, U2, U3))
            dve.tensor_tensor(SC, SC, BEST[:, :, 0:1].broadcast_to([P, NT, E3]), ALU.subtract)\
               .then_inc(A[7, "sc"], 1)
            dve.wait_ge(A[7, "sc2"], 2)
            own.link(dve.tensor_tensor(SEL, SEL, SC, ALU.mult))
            own.link(dve.tensor_reduce(out=MXS[:, :, 0:1], in_=SEL, axis=AX.X, op=ALU.add))
            own.link(dve.reciprocal(MXS[:, :, 1:2], MXS[:, :, 0:1]))
            own.link(dve.tensor_tensor(SEL, SEL, MXS[:, :, 1:2].broadcast_to([P, NT, E3]), ALU.mult))
            dve_bf16_parts(dve, own, SEL, CWB7, U1, E3).then_inc(A[7, "cw"], 1)

        def act_route7(act):
            for i in range(2):
                act.wait_ge(A[7, "sc"], i + 1)
                act.activation(work(3072, NT * E3), work(3072, NT * E3), ACT.Exp).then_inc(A[7, "sc2"], 1)

        def pe_moe7(pe):
            pe.wait_ge(A[7, "cwTs"], 1)

            def second(c, m):
                e, k = divmod(m, 4)
                pe.wait_ge(A[7, "ge"], M7 * c + m + 1)
                if k == 0:
                    pe.wait_ge(A[7, "ye"], before(c, e, E3))
                pe.matmul(bank(4 + e % 2), M3B[:, m * D:m * D + D], HG7[m % 4], start=k == 0, stop=k == 3)\
                  .then_inc(A[7, "w2"], 1)
            with pe.Fori(0, NC) as c:
                for m in range(M7):
                    e, k = divmod(m, 4)
                    if k == 0:
                        pe.wait_ge(A[7, "cc"], before(c, e, E3))
                    pe.wait_ge(A[7, "ge"], M7 * c + (m - 3 if m >= 4 else 0))
                    pe.matmul(bank(m % 4), M3A[:, m * P:m * P + P], chunk(hT, c), start=True, stop=True)\
                      .then_inc(A[7, "hm"], 1)
                    if k == 0:
                        pe.matmul(bank(6 + e % 2), SEL3[0:3 * E3, e * P:e * P + P],
                                  chunk(CWT[0:3 * E3, :], c), start=True, stop=True).then_inc(A[7, "wr"], 1)
                    if m:
                        second(c, m - 1)
                second(c, M7 - 1)
            pe.wait_ge(A[7, "acc"], E3 * NC)
            pe_turn_y(pe, ACC7)

        def act_moe7(act):
            def out(c, e):
                act.wait_ge(A[7, "w2"], M7 * c + 4 * e + 4)
                act.wait_ge(A[7, "cb"], before(c, e, E3))
                act.activation(YE7[e % 2], bank(4 + e % 2), ACT.Identity, bias=col("eb2", e))\
                   .then_inc(A[7, "ye"], 1)
            with act.Fori(0, NC) as c:
                for m in range(M7):
                    e, k = divmod(m, 4)
                    act.wait_ge(A[7, "hm"], M7 * c + m + 1)
                    act.wait_ge(A[7, "w2"], M7 * c + (m - 3 if m >= 4 else 0))
                    act.activation(HG7[m % 4], bank(m % 4), ACT.Gelu, bias=col("eb1", m))\
                       .then_inc(A[7, "ge"], 1)
                    if k == 1 and e:
                        out(c, e - 1)
                out(c, E3 - 1)

        def dve_moe7(dve):
            with dve.Fori(0, NC) as c:
                for e in range(E3):
                    n = E3 * c + e
                    dve.wait_ge(A[7, "ye"], n + 1)
                    dve.wait_ge(A[7, "cb"], n)
                    dve.tensor_scalar(CA7, YE7[e % 2], 0.0, None, ALU.max).then_inc(A[7, "ca"], 1)
                    dve.wait_ge(A[7, "ca"], n + 1)
                    dve.wait_ge(A[7, "cc"], n)
                    dve.scalar_tensor_tensor(out=CB7, in0=YE7[e % 2], scalar=0.0, in1=CA7,
                                             op0=ALU.min, op1=ALU.add).then_inc(A[7, "cb"], 1)
                    dve.wait_ge(A[7, "cb"], n + 1)
                    dve.wait_ge(A[7, "wr"], n + 1)
                    dve.wait_ge(A[7, "acc"], n)
                    if e == 0:
                        dve.tensor_tensor(chunk(ACC7, c), CB7, bank(6 + e % 2), ALU.mult)\
                           .then_inc(A[7, "cc"], 1)
                        dve.wait_ge(A[7, "cc"], n + 1)
                        dve.tensor_scalar(SMALL[:, 0:1], MV[:, 0, 0:1], 0.0, None, ALU.mult)\
                           .then_inc(A[7, "acc"], 1)
                    else:
                        dve.tensor_tensor(CC7, CB7, bank(6 + e % 2), ALU.mult).then_inc(A[7, "cc"], 1)
                        dve.wait_ge(A[7, "cc"], n + 1)
                        dve.tensor_tensor(chunk(ACC7, c), chunk(ACC7, c), CC7, ALU.add)\
                           .then_inc(A[7, "acc"], 1)

        NBASE = 3
        block = ctx.enter_context(nc.Block())

        @block.sync
        def _(sp):
            xv = x.rearrange("b (k p) d -> p (b k) d", p=P)
            Xv = X[:, :].rearrange("p (t d) -> p t d", d=D)
            sp.dma_start(Xv, xv).then_inc(x_in, 16)
            sp.dma_start(W[:, :, :], w).then_inc(w_in, 16)
            sp.dma_start(C[:, :], cols).then_inc(c_in, 16)
            sp.dma_start(RWS[:, :], rows).then_inc(c_in, 16)
            sp.dma_start(maskA[:, :], consts[0].bitcast(BF16)).then_inc(c_in, 16)
            sp.dma_start(maskB[:, :], consts[1].bitcast(BF16)).then_inc(c_in, 16)
            if on(0):
                sp.dma_start(COS, rope[0]).then_inc(rope_in, 16)
                sp.dma_start(SIN, rope[1]).then_inc(rope_in, 16)
            if on(1):
                for dst, src in ((FQ1, fc1q), (FQ2, fc2q), (FS2, s2row)):
                    sp.dma_start(dst, src).then_inc(f0_in, 16)
            if on(0):
                sp.wait_ge(v_own, 1)
                sp_stack(sp, 0)
                sp_load_group(sp, 0, 0, 0)
                sp_load_group(sp, 0, 1, 1) if False else None
                sp_max_rows(sp, 0, 0)
                over_groups(sp, lambda g, par, i, more: sp_causal(sp, g, par) if more else None)
            if on(2):
                sp_stack(sp, 1)
                sp_load_group(sp, 1, 0, 0)

                def load_next(g, par, i, more):
                    if more:
                        sp.wait_ge(A[1, "pv"], NW2 * g + NW2)
                        sp_load_group(sp, 1, g + 1, 1 - par)
                over_groups(sp, load_next)
            if any(on(n) for n in range(3, 8)):
                sp_late(sp)
            sp.wait_ge(x_done, 1)
            sp.dma_start(out.rearrange("b (k p) d -> p (b k) d", p=P), Xv).then_inc(out_done, 16)
            sp.wait_ge(out_done, 16)

        @block.gpsimd
        def _(pool):
            pool.memset(ident[:, :], 0.0).then_inc(p_own, 1)
            pool.memset(identb[:, :], 0.0).then_inc(p_own, 1)
            pool.memset(ones1[:, :], 1.0).then_inc(cbase, 1)
            pool.wait_ge(p_own, 2)
            for m in (ident, identb):
                pool.affine_select(out=m[:, :], in_=m[:, :], compare_op=ALU.not_equal, fill=1.0,
                                   base=0, pattern=[[-1, P]], channel_multiplier=1).then_inc(cbase, 1)
            for par in range(2):
                pool.memset(Vg[par][:, :, :, HD:VC], 0.0).then_inc(p_own, 1)
                pool.wait_ge(p_own, 3 + par)
                ins = pool.memset(Vg[par][:, :, :, HD:HD + 1], 1.0)
            ins.then_inc(p_own, 1)
            for L in (0, 1):
                if not on(2 * L):
                    continue
                pool_split(pool, L)
                pool.wait_ge(A[L, "vall"], NC)
                pool_group_values(pool, L, 0, 0)

                def values_next(g, par, i, more, L=L):
                    if more:
                        n = NSTEP * g + PV0 if L == 0 else NW2 * g + NW2
                        pool.wait_ge(A[L, "pv"], n)
                        pool_group_values(pool, L, g + 1, 1 - par)
                over_groups(pool, values_next)

        @block.tensor
        def _(pe):
            pe.wait_ge(cbase, NBASE)
            pe.wait_ge(w_in, 16)
            pe.wait_ge(c_in, 64)
            pe.wait_ge(v_own, 1)
            n_h = 0
            if on(0):
                pe_turn(pe)
                n_h += NC
                pe_values(pe, 0, n_h, None)
                pe_project(pe, 0, ("q0", "qs0", "k0", "ks0"))
                pe.wait_ge(A[0, "qf"], 2 * NC)
                pe.wait_ge(A[0, "ld0"], LD)
                for u in range(NU):
                    pe_max_unit(pe, 0, 0, u)
                pe_max_turn(pe, 0, 0, None)
                pe.wait_ge(A[0, "mt"], 1)
                over_groups(pe, lambda g, par, i, more: pe_causal(pe, g, par, i, more))
                pe_attention_end(pe, 0, "o0", None)
            if on(1):
                pe_turn(pe)
                n_h += NC
                pe.wait_ge(A[1, "f_w"], 1)
                pe_ffn(pe, 1, n_h, FW1, FW2, HID0, RW["fc2b"])
            if on(2):
                pe_turn(pe)
                n_h += NC
                pe_values(pe, 1, n_h, RW["bv1"])
                pe_project(pe, 1, ("q1", "k1"))
                pe.wait_ge(A[1, "qf"], 2 * NC)
                over_groups(pe, lambda g, par, i, more: pe_gated(pe, g, par, i))
                pe_attention_end(pe, 1, "o1", RW["bo1"])
            if any(on(n) for n in range(3, 8)):
                pe.wait_ge(late_in, 16 * NLATE)
            if on(3):
                pe_turn(pe)
                n_h += NC
                pe_glu(pe, n_h)
            if on(4):
                pe_turn(pe)
                n_h += NC
                pe_linear(pe, 4, n_h, WM["q2"], WM["kv2"], None, 1)
                pe_linear_norm(pe, 4, WM["p2"], RW["pb2"])
                pe_turn(pe)
                n_h += NC
                pe_ffn(pe, 4, n_h, L2A, L2B, HID4, RW["fc2b2"])
            if on(5):
                pe_turn(pe)
                n_h += NC
                pe_logits(pe, 5, n_h, R2W, E2)
                pe.wait_ge(A[5, "sc"], 1)
                pe_turn_weights(pe, 5, CWB5, 51)
                pe_moe5(pe)
            if on(6):
                pe_turn(pe)
                n_h += NC
                pe_linear(pe, 6, n_h, WM["q3"], WM["kv3"], RW["bkv3"], 0)
                pe_linear_plain(pe, 6, WM["o3"], RW["bo3"])
            if on(7):
                pe_turn(pe)
                n_h += NC
                pe_logits(pe, 7, n_h, R3W, E3)
                pe_turn_weights(pe, 7, CWB7, 3 * E3)
                pe_moe7(pe)

        @block.scalar
        def _(act):
            act.wait_ge(c_in, 64)
            if on(0):
                act_sqrt(act, EPSC[:, 0:1])
                act_turned(act)
                act_values(act, 0)
                act_split(act, 0)
                act_max_rows(act, 0)
                over_groups(act, lambda g, par, i, more: act_causal(act, g, more))
                act_attention_end(act, 0)
                act_sqrt(act, EPSC[:, 0:1])
            if on(1):
                act_sqrt(act, EPSC[:, 0:1])
                act_sqrt(act, EPSC[:, 0:1])
                act_turned(act, scale=col("g0"), bias=col("b0"))
                act_ffn(act, 1, HID0, ACT.Silu, lambda m: col("s1", m), lambda m: col("fb1", m))
                act_sqrt(act, EPSC[:, 0:1])
            if on(2):
                act_sqrt(act, EPSC[:, 0:1])
                act_sqrt(act, EPSC[:, 1:2])
                act_turned(act, scale=col("g1"), bias=col("bb1"))
                act_values(act, 1)
                act_bias_split(act, 1)
                over_groups(act, lambda g, par, i, more: act_gated(act, g))
                act_attention_end(act, 1)
                act_sqrt(act, EPSC[:, 0:1])
            if on(3):
                act_sqrt(act, EPSC[:, 0:1])
                act_turned(act)
                act_glu(act)
                act_sqrt(act, EPSC[:, 0:1])
            if on(4):
                act_sqrt(act, EPSC[:, 0:1])
                act_sqrt(act, EPSC[:, 0:1])
                act_turned(act, scale=col("g2a"), bias=col("b2a"))
                act_linear(act, 4, None)
                act_linear_norm(act, 4)
                act_sqrt(act, EPSC[:, 0:1])
                act_turned(act, scale=col("g2b"), bias=col("b2b"))
                act_ffn(act, 4, HID4, ACT.Gelu, None, lambda m: col("fb2", m))
                act_sqrt(act, EPSC[:, 0:1])
            if on(5):
                act_sqrt(act, EPSC[:, 0:1])
                act_turned(act)
                act.wait_ge(A[5, "lg"], 1)
                act.activation(SC5.rearrange("p t e -> p (t e)"), bank(6, 0, NT * E2), ACT.Sigmoid)\
                   .then_inc(A[5, "sc"], 1)
                act_turn_weights(act, 5, 51)
                act_moe5(act)
                act_sqrt(act, EPSC[:, 0:1])
            if on(6):
                act_sqrt(act, EPSC[:, 0:1])
                act_turned(act)
                act_linear(act, 6, col("bq3"))
                act_linear_plain(act, 6)
                act_sqrt(act, EPSC[:, 0:1])
            if on(7):
                act_sqrt(act, EPSC[:, 0:1])
                act_turned(act)
                act_route7(act)
                act_turn_weights(act, 7, 3 * E3)
                act_moe7(act)
                act_sqrt(act, EPSC[:, 0:1])

        @block.vector
        def _(dve):
            own = Own(dve, v_own)
            dve.memset(EPSC[:, 0:1], EPS).then_inc(A[0, "pv"], PV0)
            dve.memset(EPSC[:, 1:2], 1e-6).then_inc(A[0, "b_exp"], EXP0)
            for par in range(2):
                for hh in range(2):
                    dve.memset(KS[par][64 * hh + 32:64 * hh + 64, :, :], 1.0)
                    dve.memset(QS[par][64 * hh + 32:64 * hh + 64, :, :], 0.0)
            own.link(dve.memset(bank(6), 0.0))
            dve.wait_ge(c_in, 64)
            own.link(dve.tensor_scalar(NMU[:, :], col("mu"), -1.0, None, ALU.mult))
            dve.wait_ge(x_in, 16)
            if on(0):
                dve_ln_in(dve, own)
                dve.wait_ge(rope_in, 32)
                dve_rope(dve, 0)
                for u in range(NU):
                    dve_max_unit(dve, 0, 0, u)
                dve_max_parts(dve, 0, 0)
                over_groups(dve, lambda g, par, i, more: dve_causal(dve, own, g, par, more))
                dve_ln_out(dve, own, lambda t: tile(Yp, t))
            if on(1):
                dve_dequant0(dve)
                dve_ln_in(dve, own, second=True, keep=True)
                dve_add_y(dve, own, 0.5, n0=YB[1])
                dve_ln_out(dve, own, lambda t: tile(XH, t), waits=False)
            if on(2):
                dve_ln_in(dve, own, second=True)
                for n in range(NW2):
                    ins = None
                dve.memset(R4[:, :, :], 0.0).then_inc(A[1, "pv"], NW2)
                over_groups(dve, lambda g, par, i, more: dve_gated(dve, own, g))
                dve_ln_out(dve, own, lambda t: tile(Yp, t))
            if any(on(n) for n in range(3, 8)):
                dve.wait_ge(late_in, 16 * NLATE)
            if on(3):
                dve.tensor_scalar(LF, LI, 1.0 / 127.0, None, ALU.mult).then_inc(A[3, "w"], 1)
                dve_ln_in(dve, own)
                dve_glu(dve)
                dve_ln_out(dve, own, lambda t: tile(Yp, t))
            if on(4):
                dve_ln_in(dve, own, second=True, keep=True)
                dve_linear(dve, 4, 1)
                dve_linear_norm(dve, own, 4)
                dve_add_y(dve, own, 1.0, src=0, ready=A[4, "pj"])
                dve_stats(dve, own, lambda t: tile(XH, t))
                dve_rsqrt(dve, own, RS[:, :], MV[:, :, 1])
                dve_apply(dve, own, XN, XH, RS)
                dve_add_y(dve, own, 1.0, n0=YB[4])
                dve_ln_out(dve, own, lambda t: tile(XH, t), waits=False)
            if on(5):
                dve_ln_in(dve, own)
                dve_route5(dve, own)
                dve_moe5(dve)
                dve_ln_out(dve, own, lambda t: tile(Yp, t))
            if on(6):
                dve_ln_in(dve, own)
                dve_linear(dve, 6, 0)
                dve_ln_out(dve, own, lambda t: tile(Yp, t))
            if on(7):
                dve_ln_in(dve, own)
                dve_route7(dve, own)
                dve_moe7(dve)
                dve_ln_out(dve, own, lambda t: tile(Yp, t))
            dve.tensor_copy(SMALL[:, 0:1], RS[:, 0:1]).then_inc(x_done, 1)


_OUTS = [((B, S, D), "float32")]


def layout(inputs):
    import numpy as np
    f = {k: np.ascontiguousarray(v) for k, v in inputs.items()}
    swap = np.arange(D) ^ 1
    T = lambda a: a.T
    w = [T(f["L0_attn_W_q"]), T(f["L0_attn_W_q"][swap]), T(f["L0_attn_W_k"]), T(f["L0_attn_W_k"][swap]),
         T(f["L0_attn_W_v"]), T(f["L0_attn_W_o"]),
         T(f["L1_attn_Wq"]), T(f["L1_attn_Wk"]), T(f["L1_attn_Wv"]), T(f["L1_attn_Wo"]),
         T(f["L2_attn_qkv_w"][0:128]), T(f["L2_attn_qkv_w"][128:256]), T(f["L2_attn_qkv_w"][256:384]),
         T(f["L2_attn_proj_w"]),
         T(f["L3_attn_Wq"]), T(f["L3_attn_Wk"]), T(f["L3_attn_Wv"]), T(f["L3_attn_Wo"])]
    w = np.stack(w, 1)
    by = lambda a, n: a.reshape(n, P).T
    cols = [f["L0_ffn_ln_gamma"][:, None], f["L0_ffn_ln_beta"][:, None], by(f["L0_ffn_fc1_scales"][0], 4),
            by(f["L0_ffn_fc1_bias"], 4), f["L1_attn_ln_gamma"][:, None], f["L1_attn_ln_beta"][:, None],
            f["L1_attn_bq"][:, None], f["L1_attn_bk"][:, None],
            np.broadcast_to(f["L1_attn_mu"].reshape(1, 1), (P, 1)),
            f["L2_attn_norm1_g"][:, None], f["L2_attn_norm1_b"][:, None],
            f["L2_attn_norm2_g"][:, None], f["L2_attn_norm2_b"][:, None], by(f["L2_attn_fc1_b"], 4),
            f["L3_attn_bq"][:, None], f["L3_attn_bk"][:, None],
            by(f["L3_ffn_b1"].reshape(-1), 32), f["L3_ffn_b2"].T]
    cols = np.concatenate(cols, 1)
    assert cols.shape == (P, NCOLS), cols.shape
    rows = np.concatenate([f["L0_ffn_fc2_bias"], f["L1_attn_bv"], f["L1_attn_bo"], f["L2_attn_proj_b"],
                           f["L2_attn_fc2_b"], f["L3_attn_bk"], f["L3_attn_bv"], f["L3_attn_bo"]])[None]
    assert rows.shape == (1, NROWS)
    inv = np.float32(10000.0) ** (np.float32(-2.0) * np.arange(HD // 2, dtype=np.float32) / np.float32(HD))
    ang = np.arange(S, dtype=np.float32)[:, None] * inv[None, :]
    d = np.arange(D) % HD
    cos = np.cos(ang).astype(np.float32).T[d // 2]
    sin = np.sin(ang).astype(np.float32).T[d // 2] * np.where(d % 2 == 0, -1.0, 1.0)[:, None].astype(np.float32)
    rope = np.stack([cos, sin]).astype(np.float32)
    k, q = np.meshgrid(np.arange(P), np.arange(P))
    mA = np.where(k > q, BF16_BIG, 0).astype(np.uint16)
    consts = np.stack([mA, mA.T])
    tiles = lambda a: a.reshape(-1, P, a.shape[-1]).transpose(1, 0, 2).reshape(P, -1)
    fc1q = f["L0_ffn_fc1_q"]
    fc2q = tiles(f["L0_ffn_fc2_q"])
    s2row = np.broadcast_to(f["L0_ffn_fc2_scales"].reshape(1, -1), (P, F3))
    l1int = np.concatenate([T(f["L1_ffn_w_gate"]), T(f["L1_ffn_w_up"]), tiles(T(f["L1_ffn_w_down"]))], 1)
    l2fc = np.concatenate([T(f["L2_attn_fc1_w"]), tiles(T(f["L2_attn_fc2_w"]))], 1)
    r2w = np.concatenate([T(f["L2_ffn_gate_w"]), np.broadcast_to(f["L2_ffn_gate_bias"][None], (P, E2)),
                          f["L3_ffn_Wr"], np.broadcast_to(f["L3_ffn_br"][None], (P, E3))], 1)
    head = np.arange(D) // HD
    headm = (head[:, None] == np.arange(H)[None]).astype(np.float32)
    r2b = np.concatenate([headm, (head[:, None] == head[None]).astype(np.float32)], 1)
    pad = np.zeros((R2 * P - HID2 - I2 * NS2, D), np.float32)
    rows_of = lambda a, b: np.concatenate([a.reshape(HID2, D), b, pad], 0)
    down = rows_of(f["L2_ffn_down_proj"].transpose(0, 2, 1), T(f["L2_ffn_shared_down_w"]))
    moe2 = np.stack([T(rows_of(f["L2_ffn_gate_proj"], f["L2_ffn_shared_gate_w"])),
                     T(rows_of(f["L2_ffn_up_proj"], f["L2_ffn_shared_up_w"])), tiles(down)])
    row = np.arange(R2 * P)
    owner = np.where(row < HID2, row // I2, np.where(row < HID2 + I2 * NS2, E2, -1))
    sel = np.where(np.arange(E2 + 1)[:, None] == owner[None], BF16_ONE, 0).astype(np.uint16)
    moe2sel = np.concatenate([sel] * 3, 0)
    sel3 = np.where(np.arange(E3)[:, None] == (np.arange(E3 * P) // P)[None], BF16_ONE, 0).astype(np.uint16)
    r3w = np.concatenate([sel3] * 3, 0)
    moe3a = f["L3_ffn_W1"].transpose(1, 0, 2).reshape(P, -1)
    moe3b = tiles(f["L3_ffn_W2"].reshape(E3 * F3, D))
    return dict(x=f["L0_attn_x"], w=w, cols=cols, rows=rows, rope=rope, consts=consts, fc1q=fc1q,
                fc2q=fc2q, s2row=s2row, l1int=l1int, l2fc=l2fc, r2w=r2w, r2b=r2b, moe2=moe2,
                moe2sel=moe2sel, r3w=r3w, moe3a=moe3a, moe3b=moe3b)


ORDER = ["x", "w", "cols", "rows", "rope", "fc1q", "fc2q", "s2row", "l1int", "l2fc", "r2w", "r2b", "moe2",
         "moe2sel", "r3w", "r3b", "moe3a", "moe3b", "consts"]


def kernel(**inputs):
    import numpy as _np
    import concourse.bacc as _bacc
    from concourse import mybir as _mybir
    from concourse.bass_utils import run_bass_kernel_spmd as _run

    nc = _bacc.Bacc("TRN2", target_bir_lowering=False, num_devices=1)
    arrays, args = {}, []
    laid = layout(inputs)
    for name in ORDER:
        if name not in laid:
            args.append(None)
            continue
        a = _np.ascontiguousarray(laid[name])
        arrays[f"in_{name}"] = a
        args.append(nc.dram_tensor(f"in_{name}", a.shape, _mybir.dt.from_np(a.dtype), kind="ExternalInput").ap())
    for i, (shape, dtype) in enumerate(_OUTS):
        dt = _mybir.dt.from_np(_np.dtype(dtype))
        args.append(nc.dram_tensor(f"out_{i}", shape, dt, kind="ExternalOutput").ap())
    sandwich(nc, *args)
    r = _run(nc, [arrays], core_ids=[0])
    return r.results[0]["out_0"]
```

```python
import concourse.bass as bass
from concourse import mybir
from contextlib import ExitStack

F32 = mybir.dt.float32
BF16 = mybir.dt.bfloat16
F32R = mybir.dt.float32r
I32 = mybir.dt.int32
ALU = mybir.AluOpType
ACT = mybir.ActivationFunctionType
AX = mybir.AxisListType

P = 128
D = 128
B = 2
S = 1024
TOK = B * S
NT = TOK // P
CH = 512
NC = TOK // CH
TPC = CH // P
H = 16
HD = D // H
HG = 4
NG = B * H // HG
KT = S // P
QH = S // CH
VC = 16
TERMS = 6
ROWS = TERMS * HD
SHIFT = 3
Q_PART = (0, 0, 0, 1, 1, 2)
K_PART = (0, 1, 2, 0, 1, 0)
BF16_BIG = 0xF180
BF16_ONE = 0x3F80
SCORE_SCALE = float(HD) ** -0.5
EPS = 1e-5
EPS2 = {1: 1e-5, 2: 1e-6}
E2, I2, NS2 = 16, 176, 2
R2 = 25
HID2 = E2 * I2
NARENA = 32768
PIECES = (0, 3584, 14784, 23552, NARENA, NARENA + TOK)
E3, F3 = 8, 512

COLS = dict(g0=0, b0=1, s1=2, fb1=6, g1=10, bb1=11, bq1=12, bk1=13, mu=14, g2a=15, b2a=16,
            g2b=17, b2b=18, fb2=19, bq3=23, bk3=24, eb1=25, eb2=57)
NCOLS = 65
RW = dict(fc2b=0, bv1=128, bo1=256, pb2=384, fc2b2=512, bkv3=640, bo3=896)
NROWS = 1024
WM = dict(q0=0, qs0=1, k0=2, ks0=3, v0=4, o0=5, q1=6, k1=7, v1=8, o1=9, q2=10, kv2=11, p2=13,
          q3=14, kv3=15, o3=17)
NW = 18


def sandwich(nc, x, w, cols, rows, rope, fc1q, fc2q, s2row, l1int, l2fc, r2w, r2b, moe2, moe2sel,
             r3w, r3b, moe3a, moe3b, consts, out, only=None):
    def on(n):
        return only is None or n == only

    ctx = ExitStack()
    with ctx:
        def sb(name, shape, dt=F32):
            return ctx.enter_context(nc.sbuf_tensor(name, shape, dt))

        def sem(name):
            return ctx.enter_context(nc.semaphore(name))

        X = sb("X", [P, TOK])
        XH = sb("XH", [P, TOK])
        XN = sb("XN", [P, TOK])
        with nc.sbuf_tensor("SHARED", [P, NARENA + TOK], F32) as shared:
            pass
        ROUNDED = [(a, b, sb(f"ROUNDED{a}", [P, b - a], F32R)) for a, b in zip(PIECES, PIECES[1:])]
        ARENA, hT = shared[:, 0:NARENA], shared[:, NARENA:NARENA + TOK]
        QS = [sb(f"QS{i}", [P, 2, S], BF16) for i in range(2)]
        KZ = [sb("KZ0", [P, HG, S], BF16)[:, :, :], hT[:, :].bitcast(BF16).rearrange("p (h n) -> p h n", h=HG)]
        Vg = [sb(f"Vg{i}", [P, KT, HG, VC]) for i in range(2)]
        OS = sb("OS", [P, CH])
        NM = [sb(f"NM{i}", [P, HG * KT]) for i in range(2)]
        NR = sb("NR", [P, HG * KT])
        NB = [sb(f"NB{i}", [P, SHIFT, HG * KT], BF16) for i in range(2)]
        MT = sb("MT", [SHIFT * HG * KT, P], BF16)
        R4 = sb("R4", [P, TPC, HG])
        NMU = sb("NMU", [P, 1])
        W = sb("W", [P, NW, D])
        C = sb("C", [P, NCOLS])
        RWS = sb("RWS", [1, NROWS])
        ident = sb("ident", [P, P])
        identb = sb("identb", [P, P], BF16)
        maskA = sb("maskA", [P, P], BF16)
        maskB = sb("maskB", [P, P], BF16)
        ones1 = sb("ones1", [1, P])
        STY, STX = sb("STY", [P, NT * 6]), sb("STX", [P, NT * 6])
        MVY, MVX = sb("MVY", [P, NT, 2]), sb("MVX", [P, NT, 2])
        SDY, SDX, SDK = sb("SDY", [P, NT]), sb("SDX", [P, NT]), sb("SDK", [P, NT])
        RSY, RSX, RSK = sb("RSY", [P, NT]), sb("RSX", [P, NT]), sb("RSK", [P, NT])
        NBY, NBX = sb("NBY", [P, NT]), sb("NBX", [P, NT])
        ZERO = sb("ZERO", [P, 32])
        EPSC = sb("EPSC", [P, 3])
        PS = ctx.enter_context(nc.psum_tensor("PS", [P, 8 * CH], F32))

        def bank(i, a=0, b=CH):
            return PS[:, i * CH + a:i * CH + b]

        Yp = PS[:, 4 * CH:8 * CH]
        Vall = XH
        AT = XN

        def tile(buf, t):
            if isinstance(t, int):
                return buf[:, t * D:(t + 1) * D]
            return buf[:, bass.ds(t * D, D)]

        def chunk(buf, c):
            if isinstance(c, int):
                return buf[:, c * CH:(c + 1) * CH]
            return buf[:, bass.ds(c * CH, CH)]

        def col(name, n=0):
            return C[:, COLS[name] + n:COLS[name] + n + 1]

        def arena(at, n):
            return ARENA[:, at:at + n]

        def rounded(at, n):
            a, b, piece = [x for x in ROUNDED if x[0] <= at < x[1]][0]
            assert at + n <= b
            return piece[:, at - a:at - a + n]

        hR = rounded(NARENA, TOK)
        PB = [arena(2048 * i, 2048).rearrange("p (h q) -> p h q", h=HG) for i in range(3)]
        COS = arena(6144, S)
        SIN = arena(6144 + S, S)
        PARTS = ARENA[:, 24576:24576 + 6144].bitcast(BF16).rearrange("p (m t n) -> p m t n", m=2, t=3)
        TA = arena(14336, CH)
        TB = arena(14336 + CH, CH)
        QF = [arena(30720, CH), arena(30720 + CH, CH)]

        qx = nc.dram_tensor("qx", (B * H, ROWS + SHIFT, S), BF16, kind="Internal").ap()
        kx = nc.dram_tensor("kx", (B * H, ROWS, S), BF16, kind="Internal").ap()
        mx = nc.dram_tensor("mx", (2, SHIFT * HG * KT, P), BF16, kind="Internal").ap()

        x_in = [sem(f"x_in{c}") for c in range(NC)]
        w_in = sem("w_in")
        c_in = sem("c_in")
        rope_in = sem("rope_in")
        cbase = sem("cbase")
        v_own = sem("v_own")
        a_own = sem("a_own")
        p_own = sem("p_own")
        pads = sem("pads")
        zeros_wr = sem("zeros_wr")
        y_var, y_root, y_scale, y_norm = sem("y_var"), sem("y_root"), sem("y_scale"), sem("y_norm")
        x_var, x_root, x_scale = sem("x_var"), sem("x_root"), sem("x_scale")
        xn_ready = sem("xn_ready")
        xt_ready = sem("xt_ready")
        h_ready = sem("h_ready")
        y_ready = sem("y_ready")
        x_done = sem("x_done")
        out_done = sem("out_done")

        n_edge = [0, 0]

        class Own:

            def __init__(self, eng, s):
                self.eng, self.s, self.n = eng, s, 0

            def mark(self, ins):
                ins.then_inc(self.s, 1)
                self.n += 1

            def wait(self):
                self.eng.wait_ge(self.s, self.n)

            def link(self, ins):
                self.mark(ins)
                self.wait()

        class Edge:

            def __init__(self, y=None, y0=0, y_at=4, add=None, inner=False, turn=True, eps2=None,
                         keep=False, scale=1.0, bias=None, split=False):
                self.y, self.y0, self.y_at, self.add, self.inner = y, y0, y_at, add, inner
                self.turn, self.eps2, self.keep, self.scale, self.bias = turn, eps2, keep, scale, bias
                self.split = split
                self.norm_y = y is not None and not inner
                self.n_y, self.n_x = n_edge
                n_edge[0] += NC * self.norm_y
                n_edge[1] += NC * turn

            def stream(self):
                return XH if self.inner else X

        def dve_stats(dve, own, st, mv, src, c):
            for t in range(c * TPC, c * TPC + TPC):
                ins = dve.bn_stats(st[:, t * 6:t * 6 + 6], src(t))
            own.link(ins)
            for t in range(c * TPC, c * TPC + TPC):
                ins = dve.bn_aggr(mv[:, t, :], st[:, t * 6:t * 6 + 6])
            return ins

        def dve_scales(dve, own, mv, sd, rs, nb, c):
            k = slice(c * TPC, c * TPC + TPC)
            own.link(dve.reciprocal(rs[:, k], sd[:, k]))
            return dve.scalar_tensor_tensor(out=nb[:, k], in0=mv[:, k, 0], scalar=-1.0, in1=rs[:, k],
                                            op0=ALU.mult, op1=ALU.mult)

        def dve_edge(dve, own, e):
            def y_stats(c):
                dve.wait_ge(e.y, e.y0 + c + 1)
                if e.add is not None:
                    own.link(dve.scalar_tensor_tensor(out=chunk(XH, c), in0=bank(e.y_at + c), scalar=e.add,
                                                      in1=chunk(XH, c), op0=ALU.mult, op1=ALU.add))
                src = (lambda t: tile(XH, t)) if e.add is not None else (lambda t: tile(Yp, t))
                dve_stats(dve, own, STY, MVY, src, c).then_inc(y_var, 1)

            def y_scales(c):
                dve.wait_ge(y_root, e.n_y + c + 1)
                dve_scales(dve, own, MVY, SDY, RSY, NBY, c).then_inc(y_scale, 1)

            def x_stats(c):
                if e.norm_y:
                    dve.wait_ge(y_norm, e.n_y + c + 1)
                    own.link(dve.tensor_tensor(chunk(X, c), chunk(X, c), chunk(XN, c), ALU.add))
                elif e.inner:
                    dve.wait_ge(e.y, e.y0 + c + 1)
                    own.link(dve.tensor_tensor(chunk(XH, c), chunk(XH, c), bank(e.y_at + c), ALU.add))
                else:
                    dve.wait_ge(x_in[c], 16)
                if e.turn:
                    dve_stats(dve, own, STX, MVX, lambda t: tile(e.stream(), t), c).then_inc(x_var, 1)

            def x_scales(c):
                dve.wait_ge(x_root, e.n_x + c + 1)
                dve_scales(dve, own, MVX, SDX, RSX, NBX, c).then_inc(x_scale, 1)

            for s in range(NC + 3):
                if e.norm_y and s < NC:
                    y_stats(s)
                if e.norm_y and 0 <= s - 1 < NC:
                    y_scales(s - 1)
                if 0 <= s - 2 < NC:
                    x_stats(s - 2)
                if e.turn and 0 <= s - 3 < NC:
                    x_scales(s - 3)
            if e.keep:
                own.link(dve.reciprocal(RSK[:, :], SDK[:, :]))
                for t in range(NT):
                    ins = dve.tensor_scalar(tile(XH, t), tile(X, t), MVX[:, t, 0:1], RSK[:, t:t + 1],
                                            ALU.subtract, ALU.mult)
                own.link(ins)

        def act_edge(act, e):
            def root(sd, mv, c, bias, scale=1.0):
                k = slice(c * TPC, c * TPC + TPC)
                return act.activation(sd[:, k], mv[:, k, 1], ACT.Sqrt, bias=bias, scale=scale)

            def apply(src, rs, nb, c):
                for t in range(c * TPC, c * TPC + TPC):
                    ins = act.activation(tile(XN, t), tile(src, t), ACT.Identity, scale=rs[:, t:t + 1],
                                         bias=nb[:, t:t + 1])
                return ins

            def y_roots(c):
                act.wait_ge(y_var, e.n_y + c + 1)
                root(SDY, MVY, c, EPSC[:, 0:1]).then_inc(y_root, 1)

            def y_apply(c):
                act.wait_ge(y_scale, e.n_y + c + 1)
                apply(Yp if e.add is None else XH, RSY, NBY, c).then_inc(y_norm, 1)

            def x_roots(c):
                act.wait_ge(x_var, e.n_x + c + 1)
                if e.keep:
                    root(SDK, MVX, c, EPSC[:, 0:1])
                if e.eps2 is None:
                    ins = root(SDX, MVX, c, EPSC[:, 0:1])
                else:
                    ins = root(SDX, MVX, c, EPSC[:, e.eps2:e.eps2 + 1], 1.0 + EPS2[e.eps2])
                ins.then_inc(x_root, 1)

            def x_apply(c):
                act.wait_ge(x_scale, e.n_x + c + 1)
                apply(e.stream(), RSX, NBX, c).then_inc(xn_ready, 1)

            def turned(c):
                act.wait_ge(xt_ready, e.n_x + c + 1)
                if e.split:
                    act.activation(chunk(XH, c), bank(c), ACT.Copy)
                    ins = act.activation(chunk(hR, c), bank(c), ACT.Copy)
                elif e.bias is None:
                    ins = act.activation(chunk(hT, c), bank(c), ACT.Copy)
                else:
                    ins = act.activation(chunk(hT, c), bank(c), ACT.Identity, scale=e.scale, bias=e.bias)
                ins.then_inc(h_ready, 1)

            for s in range(NC + 4):
                if e.norm_y and s < NC:
                    y_roots(s)
                if e.norm_y and 0 <= s - 1 < NC:
                    y_apply(s - 1)
                if e.turn:
                    if 0 <= s - 2 < NC:
                        x_roots(s - 2)
                    if 0 <= s - 3 < NC:
                        x_apply(s - 3)
                    if 0 <= s - 4 < NC:
                        turned(s - 4)

        def pe_edge(pe, e):
            if e.turn:
                for c in range(NC):
                    pe.wait_ge(xn_ready, e.n_x + c + 1)
                    for t in range(c * TPC, c * TPC + TPC):
                        ins = pe.transpose(PS[:, t * D:(t + 1) * D], tile(XN, t), ident[:, :])
                    ins.then_inc(xt_ready, 1)

        A = {}
        BASE = 1

        def sems(L, names):
            for nm in names.split():
                A[L, nm] = sem(f"L{L}_{nm}")

        COMMON = "proj qf rope pads1 part0 res part1 part2 vt vall q_wr ld0 ld1 vg o_sb ot ot_free aT aTs "
        sems(0, COMMON + "a_mm a_red b_mm b_exp pv nm nmt mt m_wr m_ld0 m_ld1")
        sems(1, COMMON + "s_mm s_act mul pv")

        def group_rows(t, g, hh):
            v = t.rearrange("(g p x) r n -> g x r p n", p=2, x=2)
            if isinstance(g, int):
                return v[g, hh]
            return v[bass.ds(g, 1), hh].rearrange("g r p n -> (g r) p n")

        def gcols(buf, g, a, b):
            if isinstance(g, int):
                return buf[:, g * 256 + a:g * 256 + b]
            return buf[:, bass.ds(g * 256 + a, b - a)]

        def group_place(g, qh):
            v = AT[:, :].rearrange("p (b a i g e) -> p b a g i e", b=B, a=QH, i=TPC, g=HG)
            if isinstance(g, int):
                w = v[:, g // HG, qh, g % HG]
            else:
                w = v[:, bass.ds(g // HG, 1), qh, bass.ds(g % HG, 1)].rearrange("p b g i e -> p (b g i) e")
            return w.rearrange("p i (h d) -> p i h d", h=HG)

        def pe_values(pe, L, n_h, vbias):
            pe.wait_ge(h_ready, n_h)
            if vbias is not None:
                pe.wait_ge(cbase, NBASE)
            for t in range(NT):
                dst = PS[:, 4 * CH + t * D:4 * CH + (t + 1) * D]
                ins = pe.matmul(dst, tile(hT, t), W[:, WM[f"v{L}"], :], start=True, stop=vbias is None)
                if vbias is not None:
                    ins = pe.matmul(dst, ones1[:, :], RWS[:, vbias:vbias + D], start=False, stop=True)
                if t % TPC == TPC - 1:
                    ins.then_inc(A[L, "vt"], 1)

        def act_values(act, L):
            dst = Vall[:, :].rearrange("p (b g k e) -> p b g k e", b=B, g=HG, k=KT)
            for c in range(NC):
                act.wait_ge(A[L, "vt"], c + 1)
                k0 = (c % QH) * TPC
                act.activation(dst[:, c // QH, :, k0:k0 + TPC, :],
                               bank(4 + c).rearrange("p (k g e) -> p g k e", k=TPC, g=HG), ACT.Copy)\
                   .then_inc(A[L, "vall"], 1)

        def pool_group_values(pool, L, g, par):
            pool.tensor_copy(Vg[par][:, :, :, 0:HD],
                             gcols(Vall, g, 0, 256).rearrange("p (k h d) -> p k h d", k=KT, h=HG))\
                .then_inc(A[L, "vg"], 1)

        def pe_project(pe, L, mats):
            for c in range(NC):
                if c == 1:
                    pe.wait_ge(A[L, "vall"], NC)
                if c >= 2:
                    pe.wait_ge(A[L, "qf"], 2 * (c - 1))
                for m, name in enumerate(mats):
                    ins = pe.matmul(bank(4 * (c % 2) + m), W[:, WM[name], :], chunk(hT, c),
                                    start=True, stop=True)
                ins.then_inc(A[L, "proj"], 1)

        def dve_rope(dve, L):
            for i in range(2 * NC):
                c, m = divmod(i, 2)
                pos = slice((c % QH) * CH, (c % QH) * CH + CH)
                dve.wait_ge(A[L, "proj"], c + 1)
                if i:
                    dve.wait_ge(A[L, "qf"], i)
                dve.tensor_tensor(TA, bank(4 * (c % 2) + 2 * m), COS[:, pos], ALU.mult)
                dve.tensor_tensor(TB, bank(4 * (c % 2) + 2 * m + 1), SIN[:, pos], ALU.mult)\
                   .then_inc(A[L, "rope"], 1)
                dve.wait_ge(A[L, "rope"], i + 1)
                if i >= 2:
                    dve.wait_ge(A[L, "part2"], i - 1)
                dve.tensor_tensor(QF[m], TA, TB, ALU.add).then_inc(A[L, "qf"], 1)

        def act_split_one(act, L, i):
            c, m = divmod(i, 2)
            dst = PARTS[:, m, :, c * CH:(c + 1) * CH]
            act.wait_ge(A[L, "qf"], i + 1)
            act.activation(dst[:, 0], QF[m], ACT.Copy).then_inc(A[L, "part0"], 1)
            act.wait_ge(A[L, "res"], i + 1)
            act.activation(dst[:, 1], QF[m], ACT.Copy).then_inc(A[L, "part1"], 1)

        def act_split(act, L):
            for i in range(2 * NC):
                act_split_one(act, L, i)

        def act_bias_split(act, L):
            for i in range(2 * NC):
                c, m = divmod(i, 2)
                act.wait_ge(A[L, "proj"], c + 1)
                if i >= 2:
                    act.wait_ge(A[L, "part2"], i - 1)
                act.activation(QF[m], bank(4 * (c % 2) + m), ACT.Identity,
                               bias=col(("bq1", "bk1")[m])).then_inc(A[L, "qf"], 1)
                act_split_one(act, L, i)

        def pool_split(pool, L):
            for i in range(2 * NC):
                c, m = divmod(i, 2)
                dst = PARTS[:, m, :, c * CH:(c + 1) * CH]
                pool.wait_ge(A[L, "part0"], i + 1)
                pool.tensor_tensor(QF[m], QF[m], dst[:, 0], ALU.subtract).then_inc(A[L, "res"], 1)
                pool.wait_ge(A[L, "res"], i + 1)
                pool.wait_ge(A[L, "part1"], i + 1)
                pool.tensor_tensor(dst[:, 2], QF[m], dst[:, 1], ALU.subtract)\
                    .then_inc(A[L, "part2"], 1)

        def sp_stack(sp, L, b):
            sp.wait_ge(A[L, "part2"], 2 * QH * (b + 1))
            for m, (dst, parts) in enumerate(((qx, Q_PART), (kx, K_PART))):
                for t, part in enumerate(parts):
                    sp.dma_start(dst[b * H:(b + 1) * H, t * HD:(t + 1) * HD, :],
                                 PARTS[:, m, part, b * S:(b + 1) * S]).then_inc(A[L, "q_wr"], 16)
            sp.wait_ge(A[L, "q_wr"], 16 * 2 * TERMS * (b + 1))

        def sp_stacks(sp, L):
            sp_stack(sp, L, 0)
            sp_load_group(sp, L, 0, 0)
            sp_stack(sp, L, 1)
            sp.wait_ge(A[L, "pads1"], 4)

        def sp_load_group(sp, L, g, par):
            for hh in range(2):
                keys = KZ[par].rearrange("r (p x) n -> r x p n", x=2)[:, hh]
                for dst, rows, src in ((QS[par], ROWS + SHIFT, qx), (keys, ROWS, kx)):
                    sp.dma_start(dst[64 * hh:64 * hh + rows, :, :], group_rows(src, g, hh))\
                      .then_inc(A[L, f"ld{par}"], 16)
        LD = 64

        def pool_key_pads(pool, keys, ready):
            keys = keys.rearrange("r (p x) n -> r x p n", x=2)
            for hh in range(2):
                other = 64 - 64 * hh
                pool.memset(keys[other:other + 64, hh], 0.0).then_inc(ready, 1)
                pool.wait_ge(ready, 2 * hh + 1)
                pool.memset(keys[64 * hh + 32:64 * hh + 64, hh], 1.0).then_inc(ready, 1)
                pool.wait_ge(ready, 2 * hh + 2)

        def act_out(act, L, g, qh, pv):
            act.wait_ge(A[L, "pv"], pv)
            act.wait_ge(A[L, "ot"], BASE + QH * g + qh)
            act.activation(OS[:, :], bank(6), ACT.Copy).then_inc(A[L, "o_sb"], 1)

        def pe_out(pe, L, g, qh):
            pe.wait_ge(A[L, "o_sb"], BASE + QH * g + qh + 1)
            pe.wait_ge(A[L, "ot_free"], BASE + QH * g + qh)
            for i in range(TPC):
                ins = pe.transpose(bank(7, i * P, i * P + P), OS[:, i * P:i * P + P], ident[:, :])
            ins.then_inc(A[L, "ot"], 1)

        def dve_out(dve, own, L, g, qh):
            dve.wait_ge(A[L, "ot"], BASE + QH * g + qh + 1)
            v = bank(7).rearrange("p (i h e) -> p i h e", i=TPC, h=HG)
            dve.reciprocal(R4[:, :, :], v[:, :, :, HD]).then_inc(A[L, "rope"], 1)
            rope0 = 2 * NC if L == 0 else 0
            dve.wait_ge(A[L, "rope"], rope0 + QH * g + qh + 1)
            dve.tensor_tensor(group_place(g, qh),
                              v[:, :, :, 0:HD], R4[:, :, :].unsqueeze(3).broadcast_to([P, TPC, HG, HD]),
                              ALU.mult).then_inc(A[L, "ot_free"], 1)

        def pe_attention_end(pe, L, out_w, bias):
            pe.wait_ge(A[L, "ot_free"], BASE + QH * NG)
            for t in range(NT):
                ins = pe.transpose(PS[:, t * D:(t + 1) * D], tile(AT, t), ident[:, :])
                if t % TPC == TPC - 1:
                    ins.then_inc(A[L, "aT"], 1)
            for t in range(NT):
                if t % TPC == 0:
                    pe.wait_ge(A[L, "aTs"], t // TPC + 1)
                pe_y(pe, t, [(tile(hT, t), W[:, WM[out_w], :])], bias)

        def pe_y(pe, t, pairs, bias, at=4 * CH, ready=None):
            dst = PS[:, at + t * D:at + (t + 1) * D]
            for n, (a, b) in enumerate(pairs):
                ins = pe.matmul(dst, a, b, start=n == 0, stop=bias is None and n == len(pairs) - 1)
            if bias is not None:
                ins = pe.matmul(dst, ones1[:, :], RWS[:, bias:bias + D], start=False, stop=True)
            if t % TPC == TPC - 1:
                ins.then_inc(ready or y_ready, 1)

        def act_attention_end(act, L):
            for c in range(NC):
                act.wait_ge(A[L, "aT"], c + 1)
                act.activation(chunk(hT, c), bank(c), ACT.Copy).then_inc(A[L, "aTs"], 1)

        STEPS = [(0, kt) for kt in range(TPC)] + [(1, kt) for kt in (0, 4, 5, 6, 7, 1, 2, 3)]
        NSTEP = len(STEPS)
        NU = HG * KT
        EXP0, PV0 = 1, 2
        UNITS = [0, 4, 4, 4, 4, 4, 4, 4, 4, 0, 0, 0]
        UNIT0 = [sum(UNITS[:s]) for s in range(NSTEP + 1)]
        TURN_MAX = 10
        TURN0 = 6

        def operands(par, h):
            return QS[par][:, h // 2, :], KZ[par][:, h, :]

        def pe_max_unit(pe, g, par, u):
            h, qt = divmod(u, KT)
            q, k = operands(par, h)
            at = (u % 2) * 2 * CH
            n = (qt + 1) * P
            if not (isinstance(g, int) and g == 0 and u < 2):
                pe.wait_ge(A[0, "a_red"], NU * g + u - 1)
            for lo in range(0, n, CH):
                hi = min(n, lo + CH)
                diag = lo <= qt * P < hi
                ins = pe.matmul(PS[:, at + lo:at + hi], q[:, qt * P:qt * P + P], k[:, lo:hi],
                                start=True, stop=not diag)
                if diag:
                    ins = pe.matmul(PS[:, at + qt * P:at + qt * P + P], identb[:, :], maskA[:, :],
                                    start=False, stop=True)
            ins.then_inc(A[0, "a_mm"], 1)

        def dve_max_unit(dve, g, par, u):
            h, qt = divmod(u, KT)
            at = (u % 2) * 2 * CH
            dve.wait_ge(A[0, "a_mm"], NU * g + u + 1)
            dve.tensor_reduce(out=NM[par][:, u:u + 1], in_=PS[:, at:at + (qt + 1) * P], axis=AX.X,
                              op=ALU.max, negate=True).then_inc(A[0, "a_red"], 1)

        def dve_max_parts(dve, g, par):
            dve.wait_ge(A[0, "a_red"], NU * g + NU)
            dve.tensor_copy(NB[par][:, 0], NM[par][:, :]).then_inc(A[0, "nm"], 1)
            dve.wait_ge(A[0, "nm"], 4 * g + 1)
            dve.tensor_tensor(NR[:, :], NM[par][:, :], NB[par][:, 0], ALU.subtract).then_inc(A[0, "nm"], 1)
            dve.wait_ge(A[0, "nm"], 4 * g + 2)
            dve.tensor_copy(NB[par][:, 1], NR[:, :]).then_inc(A[0, "nm"], 1)
            dve.wait_ge(A[0, "nm"], 4 * g + 3)
            dve.tensor_tensor(NB[par][:, 2], NR[:, :], NB[par][:, 1], ALU.subtract).then_inc(A[0, "nm"], 1)

        NROW = SHIFT * NU

        def pe_max_turn(pe, g, par, outs):
            pe.wait_ge(A[0, "nm"], 4 * g + 4)
            if outs is not None:
                pe.wait_ge(A[0, "ot_free"], BASE + outs)
            pe.transpose(bank(7).bitcast(BF16)[0:NROW, 0:P], NB[par][:, :, :].rearrange("p t n -> p (t n)"),
                         identb[:, :]).then_inc(A[0, "nmt"], 1)

        def act_max_rows(act, g):
            act.wait_ge(A[0, "nmt"], g + 1)
            act.wait_ge(A[0, "m_wr"], BASE + 16 * g)
            act.activation(MT[:, :], bank(7).bitcast(BF16)[0:NROW, 0:P], ACT.Copy)\
               .then_inc(A[0, "mt"], 1)

        def sp_max_rows(sp, g, par):
            sp.wait_ge(A[0, "mt"], g + 1)
            sp.dma_start(mx[par], MT[:, :]).then_inc(A[0, "m_wr"], 16)
            sp.wait_ge(A[0, "m_wr"], BASE + 16 * g + 16)
            v = mx[par].rearrange("(t p x k) q -> x t p (k q)", t=SHIFT, p=2, x=2)
            for hh in range(2):
                sp.dma_start(QS[par][64 * hh + ROWS:64 * hh + ROWS + SHIFT, :, :], v[hh])\
                  .then_inc(A[0, f"m_ld{par}"], 16)

        def pe_scores(pe, g, par, s, heads):
            qh, kt = STEPS[s]
            q0 = max(0, kt * P - qh * CH)
            for h in heads:
                q, k = operands(par, h)
                pe.wait_ge(A[0, "b_exp"], HG * NSTEP * g + HG * s + h - 1 + EXP0)
                diag = kt // TPC == qh
                ins = pe.matmul(bank(4 + h % 2, q0), k[:, kt * P:kt * P + P],
                                q[:, qh * CH + q0:qh * CH + CH], start=True, stop=not diag)
                if diag:
                    ins = pe.matmul(bank(4 + h % 2, q0, q0 + P), identb[:, :], maskB[:, :],
                                    start=False, stop=True)
                ins.then_inc(A[0, "b_mm"], 1)

        def act_weights(act, g, s):
            qh, kt = STEPS[s]
            q0 = max(0, kt * P - qh * CH)
            act.wait_ge(A[0, "pv"], NSTEP * g + s - 2 + PV0)
            for h in range(HG):
                act.wait_ge(A[0, "b_mm"], BASE + HG * NSTEP * g + HG * s + h + 1)
                act.activation(PB[s % 3][:, h, q0:CH], bank(4 + h % 2, q0), ACT.Exp, scale=SCORE_SCALE)\
                   .then_inc(A[0, "b_exp"], 1)

        def pe_weighted(pe, g, par, s):
            qh, kt = STEPS[s]
            q0 = max(0, kt * P - qh * CH)
            pe.wait_ge(A[0, "b_exp"], HG * (NSTEP * g + s + 1) + EXP0)
            if kt == 0:
                pe.wait_ge(A[0, "o_sb"], BASE + QH * g + qh)
                pe.wait_ge(A[0, "vg"], g + 1)
            last = s + 1 in HALF
            for h in range(HG):
                ins = pe.matmul(PS[32 * h:32 * h + VC, 6 * CH + q0:7 * CH], Vg[par][:, kt, h, :],
                                PB[s % 3][:, h, q0:CH], start=kt == 0, stop=last)
            ins.then_inc(A[0, "pv"], 1)

        HALF = [TPC, NSTEP]

        def pe_causal(pe, g, par, i, more):
            pe.wait_ge(A[0, f"m_ld{par}"], 32 * (i + 1))
            for s in range(NSTEP):
                units = list(range(UNIT0[s], UNIT0[s + 1])) if more else []
                if units and units[0] == 0:
                    pe.wait_ge(A[0, f"ld{1 - par}"], LD * (i + 1 + par))

                def unit():
                    if units:
                        pe_max_unit(pe, g + 1, 1 - par, units.pop(0))
                if more and s == TURN_MAX:
                    pe_max_turn(pe, g + 1, 1 - par, QH * g + 1)
                pe_scores(pe, g, par, s, (0, 1))
                if s == TURN0:
                    pe_out(pe, 0, g, 0)
                unit()
                if s:
                    pe_weighted(pe, g, par, s - 1)
                unit()
                pe_scores(pe, g, par, s, (2, 3))
                while units:
                    unit()
            pe_weighted(pe, g, par, NSTEP - 1)
            if more:
                pe.wait_ge(A[0, "mt"], g + 2)
            pe_out(pe, 0, g, 1)

        def dve_causal(dve, own, g, par, more):
            for s in range(NSTEP):
                if s == TURN0:
                    dve_out(dve, own, 0, g, 0)
                if more:
                    for u in range(UNIT0[s], UNIT0[s + 1]):
                        dve_max_unit(dve, g + 1, 1 - par, u)
            if more:
                dve_max_parts(dve, g + 1, 1 - par)
            dve_out(dve, own, 0, g, 1)

        def act_causal(act, g, more):
            for s in range(NSTEP):
                act_weights(act, g, s)
                if s == TPC:
                    act_out(act, 0, g, 0, NSTEP * g + HALF[0] + PV0)
                if more and s == TURN_MAX - 1:
                    act_max_rows(act, g + 1)
            act_out(act, 0, g, 1, NSTEP * g + HALF[1] + PV0)

        def sp_causal(sp, g, par):
            sp.wait_ge(A[0, "b_mm"], BASE + HG * NSTEP * g)
            sp_load_group(sp, 0, g + 1, 1 - par)
            sp_max_rows(sp, g + 1, 1 - par)

        def pool_causal(pool, g, par):
            pool.wait_ge(A[0, "pv"], NSTEP * g + PV0)
            pool_group_values(pool, 0, g + 1, 1 - par)

        def over_groups(eng, step):
            with eng.Fori(0, NG // 2 - 1) as i:
                step(2 * i, 0, i, True)
                step(2 * i + 1, 1, i, True)
            step(NG - 2, 0, NG // 2 - 1, True)
            step(NG - 1, 1, NG // 2 - 1, False)

        NW2 = QH * KT
        NUP = 2 * KT
        NU2 = 4 * NUP
        RING = 8
        LAG = 3
        PV2, MUL2 = KT, RING
        EX = arena(0, NUP * 2 * CH).rearrange("p (k h q) -> p k h q", k=KT, h=HG)
        GR = [arena(NUP * 2 * CH + 2 * CH * i, 2 * CH) for i in range(RING)]

        def unit_no(qh, second, j):
            return NUP * (2 * qh + second) + j

        def pe_pair(pe, g, par, qh, second, j):
            kt, p = divmod(j, 2)
            v = unit_no(qh, second, j)
            at = (v % 3) * 2 * CH
            pe.wait_ge(A[1, "s_act"], NU2 * g + 1 + (v - 2 if v >= 3 else 0))
            for hh in range(2):
                q, k = operands(par, 2 * p + hh)
                ins = pe.matmul(PS[:, at + hh * CH:at + (hh + 1) * CH], k[:, kt * P:kt * P + P],
                                q[:, qh * CH:(qh + 1) * CH], start=True, stop=True)
            ins.then_inc(A[1, "s_mm"], 1)

        def pe_weighted2(pe, g, par, qh, kt):
            pe.wait_ge(A[1, "mul"], MUL2 + 2 * (NW2 * g + KT * qh + kt) + 2)
            if kt == 0:
                pe.wait_ge(A[1, "o_sb"], BASE + QH * g + qh)
                pe.wait_ge(A[1, "vg"], g + 1)
            for h in range(HG):
                ins = pe.matmul(PS[32 * h:32 * h + VC, 6 * CH:7 * CH], Vg[par][:, kt, h, :],
                                EX[:, kt, h, :], start=kt == 0, stop=kt == KT - 1)
            ins.then_inc(A[1, "pv"], 1)

        def pe_first_pass(pe, g, par, qh, last=None):
            for s in range(KT):
                pe_pair(pe, g, par, qh, 0, 2 * s)
                pe_pair(pe, g, par, qh, 0, 2 * s + 1)
                if last and 1 <= s <= LAG:
                    pe_weighted2(pe, *last, KT - LAG + s - 1)
                if last and s == LAG + 2:
                    pe_out(pe, 1, last[0], last[2])

        def pe_second_pass(pe, g, par, qh):
            for s in range(KT):
                pe_pair(pe, g, par, qh, 1, 2 * s)
                pe_pair(pe, g, par, qh, 1, 2 * s + 1)
                if s >= LAG:
                    pe_weighted2(pe, g, par, qh, s - LAG)

        def pe_gated(pe, g, par, i, more):
            pe_second_pass(pe, g, par, 0)
            pe_first_pass(pe, g, par, 1, (g, par, 0))
            pe_second_pass(pe, g, par, 1)
            if more:
                pe.wait_ge(A[1, f"ld{1 - par}"], LD * (i + 1 + par))
                pe_first_pass(pe, g + 1, 1 - par, 0, (g, par, 1))
            else:
                for kt in range(KT - LAG, KT):
                    pe_weighted2(pe, g, par, 1, kt)
                pe_out(pe, 1, g, 1)

        def unit_weights(j):
            kt, p = divmod(j, 2)
            return EX[:, kt, 2 * p:2 * p + 2, :].rearrange("p h q -> p (h q)")

        def act_factor(act, dst, v, exp):
            src = PS[:, (v % 3) * 2 * CH:(v % 3) * 2 * CH + 2 * CH]
            if exp:
                ins = act.activation(dst, src, ACT.Exp, scale=SCORE_SCALE)
            else:
                ins = act.activation(dst, src, ACT.Sigmoid, scale=SCORE_SCALE, bias=NMU[:, :])
            ins.then_inc(A[1, "s_act"], 1)

        def act_first_pass(act, g, qh, last=None):
            for j in range(NUP):
                v = unit_no(qh, 0, j)
                act.wait_ge(A[1, "s_mm"], NU2 * g + v + 1)
                if j % 2 == 0:
                    act.wait_ge(A[1, "pv"], PV2 + NW2 * g + KT * (qh - 1) + j // 2 + 1)
                act_factor(act, unit_weights(j), v, qh == 0)
                if last and j == 2 * (LAG + 1) + 1:
                    act_out(act, 1, *last, PV2 + NW2 * last[0] + KT * (last[1] + 1))

        def act_second_pass(act, g, qh):
            for j in range(NUP):
                v = unit_no(qh, 1, j)
                act.wait_ge(A[1, "s_mm"], NU2 * g + v + 1)
                act.wait_ge(A[1, "mul"], MUL2 + 2 * NW2 * g + NUP * qh + j - RING + 1)
                act_factor(act, GR[j % RING], v, qh == 1)

        def act_gated(act, g, more):
            act_second_pass(act, g, 0)
            act_first_pass(act, g, 1, (g, 0))
            act_second_pass(act, g, 1)
            if more:
                act_first_pass(act, g + 1, 0, (g, 1))
            else:
                act_out(act, 1, g, 1, PV2 + NW2 * g + NW2)

        def dve_gated(dve, own, g):
            for qh in range(QH):
                for j in range(NUP):
                    dve.wait_ge(A[1, "s_act"], NU2 * g + unit_no(qh, 1, j) + 2)
                    w = unit_weights(j)
                    dve.tensor_tensor(w, w, GR[j % RING], ALU.mult).then_inc(A[1, "mul"], 1)
                dve_out(dve, own, 1, g, qh)

        FQ1 = arena(16384, 512).bitcast(I32)
        FQ2 = arena(16896, 512).bitcast(I32)
        FW1 = arena(17408, 512)
        FW2 = arena(17920, 512)
        FS2 = arena(18432, 512)
        HID0 = [arena(19456 + 2048 * i, 2048).rearrange("p (m n) -> p m n", n=CH) for i in range(2)]
        HID4 = [arena(23552 + 2048 * i, 2048).rearrange("p (m n) -> p m n", n=CH) for i in range(2)]
        LI = arena(0, 1152).bitcast(I32)
        LF = arena(1152, 1152)
        L2A = arena(2304, 512)
        L2B = arena(2816, 512)
        R2W = arena(3328, E2)
        R2B = arena(3344, E2)
        R3W = arena(3360, E3)
        R3B = arena(3368, E3)
        HEADM = arena(3376, H)
        BLOCKM = arena(3392, D)
        MG = arena(3584, R2 * P)
        MU = arena(6784, R2 * P)
        MD = arena(9984, R2 * P)
        SEL2 = ARENA[:, 13184:14784].bitcast(BF16)
        M3A = arena(14784, E3 * F3)
        M3B = arena(18880, E3 * F3)
        SEL3 = ARENA[:, 22976:23488].bitcast(BF16)
        MGH, MUH = rounded(14784, R2 * P), rounded(14784 + R2 * P, R2 * P)
        MDH = rounded(0, R2 * P)
        MGL, MUL, MDL = [rounded(3584 + R2 * P * i, R2 * P) for i in range(3)]
        M3AH, M3BH = rounded(3584, E3 * F3), rounded(3584 + E3 * F3, E3 * F3)
        M3AL, M3BL = rounded(14784, E3 * F3), rounded(14784 + E3 * F3, E3 * F3)
        HTL = {5: rounded(14784 + 2 * R2 * P, TOK), 7: rounded(3584 + 2 * E3 * F3, TOK)}
        WORK = 23552

        def work(at, n):
            return arena(WORK + at, n)

        def work_rounded(at, n):
            return rounded(WORK + at, n)

        f0_in = sem("f0_in")
        N_LATE = (1, 3, 4, 3)
        late_in = [sem(f"late_in{i}") for i in range(4)]

        def late(eng, upto):
            for part in range(upto + 1):
                eng.wait_ge(late_in[part], 16 * N_LATE[part])

        def sp_late(sp):
            if on(2):
                sp.wait_ge(A[1, "pv"], NW2 * NG + PV2)
            for part, loads in enumerate((
                    ((LI, l1int),),
                    ((arena(2304, 1024), l2fc), (arena(3328, 48), r2w), (arena(3376, H + D), r2b)),
                    ((MG, moe2[0]), (MU, moe2[1]), (MD, moe2[2]), (SEL2[0:51, :], moe2sel.bitcast(BF16))),
                    ((M3A, moe3a), (M3B, moe3b), (SEL3[0:3 * E3, :], r3w.bitcast(BF16))))):
                if part == 3 and on(5):
                    sp.wait_ge(y_ready, YB[6])
                for dst, src in loads:
                    sp.dma_start(dst, src).then_inc(late_in[part], 16)
            late(sp, 3)

        YB = {n: NC * sum(1 for m in range(n) if on(m)) for n in range(9)}

        def ffn_sems(n):
            for nm in ("f_w", "f_mm", "f_act"):
                A[n, nm] = sem(f"S{n}_{nm}")

        ffn_sems(1)
        ffn_sems(4)

        def pe_ffn(pe, n, n_h, w1, w2, hid, bias):
            pe.wait_ge(h_ready, n_h)

            def down(c):
                pe.wait_ge(A[n, "f_act"], 4 * c + 4)
                for i in range(TPC):
                    pe_y(pe, TPC * c + i, [(hid[c % 2][:, m, i * P:i * P + P], w2[:, m * D:m * D + D])
                                           for m in range(4)], bias)
            for c in range(NC):
                for m in range(4):
                    if c:
                        pe.wait_ge(A[n, "f_act"], 4 * (c - 1) + m + 1)
                    pe.matmul(bank(m), w1[:, m * P:m * P + P], chunk(hT, c), start=True, stop=True)\
                      .then_inc(A[n, "f_mm"], 1)
                if c:
                    down(c - 1)
            down(NC - 1)

        def act_ffn(act, n, hid, func, scale, bias):
            for c in range(NC):
                if c >= 2:
                    act.wait_ge(y_ready, YB[n] + c - 1)
                for m in range(4):
                    act.wait_ge(A[n, "f_mm"], 4 * c + m + 1)
                    act.activation(hid[c % 2][:, m, :], bank(m), func, bias=bias(m),
                                   scale=scale(m) if scale else 1.0).then_inc(A[n, "f_act"], 1)

        def dve_dequant0(dve):
            dve.wait_ge(f0_in, 48)
            dve.tensor_scalar(FW1, FQ1, 128.0, None, ALU.subtract)
            dve.scalar_tensor_tensor(out=FW2, in0=FQ2, scalar=128.0, in1=FS2, op0=ALU.subtract,
                                     op1=ALU.mult).then_inc(A[1, "f_w"], 1)

        for nm in ("w", "mm", "sg", "mul"):
            A[3, nm] = sem(f"S3_{nm}")
        M3 = 3
        HID3 = [work(1536 * i, 1536).rearrange("p (m n) -> p m n", n=CH) for i in range(2)]
        SG3 = [work(3072 + 512 * i, 512) for i in range(2)]

        def pe_glu(pe, n_h):
            pe.wait_ge(h_ready, n_h)
            pe.wait_ge(A[3, "w"], 1)

            def down(c):
                pe.wait_ge(A[3, "mul"], M3 * c + M3)
                for i in range(TPC):
                    pe_y(pe, TPC * c + i, [(HID3[c % 2][:, m, i * P:i * P + P],
                                            LF[:, 768 + m * D:768 + m * D + D]) for m in range(M3)], None)
            for c in range(NC):
                for m in range(M3):
                    n = M3 * c + m
                    if n >= 2:
                        pe.wait_ge(A[3, "mul"], n - 1)
                    pe.matmul(bank(n % 2), LF[:, m * P:m * P + P], chunk(hT, c), start=True, stop=True)
                    pe.matmul(bank(2 + n % 2), LF[:, 384 + m * P:384 + m * P + P], chunk(hT, c),
                              start=True, stop=True).then_inc(A[3, "mm"], 1)
                if c:
                    down(c - 1)
            down(NC - 1)

        def act_glu(act):
            for n in range(M3 * NC):
                act.wait_ge(A[3, "mm"], n + 1)
                if n >= 2:
                    act.wait_ge(A[3, "mul"], n - 1)
                act.activation(SG3[n % 2], bank(n % 2), ACT.Silu).then_inc(A[3, "sg"], 1)

        def dve_glu(dve):
            for n in range(M3 * NC):
                c, m = divmod(n, M3)
                dve.wait_ge(A[3, "sg"], n + 1)
                if m == 0 and c >= 2:
                    dve.wait_ge(y_ready, YB[3] + c - 1)
                dve.tensor_tensor(HID3[c % 2][:, m, :], SG3[n % 2], bank(2 + n % 2), ALU.mult)\
                   .then_inc(A[3, "mul"], 1)

        NJ = NC + NT // 2
        T1 = [work(512 * i, 512) for i in range(2)]
        T2 = [work(1024 + 512 * i, 512) for i in range(2)]
        QFT = work(2048, TOK)
        KF = work(4096, TOK)
        VF = work(6144, NT * 130).rearrange("p (t e) -> p t e", e=130)
        KVB = [work(8224 + 144 * i, 144) for i in range(2)]
        RD = work(8512, 32)
        for n in (4, 6):
            for nm in ("mm", "exp", "vf", "feat", "kv", "kvb", "l_mm", "o", "aT", "aTs", "pj"):
                A[n, nm] = sem(f"S{n}_{nm}")

        def job_view(j, v=0):
            if j < NC:
                return bank(j)
            return bank(4 + (j - NC) % 4).rearrange("p (t e) -> p t e", t=2)[:, :, v * D:v * D + D]

        def as_job(j, buf):
            return buf if j < NC else buf[:, 0:2 * D].rearrange("p (t e) -> p t e", t=2)

        def pe_linear(pe, n, n_h, q, kv, kvrow, z):
            pe.wait_ge(h_ready, n_h)
            for c in range(NC):
                pe.matmul(bank(c), W[:, q, :], chunk(hT, c), start=True, stop=True).then_inc(A[n, "mm"], 1)
            for t in range(NT):
                i = t // 2
                if t % 2 == 0 and i >= 4:
                    pe.wait_ge(A[n, "feat"], NC + i - 3)
                    pe.wait_ge(A[n, "vf"], i - 3)
                dst = bank(4 + i % 4, t % 2 * 256, t % 2 * 256 + 256)
                ins = pe.matmul(dst, tile(hT, t), W[:, kv:kv + 2, :].rearrange("p a b -> p (a b)"),
                                start=True, stop=kvrow is None)
                if kvrow is not None:
                    ins = pe.matmul(dst, ones1[:, :], RWS[:, kvrow:kvrow + 256], start=False, stop=True)
                if t % 2:
                    ins.then_inc(A[n, "mm"], 1)
            pe.wait_ge(A[n, "feat"], NJ)
            pe.wait_ge(A[n, "vf"], NT // 2)
            for b in range(B):
                for k in range(KT):
                    t = b * KT + k
                    ins = pe.matmul(bank(b, 0, D + z), tile(KF, t), VF[:, t, 0:D + z],
                                    start=k == 0, stop=k == KT - 1)
                ins.then_inc(A[n, "kv"], 1)

        def act_linear(act, n, bias):
            for j in range(NJ):
                act.wait_ge(A[n, "mm"], j + 1)
                if j >= 2:
                    act.wait_ge(A[n, "feat"], j - 1)
                kw = dict(bias=bias) if bias is not None and j < NC else {}
                act.activation(as_job(j, T1[j % 2]), job_view(j), ACT.Exp, **kw)
                act.activation(as_job(j, T2[j % 2]), job_view(j), ACT.Relu, **kw).then_inc(A[n, "exp"], 1)
                if j >= NC:
                    i = j - NC
                    act.activation(VF[:, 2 * i:2 * i + 2, 0:D], job_view(j, 1), ACT.Copy)\
                       .then_inc(A[n, "vf"], 1)

        def dve_linear(dve, n, z):
            if z:
                dve.memset(VF[:, :, D:D + 1], 1.0)
            for j in range(NJ):
                dve.wait_ge(A[n, "exp"], j + 1)
                dst = chunk(QFT, j) if j < NC else \
                    KF[:, (j - NC) * 256:(j - NC) * 256 + 256].rearrange("p (t e) -> p t e", t=2)
                dve.scalar_tensor_tensor(out=dst, in0=as_job(j, T1[j % 2]), scalar=1.0,
                                         in1=as_job(j, T2[j % 2]), op0=ALU.min, op1=ALU.add)\
                   .then_inc(A[n, "feat"], 1)
            for b in range(B):
                dve.wait_ge(A[n, "kv"], b + 1)
                ins = dve.tensor_tensor(KVB[b][:, 0:D], bank(b, 0, D), BLOCKM, ALU.mult)
                if z:
                    ins = dve.tensor_scalar(KVB[b][:, D:D + H], HEADM, bank(b, D, D + 1), None, ALU.mult)
                ins.then_inc(A[n, "kvb"], 1)

        def pe_linear_norm(pe, n, out_w, bias):
            pe.wait_ge(A[n, "kvb"], B)
            for i in range(NT // 2):
                if i >= 2:
                    pe.wait_ge(A[n, "o"], i - 1)
                for k in range(2):
                    t = 2 * i + k
                    ins = pe.matmul(bank(2 + i % 2, k * 256, k * 256 + D + H), tile(QFT, t),
                                    KVB[t // KT], start=True, stop=True)
                ins.then_inc(A[n, "l_mm"], 1)
            for t in range(NT):
                if t % 2 == 0:
                    pe.wait_ge(A[n, "o"], t // 2 + 1)
                ins = pe.transpose(PS[:, 4 * CH + t * D:4 * CH + t * D + D], tile(XN, t), ident[:, :])
                if t % TPC == TPC - 1:
                    ins.then_inc(A[n, "aT"], 1)
            for t in range(NT):
                if t % TPC == 0:
                    pe.wait_ge(A[n, "aTs"], t // TPC + 1)
                pe_y(pe, t, [(tile(hT, t), W[:, out_w, :])], bias, at=0, ready=A[n, "pj"])

        def act_linear_norm(act, n):
            for c in range(NC):
                act.wait_ge(A[n, "aT"], c + 1)
                act.activation(chunk(hT, c), bank(4 + c), ACT.Copy).then_inc(A[n, "aTs"], 1)

        def dve_linear_norm(dve, own, n):
            for i in range(NT // 2):
                dve.wait_ge(A[n, "l_mm"], i + 1)
                v = bank(2 + i % 2).rearrange("p (t e) -> p t e", t=2)
                r = RD.rearrange("p (t h) -> p t h", t=2)
                if i:
                    dve.wait_ge(A[n, "o"], i)
                own.link(dve.tensor_scalar(r, v[:, :, D:D + H], 1e-6, None, ALU.add))
                own.link(dve.reciprocal(r, r))
                dve.tensor_tensor(XN[:, i * 256:i * 256 + 256].rearrange("p (t h d) -> p t h d", t=2, h=H),
                                  v[:, :, 0:D].rearrange("p t (h d) -> p t h d", h=H),
                                  r.unsqueeze(3).broadcast_to([P, 2, H, HD]), ALU.mult)\
                   .then_inc(A[n, "o"], 1)

        def pe_linear_plain(pe, n, out_w, bias):
            pe.wait_ge(A[n, "kvb"], B)
            for c in range(NC):
                if c >= 2:
                    pe.wait_ge(A[n, "aTs"], c - 1)
                pe.matmul(bank(2 + c % 2), KVB[c // QH][:, 0:D], chunk(QFT, c), start=True, stop=True)\
                  .then_inc(A[n, "aT"], 1)
            for t in range(NT):
                if t % TPC == 0:
                    pe.wait_ge(A[n, "aTs"], t // TPC + 1)
                pe_y(pe, t, [(tile(hT, t), W[:, out_w, :])], bias)

        def act_linear_plain(act, n):
            for c in range(NC):
                act.wait_ge(A[n, "aT"], c + 1)
                act.activation(chunk(hT, c), bank(2 + c % 2), ACT.Copy).then_inc(A[n, "aTs"], 1)

        def dve_top_k(dve, own, vals, e, k, sel, best, tmp):
            a, b, c = tmp
            for t in range(NT):
                ins = dve.max(best[:, t, :], vals[:, t, :])
            own.link(ins)
            kth = best[:, :, k - 1:k].broadcast_to([P, NT, e])
            dve.tensor_tensor(sel, vals, kth, ALU.is_gt)
            own.link(dve.tensor_tensor(a, vals, kth, ALU.is_equal))
            own.link(dve.tensor_reduce(out=best[:, :, 7:8] if k < 8 else None, in_=sel, axis=AX.X, op=ALU.add))
            own.link(dve.tensor_scalar(best[:, :, 7:8], best[:, :, 7:8], -1.0, float(k), ALU.mult, ALU.add))
            src, dst, n = a, b, 1
            while n < e:
                dve.tensor_copy(dst[:, :, 0:n], src[:, :, 0:n])
                own.link(dve.tensor_tensor(dst[:, :, n:e], src[:, :, n:e], src[:, :, 0:e - n], ALU.add))
                src, dst = dst, (c if dst is b else b)
                n *= 2
            own.link(dve.tensor_tensor(dst, src, best[:, :, 7:8].broadcast_to([P, NT, e]), ALU.is_le))
            own.link(dve.tensor_tensor(dst, dst, a, ALU.mult))
            own.link(dve.tensor_tensor(sel, sel, dst, ALU.add))

        def dve_bf16_parts(dve, own, src, dst, rest, e):
            own.link(dve.tensor_copy(dst[:, :, 0, 0:e], src))
            own.link(dve.tensor_tensor(rest, src, dst[:, :, 0, 0:e], ALU.subtract))
            own.link(dve.tensor_copy(dst[:, :, 1, 0:e], rest))
            return dve.tensor_tensor(dst[:, :, 2, 0:e], rest, dst[:, :, 1, 0:e], ALU.subtract)

        def grid(at, e):
            return work(at, NT * e).rearrange("p (t e) -> p t e", e=e)

        for n in (5, 7):
            for nm in ("lg", "sc", "sc2", "cw", "cwT", "cwTs"):
                A[n, nm] = sem(f"S{n}_{nm}")

        CWB5 = ARENA[:, WORK + 7168:WORK + 7168 + 408].bitcast(BF16).rearrange("p (t c e) -> p t c e", c=3, e=17)
        CWT = ARENA[:, WORK + 7680:WORK + 8704].bitcast(BF16)
        CWB7 = ARENA[:, WORK + 7168:WORK + 7168 + 192].bitcast(BF16).rearrange("p (t c e) -> p t c e", c=3, e=E3)
        SC5 = grid(5120, E2)

        def pe_logits(pe, n, n_h, w, e):
            pe.wait_ge(h_ready, n_h)
            for t in range(NT):
                ins = pe.matmul(bank(6, t * e, t * e + e), tile(XH, t), w, start=True, stop=True)
            ins.then_inc(A[n, "lg"], 1)

        def pe_turn_weights(pe, n, cwb, rows):
            pe.wait_ge(A[n, "cw"], 1)
            for t in range(NT):
                v = PS[:, 6 * CH:8 * CH].bitcast(BF16)
                ins = pe.transpose(v[0:rows, t * P:t * P + P], cwb[:, t].rearrange("p c e -> p (c e)"),
                                   identb[:, :])
            ins.then_inc(A[n, "cwT"], 1)

        def act_turn_weights(act, n, rows):
            act.wait_ge(A[n, "cwT"], 1)
            for k in range(2):
                ins = act.activation(CWT[0:rows, k * S:k * S + S], bank(6 + k).bitcast(BF16)[0:rows, :], ACT.Copy)
            ins.then_inc(A[n, "cwTs"], 1)

        def dve_route5(dve, own):
            g4 = lambda at: work(at, NT * 4)
            SF, SEL, TMP = grid(5376, E2), grid(5632, E2), grid(5888, E2)
            U1, U2, U3 = grid(6144, E2), grid(6400, E2), grid(6656, E2)
            BEST = work(6912, NT * 8).rearrange("p (t e) -> p t e", e=8)
            GS, GR = work(7040, NT * 4), work(7104, NT * 4)
            dve.wait_ge(A[5, "sc"], 1)
            own.link(dve.tensor_tensor(SF, SC5, R2B.unsqueeze(1).broadcast_to([P, NT, E2]), ALU.add))
            v = SF.rearrange("p t (g j) -> p (t g) j", j=4)
            first = True
            w = U1.rearrange("p t e -> p (t e)")[:, 0:NT * 4]
            for i in range(4):
                for j in range(i + 1, 4):
                    if first:
                        own.link(dve.tensor_tensor(GS, v[:, :, i], v[:, :, j], ALU.add))
                    else:
                        own.link(dve.tensor_tensor(w, v[:, :, i], v[:, :, j], ALU.add))
                        own.link(dve.tensor_tensor(GS, GS, w, ALU.max))
                    first = False
            gs = GS.rearrange("p (t g) -> p t g", g=4)
            gr = GR.rearrange("p (t g) -> p t g", g=4)
            u = w.rearrange("p (t g) -> p t g", g=4)
            own.link(dve.memset(GR, 0.0))
            for g in range(4):
                other = gs[:, :, g:g + 1]
                if g + 1 < 4:
                    dve.tensor_tensor(u[:, :, g + 1:4], other.broadcast_to([P, NT, 3 - g]), gs[:, :, g + 1:4], ALU.is_ge)
                if g:
                    dve.tensor_tensor(u[:, :, 0:g], other.broadcast_to([P, NT, g]), gs[:, :, 0:g], ALU.is_gt)
                own.link(dve.memset(u[:, :, g:g + 1], 0.0))
                own.link(dve.tensor_tensor(gr, gr, u, ALU.add))
            own.link(dve.tensor_scalar(GR, GR, 1.5, None, ALU.is_lt))
            m = TMP.rearrange("p t (g j) -> p (t g) j", j=4)
            own.link(dve.tensor_tensor(m, v, GR.unsqueeze(2).broadcast_to([P, NT * 4, 4]), ALU.mult))
            dve_top_k(dve, own, TMP, E2, 4, SEL, BEST, (U1, U2, U3))
            own.link(dve.tensor_tensor(SEL, SEL, SC5, ALU.mult))
            own.link(dve.tensor_reduce(out=BEST[:, :, 0:1], in_=SEL, axis=AX.X, op=ALU.add))
            own.link(dve.tensor_scalar(BEST[:, :, 0:1], BEST[:, :, 0:1], 1e-20, None, ALU.add))
            own.link(dve.reciprocal(BEST[:, :, 1:2], BEST[:, :, 0:1]))
            own.link(dve.tensor_tensor(SEL, SEL, BEST[:, :, 1:2].broadcast_to([P, NT, E2]), ALU.mult))
            own.link(dve.memset(CWB5[:, :, 0, 16:17], 1.0))
            own.link(dve.memset(CWB5[:, :, 1:3, 16:17], 0.0))
            dve_bf16_parts(dve, own, SEL, CWB5, U1, E2).then_inc(A[5, "cw"], 1)

        for nm in ("htl", "w", "w_own", "gm", "um", "sg", "t", "p", "hi", "h", "dm", "ot"):
            A[5, nm] = sem(f"S5_{nm}")
        HL5 = [work_rounded(512 * i, 512) for i in range(2)]
        TM5 = [work(1024 + 512 * i, 512) for i in range(2)]
        HD5 = [work_rounded(2048 + 512 * i, 512) for i in range(2)]
        OT5 = work(3072, TOK)
        spare = KZ[0].rearrange("p h n -> p (h n)").bitcast(F32)
        PR5 = [spare[:, CH * i:CH * i + CH] for i in range(2)]
        SG5 = [spare[:, CH * (2 + i):CH * (3 + i)] for i in range(2)]

        for nm in ("htl", "w", "w_own"):
            A[7, nm] = sem(f"S7_{nm}")

        def pool_split_weights(pool, stage, pairs):
            for n, (raw, hi, rest) in enumerate(pairs):
                if raw is MD and on(4):
                    pool.wait_ge(y_ready, YB[5])
                pool.tensor_copy(hi, raw).then_inc(A[stage, "w_own"], 1)
                pool.wait_ge(A[stage, "w_own"], n + 1)
                pool.tensor_tensor(rest, raw, hi.bitcast(F32), ALU.subtract).then_inc(A[stage, "w"], 1)

        def pool_rest_of_h(pool, n):
            for c in range(NC):
                pool.wait_ge(h_ready, edges[n].n_x + c + 1)
                pool.tensor_tensor(chunk(HTL[n], c), chunk(XH, c), chunk(hR, c).bitcast(F32), ALU.subtract)\
                    .then_inc(A[n, "htl"], 1)

        def before(c, r, n):
            return BASE + n * c + (r - 1 if r >= 2 else 0)

        def pe_parts(pe, dst, w, x, start, stop):
            pe.matmul(dst, w[0], x[0], start=start, stop=False)
            pe.matmul(dst, w[0], x[1], start=False, stop=False)
            return pe.matmul(dst, w[1], x[0], start=False, stop=stop)

        def pe_moe5(pe):
            pe.wait_ge(A[5, "htl"], NC)
            pe.wait_ge(A[5, "w"], 3)
            pe.wait_ge(A[5, "cwTs"], 1)

            def down(c, r):
                pe.wait_ge(A[5, "h"], BASE + R2 * c + r + 1)
                if r == 0:
                    pe.wait_ge(A[5, "ot"], BASE + c)
                k = slice(r * D, r * D + D)
                pe_parts(pe, bank(6), (MDH[:, k], MDL[:, k]), (HD5[r % 2], HL5[r % 2]),
                         r == 0, r == R2 - 1).then_inc(A[5, "dm"], 1)
            with pe.Fori(0, NC) as c:
                x = (chunk(hR, c), chunk(HTL[5], c))
                for r in range(R2):
                    k = slice(r * P, r * P + P)
                    pe.wait_ge(A[5, "sg"], before(c, r, R2))
                    pe_parts(pe, bank(r % 2), (MGH[:, k], MGL[:, k]), x, True, True).then_inc(A[5, "gm"], 1)
                    pe.wait_ge(A[5, "p"], before(c, r, R2))
                    pe_parts(pe, bank(2 + r % 2), (MUH[:, k], MUL[:, k]), x, True, True)
                    pe.matmul(bank(4 + r % 2), SEL2[0:51, k], chunk(CWT[0:51, :], c), start=True, stop=True)\
                      .then_inc(A[5, "um"], 1)
                    if r >= 2:
                        down(c, r - 2)
                down(c, R2 - 2)
                down(c, R2 - 1)
            pe.wait_ge(A[5, "ot"], BASE + NC)
            pe_turn_y(pe, OT5)

        def pe_turn_y(pe, src):
            for t in range(NT):
                ins = pe.transpose(PS[:, 4 * CH + t * D:4 * CH + t * D + D], tile(src, t), ident[:, :])
                if t % TPC == TPC - 1:
                    ins.then_inc(y_ready, 1)

        def act_moe5(act):
            def upper(c, r):
                act.wait_ge(A[5, "p"], BASE + R2 * c + r + 1)
                act.wait_ge(A[5, "dm"], before(c, r, R2))
                act.activation(HD5[r % 2], PR5[r % 2], ACT.Copy).then_inc(A[5, "hi"], 1)
            with act.Fori(0, NC) as c:
                for r in range(R2):
                    act.wait_ge(A[5, "gm"], R2 * c + r + 1)
                    act.wait_ge(A[5, "t"], before(c, r, R2))
                    act.activation(SG5[r % 2], bank(r % 2), ACT.Silu).then_inc(A[5, "sg"], 1)
                    if r:
                        upper(c, r - 1)
                upper(c, R2 - 1)
                act.wait_ge(A[5, "dm"], BASE + R2 * c + R2)
                act.activation(chunk(OT5, c), bank(6), ACT.Copy).then_inc(A[5, "ot"], 1)

        def dve_moe5(dve):
            def rest(c, r):
                dve.wait_ge(A[5, "hi"], R2 * c + r + 1)
                dve.tensor_tensor(HL5[r % 2], PR5[r % 2], HD5[r % 2].bitcast(F32), ALU.subtract)\
                   .then_inc(A[5, "h"], 1)
            with dve.Fori(0, NC) as c:
                for r in range(R2):
                    dve.wait_ge(A[5, "sg"], BASE + R2 * c + r + 1)
                    dve.wait_ge(A[5, "um"], R2 * c + r + 1)
                    dve.wait_ge(A[5, "p"], before(c, r, R2))
                    dve.tensor_tensor(TM5[r % 2], SG5[r % 2], bank(4 + r % 2), ALU.mult)\
                       .then_inc(A[5, "t"], 1)
                    if r:
                        rest(c, r - 1)
                    dve.wait_ge(A[5, "t"], BASE + R2 * c + r + 1)
                    dve.wait_ge(A[5, "h"], before(c, r, R2))
                    dve.tensor_tensor(PR5[r % 2], TM5[r % 2], bank(2 + r % 2), ALU.mult)\
                       .then_inc(A[5, "p"], 1)
                rest(c, R2 - 1)

        for nm in ("hm", "ge", "hi", "lo", "w2", "wr", "ye", "ca", "cb", "cc", "acc"):
            A[7, nm] = sem(f"S7_{nm}")
        spare7 = QS[0][:, :, :].rearrange("p a n -> p (a n)").bitcast(F32)
        GE7 = [arena(2048 + 512 * i, 512) for i in range(2)] + [spare7[:, 512 * i:512 * i + 512] for i in range(2)]
        HG7 = [rounded(512 * i, 512) for i in range(4)]
        HL7 = [work_rounded(512 * i, 512) for i in range(4)]
        YE7 = [work(2048 + 512 * i, 512) for i in range(2)]
        CA7 = work(3072, 512)
        CB7 = work(3584, 512)
        CC7 = work(4096, 512)
        ACC7 = work(4608, TOK)
        M7 = E3 * 4

        def dve_route7(dve, own):
            SC, SEL = grid(3072, E3), grid(3200, E3)
            U1, U2, U3 = grid(3328, E3), grid(3456, E3), grid(3584, E3)
            BEST = grid(3712, E3)
            MXS = grid(3840, 2)
            lg = bank(6, 0, NT * E3).rearrange("p (t e) -> p t e", e=E3)
            dve.wait_ge(A[7, "lg"], 1)
            own.link(dve.tensor_tensor(SC, lg, R3B.unsqueeze(1).broadcast_to([P, NT, E3]), ALU.add))
            own.link(dve.tensor_reduce(out=MXS[:, :, 0:1], in_=SC, axis=AX.X, op=ALU.max))
            dve.tensor_tensor(SC, SC, MXS[:, :, 0:1].broadcast_to([P, NT, E3]), ALU.subtract)\
               .then_inc(A[7, "sc"], 1)
            dve.wait_ge(A[7, "sc2"], 1)
            own.link(dve.tensor_reduce(out=MXS[:, :, 0:1], in_=SC, axis=AX.X, op=ALU.add))
            own.link(dve.reciprocal(MXS[:, :, 1:2], MXS[:, :, 0:1]))
            own.link(dve.tensor_tensor(SC, SC, MXS[:, :, 1:2].broadcast_to([P, NT, E3]), ALU.mult))
            dve_top_k(dve, own, SC, E3, 2, SEL, BEST, (U1, U2, U3))
            dve.tensor_tensor(SC, SC, BEST[:, :, 0:1].broadcast_to([P, NT, E3]), ALU.subtract)\
               .then_inc(A[7, "sc"], 1)
            dve.wait_ge(A[7, "sc2"], 2)
            own.link(dve.tensor_tensor(SEL, SEL, SC, ALU.mult))
            own.link(dve.tensor_reduce(out=MXS[:, :, 0:1], in_=SEL, axis=AX.X, op=ALU.add))
            own.link(dve.reciprocal(MXS[:, :, 1:2], MXS[:, :, 0:1]))
            own.link(dve.tensor_tensor(SEL, SEL, MXS[:, :, 1:2].broadcast_to([P, NT, E3]), ALU.mult))
            dve_bf16_parts(dve, own, SEL, CWB7, U1, E3).then_inc(A[7, "cw"], 1)

        def act_route7(act):
            for i in range(2):
                act.wait_ge(A[7, "sc"], i + 1)
                act.activation(work(3072, NT * E3), work(3072, NT * E3), ACT.Exp).then_inc(A[7, "sc2"], 1)

        BASE7 = 4
        DOWN7 = 3
        STEPS7 = M7 + 8

        def pe_moe7(pe):
            pe.wait_ge(A[7, "htl"], NC)
            pe.wait_ge(A[7, "w"], 2)
            pe.wait_ge(A[7, "cwTs"], 1)

            def second(c, m):
                e, k = divmod(m, 4)
                pe.wait_ge(A[7, "lo"], BASE7 + M7 * c + m + 1)
                if k == 0:
                    pe.wait_ge(A[7, "ye"], before(c, e, E3))
                at = slice(m * D, m * D + D)
                pe_parts(pe, bank(4 + e % 2), (M3BH[:, at], M3BL[:, at]), (HG7[m % 4], HL7[m % 4]),
                         k == 0, k == 3).then_inc(A[7, "w2"], 1)
            with pe.Fori(0, NC) as c:
                x = (chunk(hR, c), chunk(HTL[7], c))
                for m in range(STEPS7):
                    e = (m - 6) // 4
                    broadcast = m % 4 == 2 and 0 <= e < E3
                    if broadcast:
                        pe.wait_ge(A[7, "cc"], before(c, e, E3))
                    if m < M7:
                        at = slice(m * P, m * P + P)
                        pe.wait_ge(A[7, "ge"], BASE + M7 * c + (m - 3 if m >= 4 else 0))
                        pe_parts(pe, bank(m % 4), (M3AH[:, at], M3AL[:, at]), x, True, True).then_inc(A[7, "hm"], 1)
                    if DOWN7 <= m < M7 + DOWN7:
                        second(c, m - DOWN7)
                    if broadcast:
                        pe.matmul(bank(6 + e % 2), SEL3[0:3 * E3, e * P:e * P + P],
                                  chunk(CWT[0:3 * E3, :], c), start=True, stop=True).then_inc(A[7, "wr"], 1)
            pe.wait_ge(A[7, "acc"], BASE + E3 * NC)
            pe_turn_y(pe, ACC7)

        def act_moe7(act):
            with act.Fori(0, NC) as c:
                for m in range(STEPS7):
                    if m < M7:
                        act.wait_ge(A[7, "hm"], M7 * c + m + 1)
                        act.wait_ge(A[7, "lo"], BASE7 + M7 * c + m - 3)
                        act.activation(GE7[m % 4], bank(m % 4), ACT.Gelu, bias=col("eb1", m))\
                           .then_inc(A[7, "ge"], 1)
                    if 1 <= m < M7 + 1:
                        n = m - 1
                        act.wait_ge(A[7, "ge"], BASE + M7 * c + n + 1)
                        act.wait_ge(A[7, "w2"], BASE + M7 * c + (n - 3 if n >= 4 else 0))
                        act.activation(HG7[n % 4], GE7[n % 4], ACT.Copy).then_inc(A[7, "hi"], 1)
                    e = (m - 7) // 4
                    if m % 4 == 3 and 0 <= e < E3:
                        act.wait_ge(A[7, "w2"], BASE + M7 * c + 4 * e + 4)
                        act.wait_ge(A[7, "cb"], before(c, e, E3))
                        act.activation(YE7[e % 2], bank(4 + e % 2), ACT.Identity, bias=col("eb2", e))\
                           .then_inc(A[7, "ye"], 1)

        def dve_moe7(dve):
            def station(c, e, k):
                n = E3 * c + e
                if k == 0:
                    dve.wait_ge(A[7, "ye"], BASE + n + 1)
                    dve.wait_ge(A[7, "cb"], BASE + n)
                    dve.tensor_scalar(CA7, YE7[e % 2], 0.0, None, ALU.max).then_inc(A[7, "ca"], 1)
                elif k == 1:
                    dve.wait_ge(A[7, "ca"], n + 1)
                    dve.wait_ge(A[7, "cc"], BASE + n)
                    dve.scalar_tensor_tensor(out=CB7, in0=YE7[e % 2], scalar=0.0, in1=CA7,
                                             op0=ALU.min, op1=ALU.add).then_inc(A[7, "cb"], 1)
                elif k == 2:
                    dve.wait_ge(A[7, "cb"], BASE + n + 1)
                    dve.wait_ge(A[7, "wr"], n + 1)
                    dve.wait_ge(A[7, "acc"], BASE + n)
                    dst = chunk(ACC7, c) if e == 0 else CC7
                    dve.tensor_tensor(dst, CB7, bank(6 + e % 2), ALU.mult).then_inc(A[7, "cc"], 1)
                else:
                    dve.wait_ge(A[7, "cc"], BASE + n + 1)
                    if e == 0:
                        ins = dve.memset(ZERO[:, 31:32], 0.0)
                    else:
                        ins = dve.tensor_tensor(chunk(ACC7, c), chunk(ACC7, c), CC7, ALU.add)
                    ins.then_inc(A[7, "acc"], 1)
            with dve.Fori(0, NC) as c:
                for m in range(STEPS7):
                    if m < M7:
                        dve.wait_ge(A[7, "hi"], M7 * c + m + 1)
                        dve.wait_ge(A[7, "w2"], BASE + M7 * c + (m - 3 if m >= 4 else 0))
                        dve.tensor_tensor(HL7[m % 4], GE7[m % 4], HG7[m % 4].bitcast(F32), ALU.subtract)\
                           .then_inc(A[7, "lo"], 1)
                    e, k = m // 4 - 2, m % 4
                    if 0 <= e < E3:
                        station(c, e, k)

        def y_of(n):
            if n == 0 or not on(n - 1):
                return {}
            return dict(y=y_ready, y0=YB[n - 1], add={1: 0.5, 4: 1.0}.get(n - 1))

        NEXT = {1: dict(eps2=1, keep=True, scale=col("g0"), bias=col("b0")),
                2: dict(eps2=2, scale=col("g1"), bias=col("bb1")),
                4: dict(eps2=1, keep=True, scale=col("g2a"), bias=col("b2a")),
                5: dict(split=True), 7: dict(split=True)}
        edges = {}
        for n in range(9):
            if n < 8 and on(n):
                edges[n] = Edge(**y_of(n), **NEXT.get(n, {}))
            elif y_of(n):
                edges[n] = Edge(**y_of(n), turn=False)
            if n == 4 and on(4):
                edges["4b"] = Edge(y=A[4, "pj"], y_at=0, inner=True, scale=col("g2b"), bias=col("b2b"))

        NBASE = 3
        block = ctx.enter_context(nc.Block())

        @block.sync
        def _(sp):
            xv = x.rearrange("b (k p) d -> p (b k) d", p=P)
            Xv = X[:, :].rearrange("p (t d) -> p t d", d=D)
            for c in range(NC):
                k = slice(c * TPC, c * TPC + TPC)
                sp.dma_start(Xv[:, k], xv[:, k]).then_inc(x_in[c], 16)
            sp.dma_start(W[:, :, :], w).then_inc(w_in, 16)
            sp.dma_start(C[:, :], cols).then_inc(c_in, 16)
            sp.dma_start(RWS[:, :], rows).then_inc(c_in, 16)
            sp.dma_start(maskA[:, :], consts[0].bitcast(BF16)).then_inc(c_in, 16)
            sp.dma_start(maskB[:, :], consts[1].bitcast(BF16)).then_inc(c_in, 16)
            if on(0):
                sp.dma_start(COS, rope[0]).then_inc(rope_in, 16)
                sp.dma_start(SIN, rope[1]).then_inc(rope_in, 16)
            if on(1):
                for dst, src in ((FQ1, fc1q), (FQ2, fc2q), (FS2, s2row)):
                    sp.dma_start(dst, src).then_inc(f0_in, 16)
            sp.wait_ge(pads, 8)
            for i in range(SHIFT):
                sp.dma_start(qx[:, ROWS + i, :], QS[1][32:64, 0, :]).then_inc(zeros_wr, 16)
            sp.wait_ge(zeros_wr, 16 * SHIFT)
            if on(0):
                sp_stacks(sp, 0)
                sp_max_rows(sp, 0, 0)
                over_groups(sp, lambda g, par, i, more: sp_causal(sp, g, par) if more else None)
            if on(2):
                sp_stacks(sp, 1)

                def load_next(g, par, i, more):
                    if more:
                        sp.wait_ge(A[1, "pv"], NW2 * g + PV2)
                        sp_load_group(sp, 1, g + 1, 1 - par)
                over_groups(sp, load_next)
            if any(on(n) for n in range(3, 8)):
                sp_late(sp)
            sp.wait_ge(x_done, 1)
            sp.dma_start(out.rearrange("b (k p) d -> p (b k) d", p=P), Xv).then_inc(out_done, 16)
            sp.wait_ge(out_done, 16)

        @block.gpsimd
        def _(pool):
            pool.memset(ident[:, :], 0.0).then_inc(p_own, 1)
            pool.memset(identb[:, :], 0.0).then_inc(p_own, 1)
            pool.memset(ones1[:, :], 1.0).then_inc(cbase, 1)
            pool.wait_ge(p_own, 2)
            for m in (ident, identb):
                pool.affine_select(out=m[:, :], in_=m[:, :], compare_op=ALU.not_equal, fill=1.0,
                                   base=0, pattern=[[-1, P]], channel_multiplier=1).then_inc(cbase, 1)
            for par in range(2):
                pool.memset(Vg[par][:, :, :, HD:VC], 0.0).then_inc(p_own, 1)
                pool.wait_ge(p_own, 3 + par)
                ins = pool.memset(Vg[par][:, :, :, HD:HD + 1], 1.0)
            ins.then_inc(p_own, 1)
            pool.wait_ge(p_own, 5)
            pool_key_pads(pool, KZ[0], pads)
            for par in range(2):
                for hh in range(2):
                    pool.memset(QS[par][64 * hh + 32:64 * hh + 64, :, :], 0.0).then_inc(pads, 1)
                    pool.wait_ge(pads, 5 + 2 * par + hh)
            for L in (0, 1):
                if not on(2 * L):
                    continue
                pool_split(pool, L)
                pool.wait_ge(A[L, "part2"], 2 * NC)
                pool.wait_ge(A[L, "proj"], NC)
                pool_key_pads(pool, KZ[1], A[L, "pads1"])
                pool.wait_ge(A[L, "vall"], NC)
                pool_group_values(pool, L, 0, 0)

                def values_next(g, par, i, more, L=L):
                    if more:
                        n = NSTEP * g + PV0 if L == 0 else NW2 * g + PV2
                        pool.wait_ge(A[L, "pv"], n)
                        pool_group_values(pool, L, g + 1, 1 - par)
                over_groups(pool, values_next)
            if on(5):
                late(pool, 2)
                pool_split_weights(pool, 5, ((MG, MGH, MGL), (MU, MUH, MUL), (MD, MDH, MDL)))
                pool_rest_of_h(pool, 5)
            if on(7):
                late(pool, 3)
                pool_split_weights(pool, 7, ((M3A, M3AH, M3AL), (M3B, M3BH, M3BL)))
                pool_rest_of_h(pool, 7)

        @block.tensor
        def _(pe):
            pe.wait_ge(cbase, NBASE)
            n_h = 0
            if on(0):
                pe_edge(pe, edges[0])
            pe.wait_ge(w_in, 16)
            pe.wait_ge(c_in, 64)
            pe.wait_ge(v_own, 1)
            if on(0):
                n_h += NC
                pe_values(pe, 0, n_h, None)
                pe_project(pe, 0, ("q0", "qs0", "k0", "ks0"))
                pe.wait_ge(A[0, "qf"], 2 * NC)
                pe.wait_ge(A[0, "ld0"], LD)
                for u in range(NU):
                    pe_max_unit(pe, 0, 0, u)
                pe_max_turn(pe, 0, 0, None)
                pe.wait_ge(A[0, "mt"], 1)
                over_groups(pe, lambda g, par, i, more: pe_causal(pe, g, par, i, more))
                pe_attention_end(pe, 0, "o0", None)
            if on(1):
                pe_edge(pe, edges[1])
                n_h += NC
                pe.wait_ge(A[1, "f_w"], 1)
                pe_ffn(pe, 1, n_h, FW1, FW2, HID0, RW["fc2b"])
            if on(2):
                pe_edge(pe, edges[2])
                n_h += NC
                pe_values(pe, 1, n_h, RW["bv1"])
                pe_project(pe, 1, ("q1", "k1"))
                pe.wait_ge(A[1, "qf"], 2 * NC)
                pe.wait_ge(A[1, "ld0"], LD)
                pe_first_pass(pe, 0, 0, 0)
                over_groups(pe, lambda g, par, i, more: pe_gated(pe, g, par, i, more))
                pe_attention_end(pe, 1, "o1", RW["bo1"])
            if on(3):
                pe_edge(pe, edges[3])
                n_h += NC
                pe_glu(pe, n_h)
            if on(4):
                pe_edge(pe, edges[4])
                n_h += NC
                late(pe, 1)
                pe_linear(pe, 4, n_h, WM["q2"], WM["kv2"], None, 1)
                pe_linear_norm(pe, 4, WM["p2"], RW["pb2"])
                pe_edge(pe, edges["4b"])
                n_h += NC
                pe_ffn(pe, 4, n_h, L2A, L2B, HID4, RW["fc2b2"])
            if on(5):
                pe_edge(pe, edges[5])
                n_h += NC
                late(pe, 2)
                pe_logits(pe, 5, n_h, R2W, E2)
                pe.wait_ge(A[5, "sc"], 1)
                pe_turn_weights(pe, 5, CWB5, 51)
                pe_moe5(pe)
            if on(6):
                pe_edge(pe, edges[6])
                n_h += NC
                pe_linear(pe, 6, n_h, WM["q3"], WM["kv3"], RW["bkv3"], 0)
                pe_linear_plain(pe, 6, WM["o3"], RW["bo3"])
            if on(7):
                pe_edge(pe, edges[7])
                n_h += NC
                late(pe, 3)
                pe_logits(pe, 7, n_h, R3W, E3)
                pe_turn_weights(pe, 7, CWB7, 3 * E3)
                pe_moe7(pe)

        @block.scalar
        def _(act):
            if on(0):
                act_edge(act, edges[0])
            act.wait_ge(c_in, 64)
            if on(0):
                act_values(act, 0)
                act_split(act, 0)
                act_max_rows(act, 0)
                over_groups(act, lambda g, par, i, more: act_causal(act, g, more))
                act_attention_end(act, 0)
            if on(1):
                act_edge(act, edges[1])
                act_ffn(act, 1, HID0, ACT.Silu, lambda m: col("s1", m), lambda m: col("fb1", m))
            if on(2):
                act_edge(act, edges[2])
                act_values(act, 1)
                act_bias_split(act, 1)
                act_first_pass(act, 0, 0)
                over_groups(act, lambda g, par, i, more: act_gated(act, g, more))
                act_attention_end(act, 1)
            if on(3):
                act_edge(act, edges[3])
                act_glu(act)
            if on(4):
                act_edge(act, edges[4])
                act_linear(act, 4, None)
                act_linear_norm(act, 4)
                act_edge(act, edges["4b"])
                act_ffn(act, 4, HID4, ACT.Gelu, None, lambda m: col("fb2", m))
            if on(5):
                act_edge(act, edges[5])
                act.wait_ge(A[5, "lg"], 1)
                act.activation(SC5.rearrange("p t e -> p (t e)"), bank(6, 0, NT * E2), ACT.Sigmoid)\
                   .then_inc(A[5, "sc"], 1)
                act_turn_weights(act, 5, 51)
                act_moe5(act)
            if on(6):
                act_edge(act, edges[6])
                act_linear(act, 6, col("bq3"))
                act_linear_plain(act, 6)
            if on(7):
                act_edge(act, edges[7])
                act_route7(act)
                act_turn_weights(act, 7, 3 * E3)
                act_moe7(act)
            if 8 in edges:
                act_edge(act, edges[8])
            for n in range(1, 8):
                if n in edges and not on(n):
                    act_edge(act, edges[n])

        @block.vector
        def _(dve):
            own = Own(dve, v_own)
            for i, key in enumerate([(L, nm) for L in (0, 1) for nm in ("o_sb", "ot", "ot_free")] + [(0, "m_wr"), (0, "b_mm")] + \
                    [(5, nm) for nm in ("sg", "t", "p", "h", "dm", "ot")] + \
                    [(7, nm) for nm in ("ge", "w2", "ye", "cb", "cc", "acc")]):
                dve.memset(ZERO[:, i:i + 1], 0.0).then_inc(A[key], BASE)
            dve.memset(EPSC[:, 0:1], EPS).then_inc(A[0, "pv"], PV0)
            dve.memset(EPSC[:, 1:2], EPS * EPS2[1]).then_inc(A[0, "b_exp"], EXP0)
            dve.memset(EPSC[:, 2:3], EPS * EPS2[2]).then_inc(A[7, "lo"], BASE7)
            own.link(dve.memset(bank(6), 0.0))
            if on(0):
                dve_edge(dve, own, edges[0])
            dve.wait_ge(c_in, 64)
            own.link(dve.tensor_scalar(NMU[:, :], col("mu"), -1.0, None, ALU.mult))
            if on(0):
                dve.wait_ge(rope_in, 32)
                dve_rope(dve, 0)
                for u in range(NU):
                    dve_max_unit(dve, 0, 0, u)
                dve_max_parts(dve, 0, 0)
                over_groups(dve, lambda g, par, i, more: dve_causal(dve, own, g, par, more))
            if on(1):
                dve_dequant0(dve)
                dve_edge(dve, own, edges[1])
            if on(2):
                dve_edge(dve, own, edges[2])
                dve.memset(R4[:, 0, 0:1], 0.0).then_inc(A[1, "pv"], PV2)
                dve.memset(R4[:, 0, 1:2], 0.0).then_inc(A[1, "mul"], MUL2)
                dve.memset(R4[:, 0, 2:3], 0.0).then_inc(A[1, "s_act"], 1)
                over_groups(dve, lambda g, par, i, more: dve_gated(dve, own, g))
            if on(3):
                dve_edge(dve, own, edges[3])
                dve.wait_ge(late_in[0], 16 * N_LATE[0])
                dve.tensor_scalar(LF, LI, 1.0 / 127.0, None, ALU.mult).then_inc(A[3, "w"], 1)
                dve_glu(dve)
            if on(4):
                dve_edge(dve, own, edges[4])
                late(dve, 1)
                dve_linear(dve, 4, 1)
                dve_linear_norm(dve, own, 4)
                dve_edge(dve, own, edges["4b"])
            if on(5):
                dve_edge(dve, own, edges[5])
                late(dve, 2)
                dve_route5(dve, own)
                dve_moe5(dve)
            if on(6):
                dve_edge(dve, own, edges[6])
                late(dve, 1)
                dve_linear(dve, 6, 0)
            if on(7):
                dve_edge(dve, own, edges[7])
                late(dve, 2)
                dve_route7(dve, own)
                dve_moe7(dve)
            if 8 in edges:
                dve_edge(dve, own, edges[8])
            for n in range(1, 8):
                if n in edges and not on(n):
                    dve_edge(dve, own, edges[n])
            own.link(dve.memset(ZERO[:, 30:31], 0.0))
            dve.memset(ZERO[:, 30:31], 0.0).then_inc(x_done, 1)


_OUTS = [((B, S, D), "float32")]


def layout(inputs):
    import numpy as np
    f = {k: np.ascontiguousarray(v) for k, v in inputs.items()}
    swap = np.arange(D) ^ 1
    T = lambda a: a.T
    w = [T(f["L0_attn_W_q"]), T(f["L0_attn_W_q"][swap]), T(f["L0_attn_W_k"]), T(f["L0_attn_W_k"][swap]),
         T(f["L0_attn_W_v"]), T(f["L0_attn_W_o"]),
         T(f["L1_attn_Wq"]), T(f["L1_attn_Wk"]), T(f["L1_attn_Wv"]), T(f["L1_attn_Wo"]),
         T(f["L2_attn_qkv_w"][0:128]), T(f["L2_attn_qkv_w"][128:256]), T(f["L2_attn_qkv_w"][256:384]),
         T(f["L2_attn_proj_w"]),
         T(f["L3_attn_Wq"]), T(f["L3_attn_Wk"]), T(f["L3_attn_Wv"]), T(f["L3_attn_Wo"])]
    w = np.stack(w, 1)
    by = lambda a, n: a.reshape(n, P).T
    cols = [f["L0_ffn_ln_gamma"][:, None], f["L0_ffn_ln_beta"][:, None], by(f["L0_ffn_fc1_scales"][0], 4),
            by(f["L0_ffn_fc1_bias"], 4), f["L1_attn_ln_gamma"][:, None], f["L1_attn_ln_beta"][:, None],
            f["L1_attn_bq"][:, None], f["L1_attn_bk"][:, None],
            np.broadcast_to(f["L1_attn_mu"].reshape(1, 1), (P, 1)),
            f["L2_attn_norm1_g"][:, None], f["L2_attn_norm1_b"][:, None],
            f["L2_attn_norm2_g"][:, None], f["L2_attn_norm2_b"][:, None], by(f["L2_attn_fc1_b"], 4),
            f["L3_attn_bq"][:, None], f["L3_attn_bk"][:, None],
            by(f["L3_ffn_b1"].reshape(-1), 32), f["L3_ffn_b2"].T]
    cols = np.concatenate(cols, 1)
    assert cols.shape == (P, NCOLS), cols.shape
    rows = np.concatenate([f["L0_ffn_fc2_bias"], f["L1_attn_bv"], f["L1_attn_bo"], f["L2_attn_proj_b"],
                           f["L2_attn_fc2_b"], f["L3_attn_bk"], f["L3_attn_bv"], f["L3_attn_bo"]])[None]
    assert rows.shape == (1, NROWS)
    inv = np.float32(10000.0) ** (np.float32(-2.0) * np.arange(HD // 2, dtype=np.float32) / np.float32(HD))
    ang = np.arange(S, dtype=np.float32)[:, None] * inv[None, :]
    d = np.arange(D) % HD
    cos = np.cos(ang).astype(np.float32).T[d // 2]
    sin = np.sin(ang).astype(np.float32).T[d // 2] * np.where(d % 2 == 0, -1.0, 1.0)[:, None].astype(np.float32)
    rope = np.stack([cos, sin]).astype(np.float32)
    k, q = np.meshgrid(np.arange(P), np.arange(P))
    mA = np.where(k > q, BF16_BIG, 0).astype(np.uint16)
    consts = np.stack([mA, mA.T])
    tiles = lambda a: a.reshape(-1, P, a.shape[-1]).transpose(1, 0, 2).reshape(P, -1)
    fc1q = f["L0_ffn_fc1_q"]
    fc2q = tiles(f["L0_ffn_fc2_q"])
    s2row = np.broadcast_to(f["L0_ffn_fc2_scales"].reshape(1, -1), (P, F3))
    l1int = np.concatenate([T(f["L1_ffn_w_gate"]), T(f["L1_ffn_w_up"]), tiles(T(f["L1_ffn_w_down"]))], 1)
    l2fc = np.concatenate([T(f["L2_attn_fc1_w"]), tiles(T(f["L2_attn_fc2_w"]))], 1)
    r2w = np.concatenate([T(f["L2_ffn_gate_w"]), np.broadcast_to(f["L2_ffn_gate_bias"][None], (P, E2)),
                          f["L3_ffn_Wr"], np.broadcast_to(f["L3_ffn_br"][None], (P, E3))], 1)
    head = np.arange(D) // HD
    headm = (head[:, None] == np.arange(H)[None]).astype(np.float32)
    r2b = np.concatenate([headm, (head[:, None] == head[None]).astype(np.float32)], 1)
    pad = np.zeros((R2 * P - HID2 - I2 * NS2, D), np.float32)
    rows_of = lambda a, b: np.concatenate([a.reshape(HID2, D), b, pad], 0)
    down = rows_of(f["L2_ffn_down_proj"].transpose(0, 2, 1), T(f["L2_ffn_shared_down_w"]))
    moe2 = np.stack([T(rows_of(f["L2_ffn_gate_proj"], f["L2_ffn_shared_gate_w"])),
                     T(rows_of(f["L2_ffn_up_proj"], f["L2_ffn_shared_up_w"])), tiles(down)])
    row = np.arange(R2 * P)
    owner = np.where(row < HID2, row // I2, np.where(row < HID2 + I2 * NS2, E2, -1))
    sel = np.where(np.arange(E2 + 1)[:, None] == owner[None], BF16_ONE, 0).astype(np.uint16)
    moe2sel = np.concatenate([sel] * 3, 0)
    sel3 = np.where(np.arange(E3)[:, None] == (np.arange(E3 * P) // P)[None], BF16_ONE, 0).astype(np.uint16)
    r3w = np.concatenate([sel3] * 3, 0)
    moe3a = f["L3_ffn_W1"].transpose(1, 0, 2).reshape(P, -1)
    moe3b = tiles(f["L3_ffn_W2"].reshape(E3 * F3, D))
    return dict(x=f["L0_attn_x"], w=w, cols=cols, rows=rows, rope=rope, consts=consts, fc1q=fc1q,
                fc2q=fc2q, s2row=s2row, l1int=l1int, l2fc=l2fc, r2w=r2w, r2b=r2b, moe2=moe2,
                moe2sel=moe2sel, r3w=r3w, moe3a=moe3a, moe3b=moe3b)


ORDER = ["x", "w", "cols", "rows", "rope", "fc1q", "fc2q", "s2row", "l1int", "l2fc", "r2w", "r2b", "moe2",
         "moe2sel", "r3w", "r3b", "moe3a", "moe3b", "consts"]


def kernel(**inputs):
    import numpy as _np
    import concourse.bacc as _bacc
    from concourse import mybir as _mybir
    from concourse.bass_utils import run_bass_kernel_spmd as _run

    nc = _bacc.Bacc("TRN2", target_bir_lowering=False, num_devices=1)
    arrays, args = {}, []
    laid = layout(inputs)
    for name in ORDER:
        if name not in laid:
            args.append(None)
            continue
        a = _np.ascontiguousarray(laid[name])
        arrays[f"in_{name}"] = a
        args.append(nc.dram_tensor(f"in_{name}", a.shape, _mybir.dt.from_np(a.dtype), kind="ExternalInput").ap())
    for i, (shape, dtype) in enumerate(_OUTS):
        dt = _mybir.dt.from_np(_np.dtype(dtype))
        args.append(nc.dram_tensor(f"out_{i}", shape, dt, kind="ExternalOutput").ap())
    sandwich(nc, *args)
    r = _run(nc, [arrays], core_ids=[0])
    return r.results[0]["out_0"]
```
